# Optimizing a Trainium2 kernel written in Bass

```python
import numpy as np
import jax
import jax.numpy as jnp

def _softmax(x, axis=-1):
    return jax.nn.softmax(x, axis=axis)

def _gelu(x):
    return jax.nn.gelu(x, approximate=True)

def _silu(x):
    return jax.nn.silu(x)

def _sigmoid(x):
    return jax.nn.sigmoid(x)

def _layernorm(x, axis=-1, eps=1e-05):
    m = jnp.mean(x, axis=axis, keepdims=True)
    v = jnp.var(x, axis=axis, keepdims=True)
    return (x - m) / jnp.sqrt(v + eps)

def _scatter_add(tgt, idx, src, axis=0):
    return tgt.at[idx].add(src)

def _segment_sum(src, seg, n):
    return jax.ops.segment_sum(src, seg, n)
kernel_name = 'mk_xattn_ffn_d4_seqx_r8_913e8e'

def setup_inputs(seed: int=0):
    np.random.seed(seed)
    _w = jnp.asarray

    def _rec_inputs():
        import jax
        import jax.numpy as jnp
        _rk = jax.random.key(seed)
        x = -0.0002928 + 1 * jax.random.normal(jax.random.fold_in(_rk, 1), (8, 256, 128), jnp.float32)
        _lenS = 256 - jax.random.randint(jax.random.fold_in(_rk, 7), (8,), 0, max(1, 256 // 4) + 1, jnp.int32)
        _lenS2 = 64 - jax.random.randint(jax.random.fold_in(_rk, 8), (8,), 0, max(1, 64 // 4) + 1, jnp.int32)
        _ctx_1024P = jax.random.normal(jax.random.fold_in(_rk, 11), (8, 16, 128), jnp.float32)
        _ctx_1024c = jax.random.dirichlet(jax.random.fold_in(_rk, 511), 0.3 * jnp.ones((16,), jnp.float32), (8, 64))
        _ctx_1024t = jnp.einsum('bsk,bkd->bsd', _ctx_1024c, _ctx_1024P)
        _ctx_1024t = _ctx_1024t * jax.lax.rsqrt(jnp.mean(jnp.square(_ctx_1024t)) + 1e-12) * 0.953939
        ctx_1024 = -1.39393e-06 + 0.999914 * (_ctx_1024t + 0.3 * jax.random.normal(jax.random.fold_in(_rk, 611), (8, 64, 128), jnp.float32))
        return (x, ctx_1024)
    x, ctx_1024 = _rec_inputs()

    def _L0_xattn_setup():
        import jax, jax.numpy as jnp
        import numpy as np
        B, N, T, D, H = (2, 256, 256, 128, 16)
        HD = D // H
        key = jax.random.key(seed)
        ks = jax.random.split(key, 5)
        s = 0.02
        return {'x': jax.random.normal(ks[0], (B, N, D), dtype=jnp.float32), 'context': jax.random.normal(ks[1], (B, T, D), dtype=jnp.float32), 'Wq': jax.random.normal(ks[2], (D, D), dtype=jnp.float32) * s, 'Wkv': jax.random.normal(ks[3], (D, 2 * HD), dtype=jnp.float32) * s, 'Wo': jax.random.normal(ks[4], (D, D), dtype=jnp.float32) * s}
    _L0_xattn_all = _L0_xattn_setup()
    _L0_xattn_in = {k: v for k, v in _L0_xattn_all.items() if k in ('Wq', 'Wkv', 'Wo')}
    del _L0_xattn_all

    def _L0_ffn_setup():
        import jax, jax.numpy as jnp
        import numpy as np
        B, N, D = (4, 512, 128)
        E, S, F = (16, 64, 256)
        DO = 128
        EPS = 1e-05

        def _layernorm(x, g, b):
            mu = jnp.mean(x, axis=-1, keepdims=True)
            var = jnp.mean(jnp.square(x - mu), axis=-1, keepdims=True)
            return (x - mu) * jax.lax.rsqrt(var + EPS) * g + b
        key = jax.random.key(seed)
        ks = jax.random.split(key, 8)
        d = {'x': jax.random.normal(ks[0], (B, N, D), dtype=jnp.float32), 'norm_g': jnp.ones((D,), jnp.float32), 'norm_b': jnp.zeros((D,), jnp.float32), 'slot_g': jnp.ones((D,), jnp.float32), 'slot_b': jnp.zeros((D,), jnp.float32), 'scale': jnp.ones((1,), jnp.float32), 'slot_embeds': jax.random.normal(ks[1], (E, S, D), jnp.float32) / np.sqrt(D), 'Wg': jax.random.normal(ks[2], (E, D, F), jnp.float32) * np.sqrt(2.0 / (D + F)), 'bg': jnp.zeros((E, F), jnp.float32), 'Wu': jax.random.normal(ks[3], (E, D, F), jnp.float32) * np.sqrt(2.0 / (D + F)), 'bu': jnp.zeros((E, F), jnp.float32), 'Wd': jax.random.normal(ks[4], (E, F, DO), jnp.float32) * np.sqrt(2.0 / (F + DO)), 'bd': jnp.zeros((E, DO), jnp.float32)}
        return d
    _L0_ffn_all = _L0_ffn_setup()
    _L0_ffn_in = {k: v for k, v in _L0_ffn_all.items() if k in ('norm_g', 'norm_b', 'slot_g', 'slot_b', 'scale', 'slot_embeds', 'Wg', 'bg', 'Wu', 'bu', 'Wd', 'bd')}
    del _L0_ffn_all

    def _L1_xattn_setup():
        import jax, jax.numpy as jnp
        import numpy as np
        B, L_ENC, L_DEC, D = (16, 64, 128, 128)
        key = jax.random.key(seed)
        k1, k2, k3, k4, k5, k6 = jax.random.split(key, 6)
        encoder_hc = jax.random.normal(k1, (B, L_ENC, D), dtype=jnp.float32)
        decoder_hq = jax.random.normal(k2, (B, L_DEC, D), dtype=jnp.float32)
        w_sim = jax.random.normal(k3, (3 * D,), dtype=jnp.float32) * 0.02
        b_sim = jax.random.normal(k4, (1,), dtype=jnp.float32) * 0.02
        W_qv = jax.random.normal(k5, (4 * D, D), dtype=jnp.float32) * 0.02
        b_qv = jax.random.normal(k6, (D,), dtype=jnp.float32) * 0.02
        return {'encoder_hc': encoder_hc, 'decoder_hq': decoder_hq, 'w_sim': w_sim, 'b_sim': b_sim, 'W_qv': W_qv, 'b_qv': b_qv}
    _L1_xattn_all = _L1_xattn_setup()
    _L1_xattn_in = {k: v for k, v in _L1_xattn_all.items() if k in ('w_sim', 'b_sim', 'W_qv', 'b_qv')}
    del _L1_xattn_all

    def _L1_ffn_setup():
        import jax, jax.numpy as jnp
        import numpy as np
        H = 128
        I = 88
        E = 64
        TOP_K = 8
        NG = 8
        TOPK_GROUP = 4
        N_SHARED = 2
        ROUTED_SCALE = 2.5
        S_I = I * N_SHARED

        def _route(x, gate_w, gate_bias):
            T = x.shape[0]
            logits = x @ gate_w.T
            scores = jax.nn.sigmoid(logits)
            scores_for_choice = scores + gate_bias[None, :]
            grp = scores_for_choice.reshape(T, NG, E // NG)
            group_scores = jnp.sum(jax.lax.top_k(grp, 2)[0], axis=-1)
            _, gidx = jax.lax.top_k(group_scores, TOPK_GROUP)
            gmask = jnp.zeros((T, NG), dtype=scores.dtype).at[jnp.arange(T)[:, None], gidx].set(1.0)
            emask = jnp.repeat(gmask, E // NG, axis=1)
            masked = jnp.where(emask > 0, scores_for_choice, 0.0)
            _, topk_idx = jax.lax.top_k(masked, TOP_K)
            topk_w = jnp.take_along_axis(scores, topk_idx, axis=1)
            topk_w = topk_w / (jnp.sum(topk_w, axis=-1, keepdims=True) + 1e-20)
            topk_w = topk_w * ROUTED_SCALE
            rw = jnp.zeros((T, E), dtype=scores.dtype).at[jnp.arange(T)[:, None], topk_idx].add(topk_w)
            return rw

        def _mlp(x, gw, uw, dw):
            return jax.nn.silu(x @ gw.T) * (x @ uw.T) @ dw.T
        key = jax.random.key(seed)
        ks = jax.random.split(key, 10)
        sc = 0.02
        return {'hidden_states': jax.random.normal(ks[0], (1, 128, H), dtype=jnp.float32), 'gate_w': sc * jax.random.normal(ks[1], (E, H), dtype=jnp.float32), 'gate_bias': sc * jax.random.normal(ks[2], (E,), dtype=jnp.float32), 'Wg': sc * jax.random.normal(ks[3], (E, I, H), dtype=jnp.float32), 'Wu': sc * jax.random.normal(ks[4], (E, I, H), dtype=jnp.float32), 'Wd': sc * jax.random.normal(ks[5], (E, H, I), dtype=jnp.float32), 'Sg': sc * jax.random.normal(ks[6], (S_I, H), dtype=jnp.float32), 'Su': sc * jax.random.normal(ks[7], (S_I, H), dtype=jnp.float32), 'Sd': sc * jax.random.normal(ks[8], (H, S_I), dtype=jnp.float32)}
    _L1_ffn_all = _L1_ffn_setup()
    _L1_ffn_in = {k: v for k, v in _L1_ffn_all.items() if k in ('gate_w', 'gate_bias', 'Wg', 'Wu', 'Wd', 'Sg', 'Su', 'Sd')}
    del _L1_ffn_all

    def _L2_xattn_setup():
        import jax, jax.numpy as jnp
        import numpy as np
        B, S, DIN, DK, DV = (8, 256, 128, 128, 128)
        key = jax.random.key(seed)
        ks = jax.random.split(key, 9)
        s_in = 1.0 / np.sqrt(DIN)
        return {'query': jax.random.normal(ks[0], (B, S, DIN), jnp.float32), 'key_': jax.random.normal(ks[1], (B, S, DIN), jnp.float32), 'value': jax.random.normal(ks[2], (B, S, DIN), jnp.float32), 'Wq_w': jax.random.uniform(ks[3], (DK, DIN), jnp.float32, -s_in, s_in), 'Wq_b': jax.random.uniform(ks[4], (DK,), jnp.float32, -s_in, s_in), 'Wk_w': jax.random.uniform(ks[5], (DK, DIN), jnp.float32, -s_in, s_in), 'Wk_b': jax.random.uniform(ks[6], (DK,), jnp.float32, -s_in, s_in), 'Wv_w': jax.random.uniform(ks[7], (DV, DIN), jnp.float32, -s_in, s_in), 'Wv_b': jax.random.uniform(ks[8], (DV,), jnp.float32, -s_in, s_in)}
    _L2_xattn_all = _L2_xattn_setup()
    _L2_xattn_in = {k: v for k, v in _L2_xattn_all.items() if k in ('Wq_w', 'Wq_b', 'Wk_w', 'Wk_b', 'Wv_w', 'Wv_b')}
    del _L2_xattn_all

    def _L2_ffn_setup():
        import jax, jax.numpy as jnp
        import numpy as np
        N_EMBD = 128
        EXPERT_SIZES = [(4, 128), (4, 256)]
        TOP_K = 2
        B, S = (1, 256)
        WIDTHS = []
        for count, size in EXPERT_SIZES:
            WIDTHS += [size] * count
        OFFSETS = np.concatenate([[0], np.cumsum(WIDTHS)]).astype(np.int64)
        E = len(WIDTHS)
        TOTAL_W = int(OFFSETS[-1])
        MAX_W = max(WIDTHS)

        def _stack_experts(w1, w2):
            W1e, W2e = ([], [])
            for e in range(E):
                off, wd = (int(OFFSETS[e]), WIDTHS[e])
                pad = MAX_W - wd
                W1e.append(jnp.pad(w1[:, off:off + wd], ((0, 0), (0, pad))))
                W2e.append(jnp.pad(w2[off:off + wd, :], ((0, pad), (0, 0))))
            return (jnp.stack(W1e), jnp.stack(W2e))
        key = jax.random.key(seed)
        k1, k2, k3, k4 = jax.random.split(key, 4)
        x = jax.random.normal(k1, (B, S, N_EMBD), jnp.float32)
        router_w = jax.random.normal(k2, (E, N_EMBD), jnp.float32) * 0.02
        w1 = jax.random.truncated_normal(k3, -3.0, 3.0, (N_EMBD, TOTAL_W), jnp.float32) * 0.02
        w2 = jax.random.truncated_normal(k4, -3.0, 3.0, (TOTAL_W, N_EMBD), jnp.float32) * 0.02
        return {'x': x, 'router_w': router_w, 'w1': w1, 'w2': w2}
    _L2_ffn_all = _L2_ffn_setup()
    _L2_ffn_in = {k: v for k, v in _L2_ffn_all.items() if k in ('router_w', 'w1', 'w2')}
    del _L2_ffn_all

    def _L3_xattn_setup():
        import jax, jax.numpy as jnp
        import numpy as np
        D_MODEL = 128
        B, S = (4, 256)
        key = jax.random.key(seed)
        ks = jax.random.split(key, 10)
        s = 1.0 / np.sqrt(D_MODEL)
        return {'k': jax.random.normal(ks[0], (B, S, D_MODEL), jnp.float32), 'v': jax.random.normal(ks[1], (B, S, D_MODEL), jnp.float32), 'q': jax.random.normal(ks[2], (B, S, D_MODEL), jnp.float32), 'Wk': jax.random.normal(ks[3], (D_MODEL, D_MODEL), jnp.float32) * s, 'Wv': jax.random.normal(ks[4], (D_MODEL, D_MODEL), jnp.float32) * s, 'bv': jnp.zeros((D_MODEL,), jnp.float32), 'Wq': jax.random.normal(ks[5], (D_MODEL, D_MODEL), jnp.float32) * s, 'bq': jnp.zeros((D_MODEL,), jnp.float32), 'Wo': jax.random.normal(ks[6], (D_MODEL, D_MODEL), jnp.float32) * s, 'bo': jnp.zeros((D_MODEL,), jnp.float32)}
    _L3_xattn_all = _L3_xattn_setup()
    _L3_xattn_in = {k: v for k, v in _L3_xattn_all.items() if k in ('Wk', 'Wv', 'bv', 'Wq', 'bq', 'Wo', 'bo')}
    del _L3_xattn_all

    def _L3_ffn_setup():
        import jax, jax.numpy as jnp
        import numpy as np
        B, S, D_MODEL, D_HIDDEN = (4, 256, 128, 512)

        def act_quant(x):
            scale = 127.0 / jnp.clip(jnp.max(jnp.abs(x), axis=-1, keepdims=True), 1e-05)
            return jnp.clip(jnp.round(x * scale), -128, 127) / scale

        def weight_quant(w):
            scale = 1.0 / jnp.clip(jnp.mean(jnp.abs(w)), 1e-05)
            return jnp.clip(jnp.round(w * scale), -1, 1) / scale

        def bit_linear(x, w):
            xq = x + jax.lax.stop_gradient(act_quant(x) - x)
            wq = w + jax.lax.stop_gradient(weight_quant(w) - w)
            return jnp.einsum('bsd,hd->bsh', xq, wq)

        def depthwise_conv1d(x_bcl, w, b):
            y = jax.lax.conv_general_dilated(x_bcl, w, window_strides=(1,), padding=[(1, 1)], dimension_numbers=('NCH', 'OIH', 'NCH'), feature_group_count=x_bcl.shape[1])
            return y + b[None, :, None]
        key = jax.random.key(seed)
        ks = jax.random.split(key, 5)
        lim1 = 1.0 / np.sqrt(D_MODEL)
        lim2 = 1.0 / np.sqrt(D_HIDDEN)
        limc = 1.0 / np.sqrt(3.0)
        return {'x': jax.random.normal(ks[0], (B, S, D_MODEL), dtype=jnp.float32), 'w1': jax.random.uniform(ks[1], (D_HIDDEN, D_MODEL), jnp.float32, -lim1, lim1), 'conv_w': jax.random.uniform(ks[2], (D_HIDDEN, 1, 3), jnp.float32, -limc, limc), 'conv_b': jax.random.uniform(ks[3], (D_HIDDEN,), jnp.float32, -limc, limc), 'w2': jax.random.uniform(ks[4], (D_MODEL, D_HIDDEN), jnp.float32, -lim2, lim2)}
    _L3_ffn_all = _L3_ffn_setup()
    _L3_ffn_in = {k: v for k, v in _L3_ffn_all.items() if k in ('w1', 'conv_w', 'conv_b', 'w2')}
    del _L3_ffn_all
    return {'x': x, 'ctx_1024': ctx_1024, 'L0_xattn_Wq': _L0_xattn_in['Wq'], 'L0_xattn_Wkv': _L0_xattn_in['Wkv'], 'L0_xattn_Wo': _L0_xattn_in['Wo'], 'L0_ffn_norm_g': _L0_ffn_in['norm_g'], 'L0_ffn_norm_b': _L0_ffn_in['norm_b'], 'L0_ffn_slot_g': _L0_ffn_in['slot_g'], 'L0_ffn_slot_b': _L0_ffn_in['slot_b'], 'L0_ffn_scale': _L0_ffn_in['scale'], 'L0_ffn_slot_embeds': _L0_ffn_in['slot_embeds'], 'L0_ffn_Wg': _L0_ffn_in['Wg'], 'L0_ffn_bg': _L0_ffn_in['bg'], 'L0_ffn_Wu': _L0_ffn_in['Wu'], 'L0_ffn_bu': _L0_ffn_in['bu'], 'L0_ffn_Wd': _L0_ffn_in['Wd'], 'L0_ffn_bd': _L0_ffn_in['bd'], 'L1_xattn_w_sim': _L1_xattn_in['w_sim'], 'L1_xattn_b_sim': _L1_xattn_in['b_sim'], 'L1_xattn_W_qv': _L1_xattn_in['W_qv'], 'L1_xattn_b_qv': _L1_xattn_in['b_qv'], 'L1_ffn_gate_w': _L1_ffn_in['gate_w'], 'L1_ffn_gate_bias': _L1_ffn_in['gate_bias'], 'L1_ffn_Wg': _L1_ffn_in['Wg'], 'L1_ffn_Wu': _L1_ffn_in['Wu'], 'L1_ffn_Wd': _L1_ffn_in['Wd'], 'L1_ffn_Sg': _L1_ffn_in['Sg'], 'L1_ffn_Su': _L1_ffn_in['Su'], 'L1_ffn_Sd': _L1_ffn_in['Sd'], 'L2_xattn_Wq_w': _L2_xattn_in['Wq_w'], 'L2_xattn_Wq_b': _L2_xattn_in['Wq_b'], 'L2_xattn_Wk_w': _L2_xattn_in['Wk_w'], 'L2_xattn_Wk_b': _L2_xattn_in['Wk_b'], 'L2_xattn_Wv_w': _L2_xattn_in['Wv_w'], 'L2_xattn_Wv_b': _L2_xattn_in['Wv_b'], 'L2_ffn_router_w': _L2_ffn_in['router_w'], 'L2_ffn_w1': _L2_ffn_in['w1'], 'L2_ffn_w2': _L2_ffn_in['w2'], 'L3_xattn_Wk': _L3_xattn_in['Wk'], 'L3_xattn_Wv': _L3_xattn_in['Wv'], 'L3_xattn_bv': _L3_xattn_in['bv'], 'L3_xattn_Wq': _L3_xattn_in['Wq'], 'L3_xattn_bq': _L3_xattn_in['bq'], 'L3_xattn_Wo': _L3_xattn_in['Wo'], 'L3_xattn_bo': _L3_xattn_in['bo'], 'L3_ffn_w1': _L3_ffn_in['w1'], 'L3_ffn_conv_w': _L3_ffn_in['conv_w'], 'L3_ffn_conv_b': _L3_ffn_in['conv_b'], 'L3_ffn_w2': _L3_ffn_in['w2']}

def reference(x, ctx_1024, L0_xattn_Wq, L0_xattn_Wkv, L0_xattn_Wo, L0_ffn_norm_g, L0_ffn_norm_b, L0_ffn_slot_g, L0_ffn_slot_b, L0_ffn_scale, L0_ffn_slot_embeds, L0_ffn_Wg, L0_ffn_bg, L0_ffn_Wu, L0_ffn_bu, L0_ffn_Wd, L0_ffn_bd, L1_xattn_w_sim, L1_xattn_b_sim, L1_xattn_W_qv, L1_xattn_b_qv, L1_ffn_gate_w, L1_ffn_gate_bias, L1_ffn_Wg, L1_ffn_Wu, L1_ffn_Wd, L1_ffn_Sg, L1_ffn_Su, L1_ffn_Sd, L2_xattn_Wq_w, L2_xattn_Wq_b, L2_xattn_Wk_w, L2_xattn_Wk_b, L2_xattn_Wv_w, L2_xattn_Wv_b, L2_ffn_router_w, L2_ffn_w1, L2_ffn_w2, L3_xattn_Wk, L3_xattn_Wv, L3_xattn_bv, L3_xattn_Wq, L3_xattn_bq, L3_xattn_Wo, L3_xattn_bo, L3_ffn_w1, L3_ffn_conv_w, L3_ffn_conv_b, L3_ffn_w2):
    import jax
    import jax.numpy as jnp

    def _L0_xattn_ref(x, context, Wq, Wkv, Wo):
        import jax, jax.numpy as jnp
        import numpy as np
        B, N, T, D, H = (2, 256, 256, 128, 16)
        HD = D // H
        b, n, d = x.shape
        h = H
        hd = d // h
        scale = hd ** (-0.5)
        q = x @ Wq
        kv = context @ Wkv
        k, v = jnp.split(kv, 2, axis=-1)
        q = q.reshape(b, n, h, hd).transpose(0, 2, 1, 3) * scale
        sim = jnp.einsum('bhnd,btd->bhnt', q, k)
        att = jax.nn.softmax(sim, axis=-1)
        y = jnp.einsum('bhnt,btd->bhnd', att, v)
        y = y.transpose(0, 2, 1, 3).reshape(b, n, d)
        return y @ Wo

    def _L0_ffn_ref(x, norm_g, norm_b, slot_g, slot_b, scale, slot_embeds, Wg, bg, Wu, bu, Wd, bd):
        import jax, jax.numpy as jnp
        import numpy as np
        B, N, D = (4, 512, 128)
        E, S, F = (16, 64, 256)
        DO = 128
        EPS = 1e-05

        def _layernorm(x, g, b):
            mu = jnp.mean(x, axis=-1, keepdims=True)
            var = jnp.mean(jnp.square(x - mu), axis=-1, keepdims=True)
            return (x - mu) * jax.lax.rsqrt(var + EPS) * g + b
        x = _layernorm(x, norm_g, norm_b)
        se = _layernorm(slot_embeds, slot_g, slot_b) * scale
        logits = jnp.einsum('bnd,esd->bnes', x, se)
        dispatch = jax.nn.softmax(logits, axis=1)
        combine = jax.nn.softmax(logits.reshape(x.shape[0], x.shape[1], -1), axis=-1)
        slots = jnp.einsum('bnd,bnes->besd', x, dispatch)
        gate = jax.nn.gelu(jnp.einsum('besd,edf->besf', slots, Wg) + bg[None, :, None, :], approximate=False)
        up = jnp.einsum('besd,edf->besf', slots, Wu) + bu[None, :, None, :]
        eout = jnp.einsum('besf,efo->beso', gate * up, Wd) + bd[None, :, None, :]
        eout = eout.reshape(eout.shape[0], -1, eout.shape[-1])
        return jnp.einsum('bns,bso->bno', combine, eout)

    def _L1_xattn_ref(encoder_hc, decoder_hq, w_sim, b_sim, W_qv, b_qv):
        import jax, jax.numpy as jnp
        import numpy as np
        B, L_ENC, L_DEC, D = (16, 64, 128, 128)
        d = encoder_hc.shape[-1]
        w1, w2, w3 = (w_sim[:d], w_sim[d:2 * d], w_sim[2 * d:])
        Sim = (encoder_hc @ w1)[:, :, None] + (decoder_hq @ w2)[:, None, :] + jnp.einsum('bid,bjd->bij', encoder_hc * w3, decoder_hq) + b_sim[0]
        A = jax.nn.softmax(Sim, axis=2)
        hq_hat = jnp.einsum('bij,bjd->bid', A, decoder_hq)
        Batt = jax.nn.softmax(jnp.max(Sim, axis=2), axis=1)
        hc_bar = jnp.einsum('bi,bid->bd', Batt, encoder_hc)[:, None, :]
        hc_hat = jnp.broadcast_to(hc_bar, encoder_hc.shape)
        feats = jnp.concatenate([encoder_hc, hq_hat, encoder_hc * hq_hat, encoder_hc * hc_hat], axis=-1)
        hcq = feats @ W_qv + b_qv
        return hcq

    def _L1_ffn_ref(hidden_states, gate_w, gate_bias, Wg, Wu, Wd, Sg, Su, Sd):
        import jax, jax.numpy as jnp
        import numpy as np
        H = 128
        I = 88
        E = 64
        TOP_K = 8
        NG = 8
        TOPK_GROUP = 4
        N_SHARED = 2
        ROUTED_SCALE = 2.5
        S_I = I * N_SHARED

        def _route(x, gate_w, gate_bias):
            T = x.shape[0]
            logits = x @ gate_w.T
            scores = jax.nn.sigmoid(logits)
            scores_for_choice = scores + gate_bias[None, :]
            grp = scores_for_choice.reshape(T, NG, E // NG)
            group_scores = jnp.sum(jax.lax.top_k(grp, 2)[0], axis=-1)
            _, gidx = jax.lax.top_k(group_scores, TOPK_GROUP)
            gmask = jnp.zeros((T, NG), dtype=scores.dtype).at[jnp.arange(T)[:, None], gidx].set(1.0)
            emask = jnp.repeat(gmask, E // NG, axis=1)
            masked = jnp.where(emask > 0, scores_for_choice, 0.0)
            _, topk_idx = jax.lax.top_k(masked, TOP_K)
            topk_w = jnp.take_along_axis(scores, topk_idx, axis=1)
            topk_w = topk_w / (jnp.sum(topk_w, axis=-1, keepdims=True) + 1e-20)
            topk_w = topk_w * ROUTED_SCALE
            rw = jnp.zeros((T, E), dtype=scores.dtype).at[jnp.arange(T)[:, None], topk_idx].add(topk_w)
            return rw

        def _mlp(x, gw, uw, dw):
            return jax.nn.silu(x @ gw.T) * (x @ uw.T) @ dw.T
        B, S, _ = hidden_states.shape
        x = hidden_states.reshape(B * S, H)
        rw = _route(x, gate_w, gate_bias)
        expert_out = jax.vmap(lambda gw_, uw_, dw_: _mlp(x, gw_, uw_, dw_))(Wg, Wu, Wd)
        routed = jnp.einsum('eth,te->th', expert_out, rw)
        shared = _mlp(x, Sg, Su, Sd)
        out = (routed + shared).reshape(B, S, H)
        return out

    def _L2_xattn_ref(query, key_, value, Wq_w, Wq_b, Wk_w, Wk_b, Wv_w, Wv_b):
        import jax, jax.numpy as jnp
        import numpy as np
        B, S, DIN, DK, DV = (8, 256, 128, 128, 128)
        Q = jnp.einsum('bsd,kd->bsk', query, Wq_w) + Wq_b
        K = jnp.einsum('bsd,kd->bsk', key_, Wk_w) + Wk_b
        V = jnp.einsum('bsd,vd->bsv', value, Wv_w) + Wv_b
        scale = 1.0 / jnp.sqrt(jnp.asarray(Q.shape[-1], Q.dtype))
        scores = jnp.einsum('bqk,bsk->bqs', Q, K) * scale
        attn = jax.nn.softmax(scores, axis=-1)
        return jnp.einsum('bqs,bsv->bqv', attn, V)

    def _L2_ffn_ref(x, router_w, w1, w2):
        import jax, jax.numpy as jnp
        import numpy as np
        N_EMBD = 128
        EXPERT_SIZES = [(4, 128), (4, 256)]
        TOP_K = 2
        B, S = (1, 256)
        WIDTHS = []
        for count, size in EXPERT_SIZES:
            WIDTHS += [size] * count
        OFFSETS = np.concatenate([[0], np.cumsum(WIDTHS)]).astype(np.int64)
        E = len(WIDTHS)
        TOTAL_W = int(OFFSETS[-1])
        MAX_W = max(WIDTHS)

        def _stack_experts(w1, w2):
            W1e, W2e = ([], [])
            for e in range(E):
                off, wd = (int(OFFSETS[e]), WIDTHS[e])
                pad = MAX_W - wd
                W1e.append(jnp.pad(w1[:, off:off + wd], ((0, 0), (0, pad))))
                W2e.append(jnp.pad(w2[off:off + wd, :], ((0, pad), (0, 0))))
            return (jnp.stack(W1e), jnp.stack(W2e))
        b, s, d = x.shape
        xf = x.reshape(-1, d)
        logits = xf @ router_w.T
        probs = jax.nn.sigmoid(logits.astype(jnp.float32))
        topw, sel = jax.lax.top_k(probs, TOP_K)
        topw = topw / (topw.sum(-1, keepdims=True) + 1e-20)
        topw = topw.astype(x.dtype)
        onehot = sel[:, :, None] == jnp.arange(E)[None, None, :]
        combine = jnp.sum(topw[:, :, None] * onehot, axis=1)
        W1e, W2e = _stack_experts(w1, w2)
        h = jnp.einsum('td,edw->tew', xf, W1e)
        h = jnp.square(jax.nn.relu(h))
        y = jnp.einsum('tew,ewd->ted', h, W2e)
        out = jnp.einsum('ted,te->td', y, combine)
        return out.reshape(b, s, d)

    def _L3_xattn_ref(k, v, q, Wk, Wv, bv, Wq, bq, Wo, bo):
        import jax, jax.numpy as jnp
        import numpy as np
        D_MODEL = 128
        B, S = (4, 256)
        kp = jnp.einsum('bsd,ed->bse', k, Wk)
        vp = jnp.einsum('bsd,ed->bse', v, Wv) + bv
        qp = jnp.einsum('bsd,ed->bse', q, Wq) + bq
        scale = 1.0 / jnp.sqrt(jnp.float32(kp.shape[-1]))
        scores = jnp.einsum('bqd,bkd->bqk', qp, kp) * scale
        probs = jax.nn.softmax(scores, axis=-1)
        ctx = jnp.einsum('bqk,bkd->bqd', probs, vp)
        return jnp.einsum('bqd,ed->bqe', ctx, Wo) + bo

    def _L3_ffn_ref(x, w1, conv_w, conv_b, w2):
        import jax, jax.numpy as jnp
        import numpy as np
        B, S, D_MODEL, D_HIDDEN = (4, 256, 128, 512)

        def act_quant(x):
            scale = 127.0 / jnp.clip(jnp.max(jnp.abs(x), axis=-1, keepdims=True), 1e-05)
            return jnp.clip(jnp.round(x * scale), -128, 127) / scale

        def weight_quant(w):
            scale = 1.0 / jnp.clip(jnp.mean(jnp.abs(w)), 1e-05)
            return jnp.clip(jnp.round(w * scale), -1, 1) / scale

        def bit_linear(x, w):
            xq = x + jax.lax.stop_gradient(act_quant(x) - x)
            wq = w + jax.lax.stop_gradient(weight_quant(w) - w)
            return jnp.einsum('bsd,hd->bsh', xq, wq)

        def depthwise_conv1d(x_bcl, w, b):
            y = jax.lax.conv_general_dilated(x_bcl, w, window_strides=(1,), padding=[(1, 1)], dimension_numbers=('NCH', 'OIH', 'NCH'), feature_group_count=x_bcl.shape[1])
            return y + b[None, :, None]
        h = bit_linear(x, w1)
        h = depthwise_conv1d(h.transpose(0, 2, 1), conv_w, conv_b)
        h = h.transpose(0, 2, 1)
        h = jax.nn.silu(h)
        return bit_linear(h, w2)
    x = x + _L0_xattn_ref(_layernorm(x, axis=-1), ctx_1024, L0_xattn_Wq, L0_xattn_Wkv, L0_xattn_Wo)
    x = x + _L0_ffn_ref(_layernorm(x, axis=-1), L0_ffn_norm_g, L0_ffn_norm_b, L0_ffn_slot_g, L0_ffn_slot_b, L0_ffn_scale, L0_ffn_slot_embeds, L0_ffn_Wg, L0_ffn_bg, L0_ffn_Wu, L0_ffn_bu, L0_ffn_Wd, L0_ffn_bd)
    x = x + _L1_xattn_ref(_layernorm(x, axis=-1), ctx_1024, L1_xattn_w_sim, L1_xattn_b_sim, L1_xattn_W_qv, L1_xattn_b_qv)
    x = x + _L1_ffn_ref(_layernorm(x, axis=-1), L1_ffn_gate_w, L1_ffn_gate_bias, L1_ffn_Wg, L1_ffn_Wu, L1_ffn_Wd, L1_ffn_Sg, L1_ffn_Su, L1_ffn_Sd)
    x = x + _L2_xattn_ref(_layernorm(x, axis=-1), ctx_1024, ctx_1024, L2_xattn_Wq_w, L2_xattn_Wq_b, L2_xattn_Wk_w, L2_xattn_Wk_b, L2_xattn_Wv_w, L2_xattn_Wv_b)
    x = x + _L2_ffn_ref(_layernorm(x, axis=-1), L2_ffn_router_w, L2_ffn_w1, L2_ffn_w2)
    x = x + _L3_xattn_ref(ctx_1024, ctx_1024, _layernorm(x, axis=-1), L3_xattn_Wk, L3_xattn_Wv, L3_xattn_bv, L3_xattn_Wq, L3_xattn_bq, L3_xattn_Wo, L3_xattn_bo)
    x = x + _L3_ffn_ref(_layernorm(x, axis=-1), L3_ffn_w1, L3_ffn_conv_w, L3_ffn_conv_b, L3_ffn_w2)
    return x

_drawn_inputs = setup_inputs


def setup_inputs(seed=0):
    import zlib

    import numpy as np

    out = dict(_drawn_inputs(seed))
    spreads = {'L0_ffn_norm_g': (1.0, 0.2),
     'L0_ffn_norm_b': (0.0, 0.1),
     'L0_ffn_slot_g': (1.0, 0.2),
     'L0_ffn_slot_b': (0.0, 0.1),
     'L0_ffn_bg': (0.0, 0.1),
     'L0_ffn_bu': (0.0, 0.1),
     'L0_ffn_bd': (0.0, 0.1),
     'L3_xattn_bv': (0.0, 0.607),
     'L3_xattn_bq': (0.0, 2.0),
     'L3_xattn_bo': (0.0, 0.517)}
    factors = {'L0_xattn_Wq': 8.0,
     'L1_xattn_w_sim': 3.041,
     'L1_xattn_b_qv': 3.084,
     'L1_ffn_gate_w': 8.0,
     'L1_ffn_gate_bias': 8.0,
     'L1_ffn_Wg': 8.0,
     'L1_ffn_Wu': 8.0,
     'L1_ffn_Wd': 8.0,
     'L1_ffn_Sg': 8.0,
     'L1_ffn_Su': 8.0,
     'L1_ffn_Sd': 8.0,
     'L2_xattn_Wq_b': 8.0,
     'L2_xattn_Wk_b': 64.0,
     'L2_ffn_router_w': 7.076,
     'L2_ffn_w1': 6.908,
     'L2_ffn_w2': 6.369,
     'L3_ffn_w1': 6.52,
     'L3_ffn_conv_w': 6.267,
     'L3_ffn_conv_b': 5.059,
     'L3_ffn_w2': 4.056}
    for name, (base, spread) in spreads.items():
        noise = np.random.default_rng([zlib.crc32(name.encode()), seed]).standard_normal(out[name].shape)
        drawn = base * np.exp(spread * noise) if base else spread * noise
        out[name] = jnp.asarray(drawn.astype(out[name].dtype))
    for name, factor in factors.items():
        out[name] = (out[name] * factor).astype(out[name].dtype)
    return out
```

```python
from contextlib import ExitStack

import concourse.bass as bass
from concourse import mybir

ALU = mybir.AluOpType
ACT = mybir.ActivationFunctionType
AX = mybir.AxisListType
F32 = mybir.dt.float32
BF16 = mybir.dt.bfloat16

P = 128
B, N, D = 8, 256, 128
C = 64
T = B * N
NT = T // P
TB = N // P
NG = NT // 4
H0, HD = 16, D // 16
E0, S0, F0 = 16, 64, 256
ES = E0 * S0
NC0 = ES // P
E1, I1 = 64, 88
NC1 = E1 * I1 // P
G1 = 8
SH1 = 2
E2 = 8
W2 = 4 * 128 + 4 * 256
NC2 = W2 // P
HID3 = 512
NC3 = HID3 // P
EPS = 1e-5
MAGIC = 1.5 * 2.0 ** 23
LAYERS = 8

COLS = ["norm_g", "norm_b", "slot_g", "slot_b", "w_sim1", "w_sim2", "w_sim3", "q2_b", "k2_b", "q3_b"]
COL = {name: k for k, name in enumerate(COLS)}
CONV = len(COLS)
NCOL = CONV + 4 * NC3
ROWS = ["qv1_b", "v2_b", "v3_b", "o3_b"]
ROW = {name: k for k, name in enumerate(ROWS)}
EW = 3 * F0 + 5


def build_program(nc, A, out):
    with ExitStack() as ctx:
        def sb(name, shape, dt=F32):
            return ctx.enter_context(nc.sbuf_tensor(name, shape, dt))

        def sem(name):
            return ctx.enter_context(nc.semaphore(name))

        psum = ctx.enter_context(nc.psum_tensor("psum", [P, 8, 512], F32))

        X = sb("X", [P, NT, D])
        xn = sb("xn", [P, NT, D])
        xnT = sb("xnT", [P, T])
        ctxT = sb("ctxT", [P, B * C])
        ctx_tok = sb("ctx_tok", [C, B, D])
        ident = sb("ident", [P, P])
        identb = sb("identb", [P, P], BF16)
        ones = sb("ones", [P, P])
        cols = sb("cols", [P, NCOL])
        rows = sb("rows", [P, len(ROWS), D])
        scal = sb("scal", [P, 2])
        stats = sb("stats", [P, NT, 6])
        mv = sb("mv", [P, NT, 2])
        veps = sb("veps", [P, NT])
        rstd = sb("rstd", [P, NT])
        rtmp = sb("rtmp", [P, NT])
        neghalf = sb("neghalf", [P, NT])
        epst = sb("epst", [P, NT])
        wq0 = sb("wq0", [P, D])
        wk0 = sb("wk0", [P, D])
        wv0 = sb("wv0", [P, HD])
        wo0 = sb("wo0", [P, D])
        headmask = sb("headmask", [P, H0])
        seT = sb("seT", [P, ES])
        slot_gs = sb("slot_gs", [P, 2])
        ew = sb("ew", [P, 2, EW])
        wqv = sb("wqv", [P, 4, D])
        gw1 = sb("gw1", [P, E1])
        gbias = sb("gbias", [P, E1])
        sgT = sb("sgT", [P, SH1 * I1])
        suT = sb("suT", [P, SH1 * I1])
        sdT = sb("sdT", [I1, SH1, D])
        w1ring = sb("w1ring", [P, 2, 3 * P])
        wq2 = sb("wq2", [P, D])
        wk2 = sb("wk2", [P, D])
        wv2 = sb("wv2", [P, D])
        rw2 = sb("rw2", [P, E2])
        w2ring = sb("w2ring", [P, 2, 2 * P])
        wq3 = sb("wq3", [P, D])
        wk3 = sb("wk3", [P, D])
        wv3 = sb("wv3", [P, D])
        wo3 = sb("wo3", [P, D])
        w1f = sb("w1f", [P, HID3])
        w2f = sb("w2f", [P, NC3, D])
        ltmask = sb("ltmask", [P, 8, 8])

        ARENA = 36352
        arena = sb("arena", [P, ARENA])
        taken = [0]

        def carve(*shape, dt=F32):
            n = 1
            for k in shape:
                n *= k
            words = n if dt == F32 else (n + 1) // 2
            v = arena[:, taken[0]:taken[0] + words]
            taken[0] += words
            assert taken[0] <= ARENA, taken[0]
            if dt != F32:
                v = v.bitcast(dt)
            if len(shape) == 2:
                v = v.rearrange("p (a b) -> p a b", a=shape[0])
            elif len(shape) == 3:
                v = v.rearrange("p (a b c) -> p a b c", a=shape[0], b=shape[1])
            elif len(shape) == 4:
                v = v.rearrange("p (a b c d) -> p a b c d", a=shape[0], b=shape[1], c=shape[2])
            return v

        def bank(k):
            return psum[:, k, :]

        kbd = carve(B, H0, C)
        qT = carve(T)
        simS = carve(2, H0, C)
        simE = carve(2, H0 * C)
        simET = carve(2, H0 * C)
        krep = carve(B * C)
        vaug = carve(B, 2, HD + 1)
        y0 = carve(2, H0, HD)
        y0T = carve(2, P)
        mx0 = carve(2, H0)
        rden0 = carve(2, H0)
        ctxTd = carve(B * 2 * C)
        slot_raw = carve(ES // P, D)
        slot_n = carve(ES // P, D)
        smv = carve(ES // P, 2)
        sstats = carve(ES // P, 6)
        srstd = carve(3, ES // P)
        taken[0] = 0
        PT = carve(NC0, T)
        slotsT = carve(E0, B, S0)
        eo = slotsT.rearrange("p e b s -> p (e b s)").rearrange("p (b c o) -> p b c o", b=B, c=NC0)
        at_experts = taken[0]
        qb = carve(2, 2, N)
        qt = carve(2, TB, ES)
        pbuf = carve(2, ES)
        nmB = carve(2, 2)
        sumB = carve(2, 2)
        recB = carve(2, 2)
        taken[0] = at_experts
        eoT = carve(B, E0, S0)
        gel = carve(2, 512)
        h0 = carve(2, 2, 512)
        nmA = carve(NT)
        rsumA = carve(NT)
        rinvA = carve(NT)
        taken[0] = 0
        cw = carve(B * C)
        dw2 = carve(B * C)
        mx1 = carve(NT)
        s1 = carve(NT, C)
        e1 = carve(NT, C)
        e1n = carve(NT, C)
        den1 = carve(NT)
        rden1 = carve(NT)
        aT = carve(T)
        hqT = carve(T)
        xhT = carve(T)
        xcT = carve(T)
        bt = carve(N)
        btn = carve(N)
        bsm = carve(4)
        btT = carve(TB, B)
        hcT = carve(B)
        sel1 = carve(NC1 * P, dt=BF16)
        sc1 = carve(NT, E1)
        sfc = carve(NT, E1)
        t1 = carve(NT, E1)
        t2 = carve(NT, E1)
        t3 = carve(NT, E1)
        gs = carve(NT, G1)
        rank = carve(NT, G1)
        top8 = carve(NT, 8)
        rsum1 = carve(2, NT)
        rwp = carve(NT, P, dt=BF16)
        rwl = carve(NT, P, dt=BF16)
        rwT1 = carve(T, dt=BF16)
        rwT2 = carve(T, dt=BF16)
        osh = carve(T)
        sil = carve(2, 512)
        u1 = carve(2, 512)
        h1 = carve(2, 512)
        taken[0] = 0
        q2T = carve(T)
        k2T = carve(B * C)
        v2 = carve(B, D)
        s2 = carve(NT, C)
        e2 = carve(NT, C)
        mx2 = carve(NT)
        den2 = carve(NT)
        rden2 = carve(NT)
        e2T = carve(T)
        c3T = carve(T)
        xtmp = carve(2, D)
        taken[0] = 0
        sel2 = carve(NC2, P, dt=BF16)
        pr2 = carve(NT, E2)
        g2a = carve(NT, 8, 8)
        g2b = carve(NT, 8, 8)
        rank2 = carve(NT, 8)
        rs2 = carve(2, NT)
        cpk = carve(NT, P, dt=BF16)
        cT = carve(T, dt=BF16)
        r2 = carve(2, 512)
        u2 = carve(2, 512)
        h2 = carve(2, 512)
        o2T = carve(T)
        taken[0] = 0
        am3 = carve(NT)
        qs3 = carve(NT)
        rs3 = carve(NT)
        qa = carve(NT, D)
        xi = carve(NT, D, dt=BF16)
        xiT = carve(T, dt=BF16)
        rsB = carve(T)
        wa = carve(HID3)
        w1q = carve(HID3, dt=BF16)
        w2q = carve(NC3, D, dt=BF16)
        wsum = carve(2)
        wm = carve(2)
        wr = carve(2)
        hpad = carve(2, B, N + 2)
        yc = carve(2, T)
        g3 = carve(NC3, T)
        am4 = carve(NT)
        qs4 = carve(NT)
        rs4 = carve(NT)
        ga = carve(2, HID3)
        gi = carve(2, HID3, dt=BF16)
        giT = carve(2, NC3, P, dt=BF16)

        x_in = [sem(f"x_in{g}") for g in range(NG)]
        w_l0 = sem("w_l0")
        w_slots = sem("w_slots")
        w_rest = sem("w_rest")
        ew_in = [sem(f"ew_in{k}") for k in range(2)]
        w1_in = [sem(f"w1_in{k}") for k in range(2)]
        w2_in = [sem(f"w2_in{k}") for k in range(2)]
        out_done = sem("out_done")
        consts = sem("consts")
        pool_step = sem("pool_step")
        dve_step = sem("dve_step")
        act_step = sem("act_step")
        x_done = sem("x_done")
        ln_var = sem("ln_var")
        ln_rstd = sem("ln_rstd")
        ln_xn = sem("ln_xn")
        ln_tp = sem("ln_tp")
        ln_xnT = sem("ln_xnT")
        se_var = sem("se_var")
        se_rstd = sem("se_rstd")
        se_n = sem("se_n")
        se_tp = sem("se_tp")
        se_T = sem("se_T")
        kv_mm = sem("kv_mm")
        krep_done = sem("krep_done")
        vaug_done = sem("vaug_done")
        kbd_done = [sem("kbd_even"), sem("kbd_odd")]
        q_mm = sem("q_mm")
        q_sb = sem("q_sb")
        sim_ready = sem("sim_ready")
        sim_used = sem("sim_used")
        exp_done = sem("exp_done")
        et_ready = sem("et_ready")
        et_sb = sem("et_sb")
        av_ready = sem("av_ready")
        y_ready = sem("y_ready")
        yT_ready = sem("yT_ready")
        yT_sb = sem("yT_sb")
        out_ready = sem("out_ready")
        bl_ready = sem("bl_ready")
        bmax_done = sem("bmax_done")
        bexp_done = sem("bexp_done")
        brec_done = sem("brec_done")
        bnorm_done = sem("bnorm_done")
        bT_ready = sem("bT_ready")
        qt_sb = sem("qt_sb")
        al_ready = sem("al_ready")
        amax_done = sem("amax_done")
        aexp_done = sem("aexp_done")
        pT_ready = sem("pT_ready")
        pt_sb = sem("pt_sb")
        slots_mm = sem("slots_mm")
        slots_sb = sem("slots_sb")
        eg_ready = sem("eg_ready")
        eu_ready = sem("eu_ready")
        gelu_done = sem("gelu_done")
        h0_done = sem("h0_done")
        ed_ready = sem("ed_ready")
        eo_sb = sem("eo_sb")
        eoT_tp = sem("eoT_tp")
        eo_tok = [sem("eo_tok_act"), sem("eo_tok_dve")]
        comb_ready = sem("comb_ready")
        cw_done = sem("cw_done")
        dw2_mm = sem("dw2_mm")
        dw2_sb = sem("dw2_sb")
        s1_mm = sem("s1_mm")
        s1_sub = sem("s1_sub")
        e1_exp = sem("e1_exp")
        e1_norm = sem("e1_norm")
        aT_tp = sem("aT_tp")
        aT_sb = sem("aT_sb")
        hq_mm = sem("hq_mm")
        hq_sb = sem("hq_sb")
        xh_done = sem("xh_done")
        bt_tp = sem("bt_tp")
        bt_max = sem("bt_max")
        bt_exp = sem("bt_exp")
        bt_norm = sem("bt_norm")
        btT_tp = sem("btT_tp")
        btT_sb = sem("btT_sb")
        hc_mm = sem("hc_mm")
        hc_sb = sem("hc_sb")
        xc_done = sem("xc_done")
        xbias_done = sem("xbias_done")
        qv_ready = sem("qv_ready")
        rl_mm = sem("rl_mm")
        rl_sig = sem("rl_sig")
        rw_done = sem("rw_done")
        rw_tp = sem("rw_tp")
        rw_sb = sem("rw_sb")
        sg_ready = sem("sg_ready")
        sil_s = sem("sil_s")
        hs_done = sem("hs_done")
        sd_ready = sem("sd_ready")
        osh_done = sem("osh_done")
        sel1_done = sem("sel1_done")
        g1_ready = sem("g1_ready")
        u1_ready = sem("u1_ready")
        sil1_done = sem("sil1_done")
        u1_done = sem("u1_done")
        h1_done = sem("h1_done")
        d1_done = sem("d1_done")
        o1_done = sem("o1_done")
        o1_tp = sem("o1_tp")
        qk2_mm = sem("qk2_mm")
        qk2_sb = sem("qk2_sb")
        v2_mm = sem("v2_mm")
        v2_sb = sem("v2_sb")
        s2_mm = sem("s2_mm")
        s2_sub = sem("s2_sub")
        e2_exp = sem("e2_exp")
        rden2_done = sem("rden2_done")
        e2_tp = sem("e2_tp")
        e2_sb = sem("e2_sb")
        av2_ready = sem("av2_ready")
        c3_mm = sem("c3_mm")
        c3_sb = sem("c3_sb")
        sel2_done = sem("sel2_done")
        h2_ready = sem("h2_ready")
        r2_done = sem("r2_done")
        u2_done = sem("u2_done")
        h2_done = sem("h2_done")
        d2_done = sem("d2_done")
        o2_sb = sem("o2_sb")
        o2_tp = sem("o2_tp")
        wsum_done = sem("wsum_done")
        wsum_mm = sem("wsum_mm")
        wq_done = sem("wq_done")
        rs3_done = sem("rs3_done")
        xi_done = sem("xi_done")
        xi_tp = sem("xi_tp")
        xi_sb = sem("xi_sb")
        rsB_mm = sem("rsB_mm")
        rsB_sb = sem("rsB_sb")
        l1_ready = sem("l1_ready")
        hpad_done = sem("hpad_done")
        conv_done = sem("conv_done")
        g3_done = sem("g3_done")
        g3_tp = sem("g3_tp")
        qs4_done = sem("qs4_done")
        ga_done = sem("ga_done")
        gi_done = sem("gi_done")
        gi_tp = sem("gi_tp")
        gi_sb = sem("gi_sb")
        l2_ready = sem("l2_ready")
        hpad_zero = sem("hpad_zero")

        block = ctx.enter_context(nc.Block())

        def wide(ap, *shape):
            return ap.broadcast_to([P, *shape])

        N_L0 = 9
        REST = ["wqv", "gw1", "sgT", "suT", "sdT", "wq2", "wk2", "wv2", "rw2", "wq3", "wk3", "wv3", "wo3", "w1f", "w2f"]

        @block.sync
        def _(sp):
            xt = A["x"].rearrange("(t p) d -> p t d", p=P)
            for g in range(NG):
                sp.dma_start(X[:, 4 * g:4 * g + 4, :], xt[:, 4 * g:4 * g + 4, :]).then_inc(x_in[g], 16)
            for dst, src in ((ctxT[:, :], A["ctxT"]), (ctxTd, A["ctxTd"]), (wk0[:, :], A["wk0"]), (wv0[:, :], A["wv0"]),
                             (wq0[:, :], A["wq0"]), (cols[:, :], A["cols"]), (scal[:, :], A["scal"].partition_broadcast(P)),
                             (wo0[:, :], A["wo0"]), (rows[:, :, :], A["rows"].partition_broadcast(P))):
                sp.dma_start(dst, src).then_inc(w_l0, 16)
            sp.dma_start(slot_raw, A["slots"].rearrange("(t p) d -> p t d", p=P)).then_inc(w_slots, 16)
            for k in range(2):
                sp.dma_start(ew[:, k, :], A["ew"][k, :, :]).then_inc(ew_in[k], 16)
                sp.dma_start(w1ring[:, k, :], A["w1"][k, :, :]).then_inc(w1_in[k], 16)
                sp.dma_start(w2ring[:, k, :], A["w2"][k, :, :]).then_inc(w2_in[k], 16)
            sp.dma_start(ctx_tok[:, :, :], A["ctx"].rearrange("(b j) d -> j b d", j=C)).then_inc(w_rest, 16)
            sp.dma_start(gbias[:, :], A["gbias"].partition_broadcast(P)).then_inc(w_rest, 16)
            for dst, name in ((wqv, "wqv"), (gw1, "gw1"), (sgT, "sgT"), (suT, "suT"), (sdT, "sdT"), (wq2, "wq2"), (wk2, "wk2"),
                              (wv2, "wv2"), (rw2, "rw2"), (wq3, "wq3"), (wk3, "wk3"), (wv3, "wv3"), (wo3, "wo3"), (w1f, "w1f"),
                              (w2f, "w2f")):
                whole = dst[:, :, :] if len(A[name].shape) == 3 else dst[:, :]
                sp.dma_start(whole, A[name]).then_inc(w_rest, 16)
            if LAYERS > 1:
                with sp.Fori(0, E0 // 2 - 1) as i:
                    for k in range(2):
                        sp.wait_ge(eo_sb, i * 2 + (k + 1))
                        sp.dma_start(ew[:, k, :], A["ew"][bass.ds(i * 2 + (k + 2), 1), :, :].rearrange("a p n -> (a p) n")).then_inc(ew_in[k], 16)
            if LAYERS > 3:
                with sp.Fori(0, NC1 // 2 - 1) as i:
                    for k in range(2):
                        sp.wait_ge(d1_done, i * 4 + 2 * (k + 1))
                        sp.dma_start(w1ring[:, k, :], A["w1"][bass.ds(i * 2 + (k + 2), 1), :, :].rearrange("a p n -> (a p) n")).then_inc(w1_in[k], 16)
                for k in range(2):
                    sp.wait_ge(d1_done, 2 * (NC1 - 2 + k + 1))
                    sp.dma_start(w1ring[:, k, :], A["w1"][k, :, :]).then_inc(w1_in[k], 16)
                with sp.Fori(0, NC1 // 2 - 1) as i:
                    for k in range(2):
                        sp.wait_ge(d1_done, i * 4 + (2 * NC1 + 2 * (k + 1)))
                        sp.dma_start(w1ring[:, k, :], A["w1"][bass.ds(i * 2 + (k + 2), 1), :, :].rearrange("a p n -> (a p) n")).then_inc(w1_in[k], 16)
            if LAYERS > 5:
                with sp.Fori(0, NC2 // 2 - 1) as i:
                    for k in range(2):
                        sp.wait_ge(d2_done, i * 8 + 4 * (k + 1))
                        sp.dma_start(w2ring[:, k, :], A["w2"][bass.ds(i * 2 + (k + 2), 1), :, :].rearrange("a p n -> (a p) n")).then_inc(w2_in[k], 16)
            ot = out.rearrange("(t p) d -> p t d", p=P)
            for g in range(NG):
                sp.wait_ge(x_done, (LAYERS - 1) * NT + 4 * g + 4)
                sp.dma_start(ot[:, 4 * g:4 * g + 4, :], X[:, 4 * g:4 * g + 4, :]).then_inc(out_done, 16)
            sp.wait_ge(out_done, 16 * NG)

        @block.gpsimd
        def _(pool):
            step = [0]

            def then(ins):
                step[0] += 1
                ins.then_inc(pool_step, 1)
                pool.wait_ge(pool_step, step[0])

            pool.memset(neghalf[:, :], -0.5)
            pool.memset(epst[:, :], EPS)
            pool.memset(ones[:, :], 1.0)
            then(pool.memset(ident[:, :], 0.0))
            then(pool.affine_select(out=ident[:, :], in_=ident[:, :], compare_op=ALU.not_equal, fill=1.0, base=0,
                                    pattern=[[-1, P]], channel_multiplier=1))
            pool.memset(headmask[:, :], 1.0)
            then(pool.memset(ltmask[:, :, :], 1.0))
            then(pool.affine_select(out=headmask[:, :], in_=headmask[:, :], compare_op=ALU.is_ge, fill=0.0, base=0,
                                    pattern=[[-HD, H0]], channel_multiplier=1))
            then(pool.affine_select(out=headmask[:, :], in_=headmask[:, :], compare_op=ALU.is_ge, fill=0.0, base=HD - 1,
                                    pattern=[[HD, H0]], channel_multiplier=-1))
            then(pool.affine_select(out=ltmask[:, :, :], in_=ltmask[:, :, :], compare_op=ALU.is_ge, fill=0.0, base=-1,
                                    pattern=[[1, 8], [-1, 8]], channel_multiplier=0))
            then(pool.memset(vaug, 0.0))
            pool.memset(vaug[0:C, :, 0, HD:HD + 1], 1.0)
            then(pool.memset(vaug[C:P, :, 1, HD:HD + 1], 1.0))
            pool.tensor_copy(identb[:, :], ident[:, :]).then_inc(consts, 1)

            def ln_power(L, g):
                s = slice(4 * g, 4 * g + 4)
                pool.wait_ge(ln_var, NG * L + g + 1)
                if L != 1:
                    pool.tensor_tensor(rstd[:, s], veps[:, s], neghalf[:, s], ALU.pow).then_inc(ln_rstd, 1)
                    return
                then(pool.tensor_tensor(rtmp[:, s], veps[:, s], neghalf[:, s], ALU.pow))
                then(pool.tensor_tensor(rstd[:, s], rtmp[:, s], rtmp[:, s], ALU.mult))
                then(pool.tensor_tensor(rstd[:, s], rstd[:, s], mv[:, s, 1], ALU.mult))
                then(pool.tensor_tensor(rstd[:, s], rstd[:, s], epst[:, s], ALU.add))
                then(pool.tensor_tensor(rstd[:, s], rstd[:, s], neghalf[:, s], ALU.pow))
                pool.tensor_tensor(rstd[:, s], rstd[:, s], rtmp[:, s], ALU.mult).then_inc(ln_rstd, 1)

            for L in range(LAYERS):
                for g in range(NG):
                    ln_power(L, g)
                if L == 0:
                    pool.wait_ge(krep_done, 1)
                    for b in range(1, B, 2):
                        pool.tensor_tensor(kbd[:, b], wide(krep[:, b * C:(b + 1) * C].unsqueeze(1), H0, C),
                                           wide(headmask[:, :].unsqueeze(2), H0, C), ALU.mult).then_inc(kbd_done[1], 1)
                    pool.wait_ge(se_var, 1)
                    pool.tensor_tensor(srstd[:, 1, :], srstd[:, 0, :], neghalf[:, 0:ES // P], ALU.pow).then_inc(se_rstd, 1)
                if L == 1:
                    for k in range(4 * B):
                        pool.wait_ge(brec_done, k + 1)
                        pool.tensor_tensor(qb[:, k % 2], qb[:, k % 2], wide(recB[:, k % 2].unsqueeze(2), 2, N), ALU.mult)\
                            .then_inc(bnorm_done, 1)
                if L == 2:
                    pool.wait_ge(ln_xn, NG * L + NG)
                    pool.tensor_tensor(X[:, :, :], X[:, :, :], wide(rows[:, ROW["qv1_b"], :].unsqueeze(1), NT, D), ALU.add)\
                        .then_inc(xbias_done, 1)
                    then(pool.memset(sel1, 0.0))
                    for base in (0, -E1):
                        then(pool.affine_select(out=sel1.rearrange("p (e i) -> p e i", i=I1), in_=sel1.rearrange("p (e i) -> p e i", i=I1),
                                                compare_op=ALU.not_equal, fill=1.0, base=base,
                                                pattern=[[-1, E1], [0, I1]], channel_multiplier=1))
                    pool.memset(rwl, 0.0).then_inc(sel1_done, 1)
                if L == 5:
                    pool.wait_ge(x_done, NT * L)
                    pool.memset(cpk, 0.0)
                    then(pool.memset(sel2, 0.0))
                    wide2 = sel2[:, 4:12, :].rearrange("p (e c) n -> p e (c n)", c=2)
                    for part in range(3):
                        then(pool.affine_select(out=sel2[:, 0:4, :], in_=sel2[:, 0:4, :], compare_op=ALU.not_equal, fill=1.0,
                                                base=-E2 * part, pattern=[[-1, 4], [0, P]], channel_multiplier=1))
                        last = pool.affine_select(out=wide2, in_=wide2, compare_op=ALU.not_equal, fill=1.0,
                                                  base=-E2 * part - 4, pattern=[[-1, 4], [0, 2 * P]], channel_multiplier=1)
                        if part < 2:
                            then(last)
                    last.then_inc(sel2_done, 1)
                if L == 6:
                    pool.wait_ge(ln_xn, NG * L + NG)
                    pool.tensor_tensor(X[:, :, :], X[:, :, :], wide(rows[:, ROW["o3_b"], :].unsqueeze(1), NT, D), ALU.add)\
                        .then_inc(xbias_done, 1)
                if L == 7:
                    pool.wait_ge(x_done, NT * L)
                    pool.memset(hpad, 0.0).then_inc(hpad_zero, 1)

        @block.scalar
        def _(act):
            def copy(dst, src):
                return act.activation(dst, src, ACT.Copy)

            def ln_evac(L):
                for g in range(NG):
                    act.wait_ge(ln_tp, NG * L + g + 1)
                    dst = xnT[:, 512 * g:512 * g + 512]
                    if L == 1:
                        ins = act.activation(dst, bank(6 + g % 2), ACT.Identity, scale=cols[:, COL["norm_g"]:COL["norm_g"] + 1],
                                             bias=cols[:, COL["norm_b"]:COL["norm_b"] + 1])
                    else:
                        ins = copy(dst, bank(6 + g % 2))
                    ins.then_inc(ln_xnT, 1)

            act.wait_ge(kv_mm, 1)
            copy(krep, bank(0)).then_inc(krep_done, 1)
            act.wait_ge(consts, 1)
            vps = psum[:, 1, 0:B * HD].rearrange("p (b d) -> p b d", b=B)
            copy(vaug[0:C, :, 0, 0:HD], vps[0:C])
            copy(vaug[C:P, :, 1, 0:HD], vps[C:P]).then_inc(vaug_done, 1)
            ln_evac(0)
            for g in range(NG):
                act.wait_ge(q_mm, g + 1)
                act.activation(qT[:, 512 * g:512 * g + 512], bank(2 + g), ACT.Copy, scale=float(HD) ** -0.5).then_inc(q_sb, 1)
            act.wait_ge(se_n, 2)
            for g in range(2):
                act.wait_ge(se_tp, g + 1)
                act.activation(seT[:, 512 * g:512 * g + 512], bank(6 + g), ACT.Identity, scale=slot_gs[:, 0:1], bias=slot_gs[:, 1:2])\
                    .then_inc(se_T, 1)
            for t in range(NT + 2):
                if t >= 2:
                    act.wait_ge(yT_ready, t - 1)
                    if t >= 4:
                        act.wait_ge(out_ready, t - 3)
                    copy(y0T[:, t % 2, :], psum[:, 6, 256:384]).then_inc(yT_sb, 1)
                if 1 <= t <= NT:
                    act.wait_ge(et_ready, t)
                    if t >= 3:
                        act.wait_ge(av_ready, t - 2)
                    copy(simET[:, (t - 1) % 2, :], psum[:, 4:6, :].rearrange("p a n -> p (a n)")).then_inc(et_sb, 1)
                if t < NT:
                    act.wait_ge(sim_used, t + 1)
                    if t >= 2:
                        act.wait_ge(et_ready, t - 1)
                    act.activation(simE[:, t % 2, :], simS[:, t % 2].rearrange("p h k -> p (h k)"), ACT.Exp).then_inc(exp_done, 1)

            act.wait_ge(x_done, NT)
            ln_evac(1)

            def bexp(k):
                act.wait_ge(bmax_done, k + 1)
                if k >= 2:
                    act.wait_ge(bT_ready, k - 1)
                for c in range(2):
                    last = act.activation(qb[:, k % 2, c, :], psum[:, k % 2, c * N:(c + 1) * N], ACT.Exp,
                                          bias=nmB[:, k % 2, c:c + 1], accum_out=sumB[:, k % 2, c:c + 1])
                last.then_inc(bexp_done, 1)

            def aexp(t):
                act.wait_ge(amax_done, t + 1)
                if t >= 2:
                    act.wait_ge(pT_ready, t - 1)
                act.activation(pbuf[:, t % 2, :], psum[:, 2:4, :].rearrange("p a n -> p (a n)"), ACT.Exp, bias=nmA[:, t:t + 1],
                               accum_out=rsumA[:, t:t + 1]).then_inc(aexp_done, 1)

            def pt_evac(t):
                act.wait_ge(pT_ready, t + 1)
                copy(PT[:, :, t * P:(t + 1) * P], psum[:, 4:6, :].rearrange("p a (c n) -> p (a c) n", c=4)).then_inc(pt_sb, 1)

            def slots_evac(b, hf):
                act.wait_ge(slots_mm, 2 * b + hf + 1)
                act.activation(slotsT[:, 8 * hf:8 * hf + 8, b, :], bank(6 + hf).rearrange("p (e s) -> p e s", s=S0), ACT.Identity,
                               scale=cols[:, COL["norm_g"]:COL["norm_g"] + 1], bias=cols[:, COL["norm_b"]:COL["norm_b"] + 1])\
                    .then_inc(slots_sb, 1)

            for b in range(B):
                bexp(4 * b)
                bexp(4 * b + 1)
                aexp(2 * b)
                bexp(4 * b + 2)
                bexp(4 * b + 3)
                pt_evac(2 * b)
                aexp(2 * b + 1)
                pt_evac(2 * b + 1)
                slots_evac(b, 0)
                slots_evac(b, 1)

            def gelu(e, f, k):
                n = 2 * e + f
                act.wait_ge(eg_ready, n + 1)
                if not isinstance(n, int) or n >= 2:
                    act.wait_ge(h0_done, n - 1)
                act.activation(gel[:, f, :], bank(f), ACT.Gelu, bias=ew[:, k, 3 * F0 + f:3 * F0 + f + 1]).then_inc(gelu_done, 1)

            def eo_evac(e, k):
                act.wait_ge(ed_ready, e + 1)
                act.activation(eoT[:, :, bass.ds(e, 1), :].rearrange("p b a s -> p b (a s)"),
                               bank(4 + k).rearrange("p (b s) -> p b s", s=S0), ACT.Identity,
                               bias=ew[:, k, 3 * F0 + 4:3 * F0 + 5]).then_inc(eo_sb, 1)

            def expert_pair(i, first):
                for k in range(2):
                    gelu(i * 2 + k, 0, k)
                    if not (first and k == 0):
                        eo_evac(i * 2 + (k - 1), 1 - k)
                    gelu(i * 2 + k, 1, k)

            expert_pair(0, True)
            with act.Fori(1, E0 // 2) as i:
                expert_pair(i, False)
            eo_evac(E0 - 1, 1)
            for q in range(0, 2 * B, 2):
                act.wait_ge(eoT_tp, q + 1)
                copy(eo[:, q // 2, 4 * (q % 2):4 * (q % 2) + 4, :].rearrange("p c o -> p (c o)"), bank(q % 4)).then_inc(eo_tok[0], 1)

            act.wait_ge(x_done, 2 * NT)
            act.wait_ge(dw2_mm, 1)
            act.activation(dw2[0:1, :], psum[0:1, 0, :], ACT.Identity, bias=scal[0:1, 1:2]).then_inc(dw2_sb, 1)
            ln_evac(2)
            for hf in range(2):
                act.wait_ge(s1_sub, hf + 1)
                act.activation(e1[:, 8 * hf:8 * hf + 8, :], s1[:, 8 * hf:8 * hf + 8, :], ACT.Exp).then_inc(e1_exp, 1)
            act.wait_ge(bt_max, 1)
            act.activation(bt[0:B, :], psum[0:B, 7, 0:N], ACT.Exp, bias=bsm[0:B, 0:1], accum_out=bsm[0:B, 1:2]).then_inc(bt_exp, 1)
            for g in range(NG):
                act.wait_ge(aT_tp, g + 1)
                copy(aT[0:C, 512 * g:512 * g + 512], psum[0:C, 2 + g, :]).then_inc(aT_sb, 1)
            act.wait_ge(btT_tp, 1)
            copy(btT, psum[:, 7, 256:256 + TB * B].rearrange("p (k b) -> p k b", k=TB)).then_inc(btT_sb, 1)
            act.wait_ge(hc_mm, 1)
            copy(hcT, psum[:, 7, 288:288 + B]).then_inc(hc_sb, 1)
            for g in range(NG):
                act.wait_ge(hq_mm, g + 1)
                copy(hqT[:, 512 * g:512 * g + 512], bank((6, 0, 1, 2)[g])).then_inc(hq_sb, 1)

            act.wait_ge(x_done, 3 * NT)
            ln_evac(3)
            for hf in range(2):
                act.wait_ge(rl_mm, hf + 1)
                act.activation(sc1[:, 8 * hf:8 * hf + 8, :], bank(hf).rearrange("p (t e) -> p t e", e=E1), ACT.Sigmoid).then_inc(rl_sig, 1)
            for m in range(2 * NG):
                act.wait_ge(sg_ready, m + 1)
                if m >= 2:
                    act.wait_ge(hs_done, m - 1)
                act.activation(sil[0:I1, m % 2, :], psum[0:I1, 2 + m % 2, :], ACT.Silu).then_inc(sil_s, 1)
            for q in range(4):
                act.wait_ge(rw_tp, q + 1)
                dst = (rwT1, rwT2)[q // 2][:, 1024 * (q % 2):1024 * (q % 2) + 1024]
                copy(dst, bank(q).bitcast(BF16)).then_inc(rw_sb, 1)

            def silu1(n, k, first):
                act.wait_ge(g1_ready, n + 1)
                if not first:
                    act.wait_ge(h1_done, n - 1)
                act.activation(sil[:, k, :], bank(k), ACT.Silu).then_inc(sil1_done, 1)

            for hf in range(2):
                for s in range(4):
                    silu1(2 * NC1 * hf + s, s % 2, hf == 0 and s < 2)
                with act.Fori(1, NC1 // 2) as i:
                    for s in range(4):
                        silu1(i * 4 + (2 * NC1 * hf + s), s % 2, False)

            def attention_tail(L, base):
                act.wait_ge(s2_sub, base + 1)
                for hf in range(2):
                    act.wait_ge(s2_sub, base + hf + 1)
                    act.activation(e2[:, 8 * hf:8 * hf + 8, :], s2[:, 8 * hf:8 * hf + 8, :], ACT.Exp).then_inc(e2_exp, 1)
                for g in range(NG):
                    act.wait_ge(e2_tp, 2 * base + g + 1)
                    copy(e2T[0:C, 512 * g:512 * g + 512], psum[0:C, 2 + g, :]).then_inc(e2_sb, 1)

            act.wait_ge(x_done, 4 * NT)
            ln_evac(4)
            attention_tail(4, 0)

            act.wait_ge(x_done, 5 * NT)
            ln_evac(5)
            act.wait_ge(rl_mm, 3)
            act.activation(pr2, psum[:, 0, 0:NT * E2].rearrange("p (t e) -> p t e", e=E2), ACT.Sigmoid).then_inc(rl_sig, 1)
            for q in range(2):
                act.wait_ge(rw_tp, 4 + q + 1)
                copy(cT[:, 1024 * q:1024 * q + 1024], bank(1 + q).bitcast(BF16)).then_inc(rw_sb, 1)

            def relu2(n, k, first):
                act.wait_ge(h2_ready, n + 1)
                if not first:
                    act.wait_ge(h2_done, n - 1)
                act.activation(r2[:, k, :], bank(k), ACT.Relu).then_inc(r2_done, 1)

            for s in range(8):
                relu2(s, s % 2, s < 2)
            with act.Fori(1, NC2 // 2) as i:
                for s in range(8):
                    relu2(i * 8 + s, s % 2, False)
            act.wait_ge(d2_done, 4 * NC2)
            for q in range(NG):
                copy(o2T[:, 512 * q:512 * q + 512], bank(4 + q)).then_inc(o2_sb, 1)

            act.wait_ge(x_done, 6 * NT)
            ln_evac(6)
            attention_tail(6, 2)
            for g in range(NG):
                act.wait_ge(c3_mm, g + 1)
                copy(c3T[:, 512 * g:512 * g + 512], bank((0, 1, 2, 3)[g])).then_inc(c3_sb, 1)

            act.wait_ge(x_done, 7 * NT)
            for g in range(2):
                act.wait_ge(xi_tp, g + 1)
                copy(xiT[:, 1024 * g:1024 * g + 1024], bank(g).bitcast(BF16)).then_inc(xi_sb, 1)
            act.wait_ge(wq_done, 1)
            for g in range(NG):
                act.wait_ge(rsB_mm, g + 1)
                act.activation(rsB[:, 512 * g:512 * g + 512], bank(2 + g), ACT.Copy, scale=wm[:, 0:1]).then_inc(rsB_sb, 1)
            for c in range(NC3):
                act.wait_ge(conv_done, c + 1)
                act.activation(g3[:, c, :], yc[:, c % 2, :], ACT.Silu).then_inc(g3_done, 1)
            for t in range(NT + 1):
                if t < NT:
                    act.wait_ge(qs4_done, t + 1)
                    if t >= 2:
                        act.wait_ge(gi_done, t - 1)
                    act.activation(ga[:, t % 2, :], bank(t % 4), ACT.Copy, scale=qs4[:, t:t + 1]).then_inc(ga_done, 1)
                if t >= 1:
                    act.wait_ge(gi_tp, t)
                    if t >= 3:
                        act.wait_ge(l2_ready, t - 2)
                    copy(giT[:, (t - 1) % 2], psum[:, 4 + (t - 1) % 2, 0:NC3 * P // 2].bitcast(BF16).rearrange("p (c n) -> p c n", c=NC3))\
                        .then_inc(gi_sb, 1)

        @block.vector
        def _(dve):
            step = [0]

            def then(ins):
                step[0] += 1
                ins.then_inc(dve_step, 1)
                dve.wait_ge(dve_step, step[0])

            def ln_stats(L, g):
                ts = range(4 * g, 4 * g + 4)
                if L == 0:
                    dve.wait_ge(x_in[g], 16)
                if L > 0:
                    dve.wait_ge(x_done, NT * L)
                for t in ts:
                    last = dve.bn_stats(stats[:, t, :], X[:, t, :])
                then(last)
                for t in ts:
                    last = dve.bn_aggr(mv[:, t, :], stats[:, t, :])
                then(last)
                s = slice(4 * g, 4 * g + 4)
                dve.tensor_scalar(veps[:, s], mv[:, s, 1], EPS, None, ALU.add).then_inc(ln_var, 1)

            def ln_apply(L, g):
                dve.wait_ge(ln_rstd, NG * L + g + 1)
                for t in range(4 * g, 4 * g + 4):
                    last = dve.tensor_scalar(xn[:, t, :], X[:, t, :], mv[:, t, 0:1], rstd[:, t:t + 1], ALU.subtract, ALU.mult)
                last.then_inc(ln_xn, 1)

            def layer_norm(L):
                ln_stats(L, 0)
                for g in range(1, NG):
                    ln_stats(L, g)
                    ln_apply(L, g - 1)
                ln_apply(L, NG - 1)

            layer_norm(0)
            dve.wait_ge(krep_done, 1)
            dve.wait_ge(consts, 1)
            for b in range(0, B, 2):
                dve.tensor_tensor(kbd[:, b], wide(krep[:, b * C:(b + 1) * C].unsqueeze(1), H0, C),
                                  wide(headmask[:, :].unsqueeze(2), H0, C), ALU.mult).then_inc(kbd_done[0], 1)
            dve.wait_ge(w_slots, 16)
            for t in range(ES // P):
                last = dve.bn_stats(sstats[:, t, :], slot_raw[:, t, :])
            then(last)
            for t in range(ES // P):
                last = dve.bn_aggr(smv[:, t, :], sstats[:, t, :])
            then(last)
            dve.tensor_scalar(srstd[:, 0, :], smv[:, :, 1], EPS, None, ALU.add).then_inc(se_var, 1)
            dve.wait_ge(w_l0, 16 * N_L0)
            dve.tensor_scalar(slot_gs[:, :], cols[:, COL["slot_g"]:COL["slot_g"] + 2], scal[:, 0:1], None, ALU.mult).then_inc(se_n, 1)
            dve.wait_ge(se_rstd, 1)
            for t in range(ES // P):
                last = dve.tensor_scalar(slot_n[:, t, :], slot_raw[:, t, :], smv[:, t, 0:1], srstd[:, 1, t:t + 1], ALU.subtract, ALU.mult)
            last.then_inc(se_n, 1)
            for t in range(NT + 2):
                if t < NT:
                    dve.wait_ge(sim_ready, t + 1)
                    sim = psum[:, 2 * (t % 2):2 * (t % 2) + 2, :].rearrange("p a (h k) -> p (a h) k", k=C)
                    then(dve.tensor_reduce(mx0[:, t % 2, :], sim, AX.X, ALU.max))
                    if t >= 2:
                        dve.wait_ge(exp_done, t - 1)
                    dve.tensor_tensor(simS[:, t % 2], sim, wide(mx0[:, t % 2, :].unsqueeze(2), H0, C), ALU.subtract).then_inc(sim_used, 1)
                if 1 <= t <= NT:
                    dve.wait_ge(av_ready, t)
                    av = psum[:, 6, 0:H0 * (HD + 1)].rearrange("p (h k) -> p h k", k=HD + 1)
                    then(dve.reciprocal(rden0[:, t % 2, :], av[:, :, HD]))
                    if t >= 3:
                        dve.wait_ge(yT_ready, t - 2)
                    dve.tensor_tensor(y0[:, (t - 1) % 2], av[:, :, 0:HD], wide(rden0[:, t % 2, :].unsqueeze(2), H0, HD), ALU.mult)\
                        .then_inc(y_ready, 1)
                if t >= 2:
                    dve.wait_ge(out_ready, t - 1)
                    dve.tensor_tensor(X[:, t - 2, :], X[:, t - 2, :], psum[:, 7, 0:D], ALU.add).then_inc(x_done, 1)

            layer_norm(1)

            def bmax(k):
                dve.wait_ge(bl_ready, k + 1)
                if k >= 2:
                    dve.wait_ge(bexp_done, k - 1)
                dve.tensor_reduce(nmB[:, k % 2, :], bank(k % 2).rearrange("p (c n) -> p c n", c=2), AX.X, ALU.max, negate=True)\
                    .then_inc(bmax_done, 1)

            def brec(k):
                dve.wait_ge(bexp_done, k + 1)
                if k >= 2:
                    dve.wait_ge(bnorm_done, k - 1)
                dve.reciprocal(recB[:, k % 2, :], sumB[:, k % 2, :]).then_inc(brec_done, 1)

            def amax(t):
                dve.wait_ge(al_ready, t + 1)
                dve.tensor_reduce(nmA[:, t:t + 1], psum[:, 2:4, :].rearrange("p a n -> p (a n)"), AX.X, ALU.max, negate=True)\
                    .then_inc(amax_done, 1)

            def qt_evac(b, j):
                k = 4 * b + j
                dve.wait_ge(bT_ready, k + 1)
                if b >= 2:
                    dve.wait_ge(slots_mm, 2 * (b - 1))
                dve.tensor_copy(qt[:, b % 2, :, N * j:N * j + N], bank(4 + j % 2).rearrange("p (a n) -> p a n", a=TB)).then_inc(qt_sb, 1)

            for b in range(B):
                k = 4 * b
                bmax(k)
                bmax(k + 1)
                brec(k)
                amax(2 * b)
                brec(k + 1)
                qt_evac(b, 0)
                bmax(k + 2)
                qt_evac(b, 1)
                bmax(k + 3)
                brec(k + 2)
                brec(k + 3)
                qt_evac(b, 2)
                amax(2 * b + 1)
                qt_evac(b, 3)
            dve.wait_ge(aexp_done, NT)
            dve.reciprocal(rinvA, rsumA)

            def hidden0(e, f, k, first):
                n = 2 * e + f
                dve.wait_ge(eu_ready, n + 1)
                dve.wait_ge(gelu_done, n + 1)
                if not first:
                    dve.wait_ge(ed_ready, e - 1)
                dve.scalar_tensor_tensor(h0[:, k, f, :], bank(2 + f), ew[:, k, 3 * F0 + 2 + f:3 * F0 + 3 + f], gel[:, f, :],
                                         ALU.add, ALU.mult).then_inc(h0_done, 1)

            for e in range(2):
                for f in range(2):
                    hidden0(e, f, e, True)
            with dve.Fori(1, E0 // 2) as i:
                for k in range(2):
                    for f in range(2):
                        hidden0(i * 2 + k, f, k, False)
            for q in range(1, 2 * B, 2):
                dve.wait_ge(eoT_tp, q + 1)
                dve.tensor_copy(eo[:, q // 2, 4 * (q % 2):4 * (q % 2) + 4, :].rearrange("p c o -> p (c o)"), bank(q % 4)).then_inc(eo_tok[1], 1)
            for t in range(NT):
                dve.wait_ge(comb_ready, t + 1)
                dve.scalar_tensor_tensor(X[:, t, :], psum[:, 4 + t % 4, 0:D], rinvA[:, t:t + 1], X[:, t, :], ALU.mult, ALU.add)\
                    .then_inc(x_done, 1)

            dve.wait_ge(w_rest, 16 * (len(REST) + 2))
            dve.tensor_scalar(cw, ctxT[:, :], cols[:, COL["w_sim3"]:COL["w_sim3"] + 1], cols[:, COL["w_sim1"]:COL["w_sim1"] + 1],
                              ALU.mult, ALU.add).then_inc(cw_done, 1)
            layer_norm(2)
            for hf in range(2):
                r = slice(8 * hf, 8 * hf + 8)
                sim = bank(hf).rearrange("p (t j) -> p t j", j=C)
                dve.wait_ge(s1_mm, hf + 1)
                then(dve.tensor_reduce(mx1[:, r], sim, AX.X, ALU.max))
                dve.tensor_tensor(s1[:, r, :], sim, wide(mx1[:, r].unsqueeze(2), 8, C), ALU.subtract).then_inc(s1_sub, 1)
            for hf in range(2):
                r = slice(8 * hf, 8 * hf + 8)
                dve.wait_ge(e1_exp, hf + 1)
                then(dve.tensor_reduce(den1[:, r], e1[:, r, :], AX.X, ALU.add))
                then(dve.reciprocal(rden1[:, r], den1[:, r]))
                dve.tensor_tensor(e1n[:, r, :], e1[:, r, :], wide(rden1[:, r].unsqueeze(2), 8, C), ALU.mult).then_inc(e1_norm, 1)
                if hf == 0:
                    dve.wait_ge(bt_tp, 1)
                    dve.tensor_reduce(bsm[0:B, 0:1], psum[0:B, 7, 0:N], AX.X, ALU.max, negate=True).then_inc(bt_max, 1)
            dve.wait_ge(bt_exp, 1)
            then(dve.reciprocal(bsm[0:B, 2:3], bsm[0:B, 1:2]))
            dve.tensor_scalar(btn[0:B, :], bt[0:B, :], bsm[0:B, 2:3], None, ALU.mult).then_inc(bt_norm, 1)
            dve.wait_ge(hc_sb, 1)
            for b in range(B):
                last = dve.tensor_scalar(xcT[:, N * b:N * b + N], xnT[:, N * b:N * b + N], hcT[:, b:b + 1], None, ALU.mult)
            last.then_inc(xc_done, 1)
            for g in range(NG):
                r = slice(512 * g, 512 * g + 512)
                dve.wait_ge(hq_sb, g + 1)
                dve.tensor_tensor(xhT[:, r], hqT[:, r], xnT[:, r], ALU.mult).then_inc(xh_done, 1)
            dve.wait_ge(xbias_done, 1)
            for t in range(NT):
                dve.wait_ge(qv_ready, t + 1)
                dve.tensor_tensor(X[:, t, :], psum[:, 3 + t % 3, 0:D], X[:, t, :], ALU.add).then_inc(x_done, 1)

            def rank_of(dst, v, a, b2, n):
                own = wide(v.unsqueeze(3), n, 8, 8)
                other = wide(v.unsqueeze(2), n, 8, 8)
                dve.tensor_tensor(b2, other, own, ALU.is_equal)
                then(dve.tensor_tensor(a, other, own, ALU.is_gt))
                then(dve.tensor_tensor(b2, b2, wide(ltmask[:, :, :].unsqueeze(1), n, 8, 8), ALU.mult))
                then(dve.tensor_tensor(a, a, b2, ALU.add))
                then(dve.tensor_reduce(dst, a, AX.X, ALU.add))

            layer_norm(3)

            def routing():
                dve.wait_ge(rl_sig, 2)
                then(dve.tensor_tensor(sfc, sc1, wide(gbias[:, :].unsqueeze(1), NT, E1), ALU.add))
                v = sfc.rearrange("p t (g j) -> p (t g) j", j=8)
                hi = t1.rearrange("p t (g j) -> p (t g) j", j=8)
                lo = t2.rearrange("p t (g j) -> p (t g) j", j=8)
                tmp = t3.rearrange("p t (g j) -> p (t g) j", j=8)
                dve.tensor_tensor(hi[:, :, 0:4], v[:, :, 0:4], v[:, :, 4:8], ALU.max)
                then(dve.tensor_tensor(lo[:, :, 0:4], v[:, :, 0:4], v[:, :, 4:8], ALU.min))
                at = 0
                for k in (2, 1):
                    x0, x1, y = slice(at, at + k), slice(at + k, at + 2 * k), slice(at + 2 * k, at + 3 * k)
                    dve.tensor_tensor(tmp[:, :, 0:k], hi[:, :, x0], hi[:, :, x1], ALU.min)
                    dve.tensor_tensor(tmp[:, :, 4:4 + k], lo[:, :, x0], lo[:, :, x1], ALU.max)
                    then(dve.tensor_tensor(hi[:, :, y], hi[:, :, x0], hi[:, :, x1], ALU.max))
                    then(dve.tensor_tensor(lo[:, :, y], tmp[:, :, 0:k], tmp[:, :, 4:4 + k], ALU.max))
                    at += 2 * k
                then(dve.tensor_tensor(gs.rearrange("p t g -> p (t g)"), hi[:, :, at], lo[:, :, at], ALU.add))
                rank_of(rank, gs, t1.rearrange("p t (g j) -> p t g j", j=8), t2.rearrange("p t (g j) -> p t g j", j=8), NT)
                then(dve.tensor_scalar(rank, rank, 3.5, None, ALU.is_lt))
                then(dve.tensor_tensor(t1.rearrange("p t (g j) -> p t g j", j=8), sfc.rearrange("p t (g j) -> p t g j", j=8),
                                       wide(rank.unsqueeze(3), NT, 8, 8), ALU.mult))
                for t in range(NT):
                    last = dve.max(top8[:, t, :], t1[:, t, :])
                then(last)
                for t in range(NT):
                    last = dve.match_replace(t2[:, t, :], top8[:, t, :], t1[:, t, :], -3.0e38)
                then(last)
                then(dve.tensor_tensor(t3, t1, t2, ALU.not_equal))
                then(dve.tensor_tensor(t3, t3, sc1, ALU.mult))
                then(dve.tensor_reduce(rsum1[:, 0, :], t3, AX.X, ALU.add))
                then(dve.tensor_scalar(rsum1[:, 0, :], rsum1[:, 0, :], 1e-20, None, ALU.add))
                then(dve.reciprocal(rsum1[:, 1, :], rsum1[:, 0, :]))
                then(dve.tensor_scalar(rsum1[:, 1, :], rsum1[:, 1, :], 2.5, None, ALU.mult))
                then(dve.tensor_tensor(t3, t3, wide(rsum1[:, 1, :].unsqueeze(2), NT, E1), ALU.mult))
                dve.wait_ge(sel1_done, 1)
                then(dve.tensor_copy(rwp[:, :, 0:E1], t3))
                then(dve.tensor_tensor(t3, t3, rwp[:, :, 0:E1], ALU.subtract))
                then(dve.tensor_copy(rwp[:, :, E1:2 * E1], t3))
                then(dve.tensor_tensor(t3, t3, rwp[:, :, E1:2 * E1], ALU.subtract))
                dve.tensor_copy(rwl[:, :, 0:E1], t3).then_inc(rw_done, 1)

            def shared_hidden(m):
                dve.wait_ge(sil_s, m + 1)
                if m >= 2:
                    dve.wait_ge(sd_ready, m // 2)
                dve.tensor_tensor(h1[0:I1, m % 2, :], psum[0:I1, 4 + m % 2, :], sil[0:I1, m % 2, :], ALU.mult).then_inc(hs_done, 1)
                if m % 2:
                    g = m // 2
                    dve.wait_ge(sd_ready, g + 1)
                    dve.tensor_copy(osh[:, 512 * g:512 * g + 512], bank(6 + g % 2)).then_inc(osh_done, 1)

            for m in range(2 * NG):
                shared_hidden(m)
            routing()

            def hidden1(n, k, first):
                dve.wait_ge(u1_ready, n + 1)
                dve.wait_ge(sil1_done, n + 1)
                dve.tensor_tensor(u1[:, k, :], bank(2 + k), sil[:, k, :], ALU.mult).then_inc(u1_done, 1)
                dve.wait_ge(u1_done, n + 1)
                if not first:
                    dve.wait_ge(d1_done, n - 1)
                dve.tensor_tensor(h1[:, k, :], bank(4 + k), u1[:, k, :], ALU.mult).then_inc(h1_done, 1)

            for hf in range(2):
                for s in range(4):
                    hidden1(2 * NC1 * hf + s, s % 2, hf == 0 and s < 2)
                with dve.Fori(1, NC1 // 2) as i:
                    for s in range(4):
                        hidden1(i * 4 + (2 * NC1 * hf + s), s % 2, False)
                dve.wait_ge(d1_done, 2 * NC1 * (hf + 1))
                for q in range(2):
                    r = slice(1024 * hf + 512 * q, 1024 * hf + 512 * q + 512)
                    dve.tensor_tensor(osh[:, r], osh[:, r], bank(6 + q), ALU.add).then_inc(o1_done, 1)
            for t in range(NT):
                dve.wait_ge(o1_tp, t + 1)
                dve.tensor_tensor(X[:, t, :], psum[:, t % 4, 0:D], X[:, t, :], ALU.add).then_inc(x_done, 1)

            def project(L, base, qb_, kb_, vrow, mm):
                dve.wait_ge(qk2_mm, mm + 1)
                if kb_ is None:
                    dve.tensor_copy(k2T, bank(0)).then_inc(qk2_sb, 1)
                else:
                    dve.tensor_scalar(k2T, bank(0), cols[:, kb_:kb_ + 1], None, ALU.add).then_inc(qk2_sb, 1)
                dve.wait_ge(v2_mm, mm // 5 + 1)
                dve.tensor_tensor(v2[0:C], psum[0:C, 6:8, :].rearrange("p a (b d) -> p (a b) d", d=D),
                                  rows[0:C, vrow, :].unsqueeze(1).broadcast_to([C, B, D]), ALU.add).then_inc(v2_sb, 1)
                layer_norm(L)
                for g in range(NG):
                    dve.wait_ge(qk2_mm, mm + g + 2)
                    dve.tensor_scalar(q2T[:, 512 * g:512 * g + 512], bank(2 + g), cols[:, qb_:qb_ + 1], float(D) ** -0.5, ALU.add, ALU.mult)\
                        .then_inc(qk2_sb, 1)

            def softmax(base):
                for hf in range(2):
                    r = slice(8 * hf, 8 * hf + 8)
                    sim = bank(hf).rearrange("p (t j) -> p t j", j=C)
                    dve.wait_ge(s2_mm, base + hf + 1)
                    then(dve.tensor_reduce(mx2[:, r], sim, AX.X, ALU.max))
                    dve.tensor_tensor(s2[:, r, :], sim, wide(mx2[:, r].unsqueeze(2), 8, C), ALU.subtract).then_inc(s2_sub, 1)
                for hf in range(2):
                    r = slice(8 * hf, 8 * hf + 8)
                    dve.wait_ge(e2_exp, base + hf + 1)
                    then(dve.tensor_reduce(den2[:, r], e2[:, r, :], AX.X, ALU.add))
                    then(dve.reciprocal(rden2[:, r], den2[:, r]))

            project(4, 0, COL["q2_b"], COL["k2_b"], ROW["v2_b"], 0)
            softmax(0)
            for t in range(NT):
                dve.wait_ge(av2_ready, t + 1)
                dve.scalar_tensor_tensor(X[:, t, :], psum[:, (6, 7, 0, 1)[t % 4], 0:D], rden2[:, t:t + 1], X[:, t, :], ALU.mult, ALU.add)\
                    .then_inc(x_done, 1)

            layer_norm(5)
            dve.wait_ge(rl_sig, 3)
            rank_of(rank2, pr2, g2a, g2b, NT)
            then(dve.tensor_scalar(rank2, rank2, 1.5, None, ALU.is_lt))
            then(dve.tensor_tensor(rank2, rank2, pr2, ALU.mult))
            then(dve.tensor_reduce(rs2[:, 0, :], rank2, AX.X, ALU.add))
            then(dve.tensor_scalar(rs2[:, 0, :], rs2[:, 0, :], 1e-20, None, ALU.add))
            then(dve.reciprocal(rs2[:, 1, :], rs2[:, 0, :]))
            then(dve.tensor_tensor(rank2, rank2, wide(rs2[:, 1, :].unsqueeze(2), NT, E2), ALU.mult))
            dve.wait_ge(sel2_done, 1)
            then(dve.tensor_copy(cpk[:, :, 0:E2], rank2))
            then(dve.tensor_tensor(rank2, rank2, cpk[:, :, 0:E2], ALU.subtract))
            then(dve.tensor_copy(cpk[:, :, E2:2 * E2], rank2))
            then(dve.tensor_tensor(rank2, rank2, cpk[:, :, E2:2 * E2], ALU.subtract))
            dve.tensor_copy(cpk[:, :, 2 * E2:3 * E2], rank2).then_inc(rw_done, 1)

            def hidden2(n, k, first):
                dve.wait_ge(r2_done, n + 1)
                dve.tensor_tensor(u2[:, k, :], bank(2 + k), r2[:, k, :], ALU.mult).then_inc(u2_done, 1)
                dve.wait_ge(u2_done, n + 1)
                if not first:
                    dve.wait_ge(d2_done, n - 1)
                dve.tensor_tensor(h2[:, k, :], u2[:, k, :], r2[:, k, :], ALU.mult).then_inc(h2_done, 1)

            for s in range(8):
                hidden2(s, s % 2, s < 2)
            with dve.Fori(1, NC2 // 2) as i:
                for s in range(8):
                    hidden2(i * 8 + s, s % 2, False)
            for t in range(NT):
                dve.wait_ge(o2_tp, t + 1)
                dve.tensor_tensor(X[:, t, :], psum[:, t % 4, 0:D], X[:, t, :], ALU.add).then_inc(x_done, 1)

            project(6, 2, COL["q3_b"], None, ROW["v3_b"], 5)
            softmax(2)
            dve.wait_ge(xbias_done, 2)
            for t in range(NT):
                dve.wait_ge(av2_ready, NT + t + 1)
                dve.scalar_tensor_tensor(X[:, t, :], psum[:, 4 + t % 4, 0:D], rden2[:, t:t + 1], X[:, t, :], ALU.mult, ALU.add)\
                    .then_inc(x_done, 1)

            dve.wait_ge(x_done, 7 * NT)
            dve.tensor_reduce(wsum[:, 0:1], w1f[:, :], AX.X, ALU.add, apply_absolute_value=True)
            dve.tensor_reduce(wsum[:, 1:2], w2f[:, :, :].rearrange("p c o -> p (c o)"), AX.X, ALU.add, apply_absolute_value=True)\
                .then_inc(wsum_done, 1)
            layer_norm(7)
            dve.wait_ge(wsum_mm, 1)
            then(dve.tensor_scalar(wm, psum[:, 7, 0:2], 1.0 / (D * HID3), 1e-5, ALU.mult, ALU.max))
            then(dve.reciprocal(wr, wm))
            for k, (w, q) in enumerate(((w1f[:, :], w1q), (w2f[:, :, :].rearrange("p c o -> p (c o)"), w2q.rearrange("p c o -> p (c o)")))):
                then(dve.tensor_scalar(wa, w, wr[:, k:k + 1], MAGIC, ALU.mult, ALU.add))
                then(dve.tensor_scalar(wa, wa, MAGIC + 1.0, MAGIC - 1.0, ALU.min, ALU.max))
                last = dve.tensor_scalar(q, wa, MAGIC, None, ALU.subtract)
                if k == 0:
                    then(last)
            last.then_inc(wq_done, 1)
            dve.wait_ge(ln_xn, NG * 8)
            then(dve.tensor_reduce(am3, xn[:, :, :], AX.X, ALU.max, apply_absolute_value=True))
            then(dve.tensor_scalar(am3, am3, 1e-5, None, ALU.max))
            dve.tensor_scalar(rs3, am3, 1.0 / 127.0, None, ALU.mult).then_inc(rs3_done, 1)
            then(dve.reciprocal(qs3, am3))
            then(dve.tensor_scalar(qs3, qs3, 127.0, None, ALU.mult))
            for t in range(NT):
                last = dve.tensor_scalar(qa[:, t, :], xn[:, t, :], qs3[:, t:t + 1], MAGIC, ALU.mult, ALU.add)
            then(last)
            then(dve.tensor_scalar(qa, qa, MAGIC + 127.0, MAGIC - 128.0, ALU.min, ALU.max))
            dve.tensor_scalar(xi, qa, MAGIC, None, ALU.subtract).then_inc(xi_done, 1)
            dve.wait_ge(hpad_zero, 1)
            dve.wait_ge(rsB_sb, NG)
            for c in range(NC3):
                w = CONV + 4 * c
                for g in range(NG):
                    dve.wait_ge(l1_ready, NG * c + g + 1)
                    last = dve.tensor_tensor(hpad[:, c % 2, 2 * g:2 * g + 2, 1:N + 1],
                                             bank((NG * c + g) % 8).rearrange("p (b n) -> p b n", b=2),
                                             rsB[:, 512 * g:512 * g + 512].rearrange("p (b n) -> p b n", b=2), ALU.mult)
                    last.then_inc(hpad_done, 1)
                dve.wait_ge(hpad_done, NG * (c + 1))
                if c >= 2:
                    dve.wait_ge(g3_done, c - 1)
                y = yc[:, c % 2, :].rearrange("p (b n) -> p b n", b=B)
                then(dve.tensor_scalar(y, hpad[:, c % 2, :, 1:N + 1], cols[:, w + 1:w + 2], cols[:, w + 3:w + 4], ALU.mult, ALU.add))
                then(dve.scalar_tensor_tensor(y, hpad[:, c % 2, :, 0:N], cols[:, w:w + 1], y, ALU.mult, ALU.add))
                dve.scalar_tensor_tensor(y, hpad[:, c % 2, :, 2:N + 2], cols[:, w + 2:w + 3], y, ALU.mult, ALU.add).then_inc(conv_done, 1)

            def quant_scale(t):
                dve.wait_ge(g3_tp, t + 1)
                then(dve.tensor_reduce(am4[:, t:t + 1], bank(t % 4), AX.X, ALU.max, apply_absolute_value=True))
                then(dve.tensor_scalar(am4[:, t:t + 1], am4[:, t:t + 1], 1e-5, None, ALU.max))
                then(dve.reciprocal(qs4[:, t:t + 1], am4[:, t:t + 1]))
                dve.tensor_scalar(rs4[:, t:t + 1], am4[:, t:t + 1], wm[:, 1:2], 1.0 / 127.0, ALU.mult, ALU.mult)
                dve.tensor_scalar(qs4[:, t:t + 1], qs4[:, t:t + 1], 127.0, None, ALU.mult).then_inc(qs4_done, 1)

            for t in range(NT + 2):
                if t < NT:
                    quant_scale(t)
                if 1 <= t <= NT:
                    k = (t - 1) % 2
                    dve.wait_ge(ga_done, t)
                    then(dve.tensor_scalar(ga[:, k, :], ga[:, k, :], MAGIC, MAGIC + 127.0, ALU.add, ALU.min))
                    if t >= 3:
                        dve.wait_ge(gi_tp, t - 2)
                    dve.tensor_scalar(gi[:, k, :], ga[:, k, :], MAGIC - 128.0, MAGIC, ALU.max, ALU.subtract).then_inc(gi_done, 1)
                if t >= 2:
                    dve.wait_ge(l2_ready, t - 1)
                    dve.scalar_tensor_tensor(X[:, t - 2, :], psum[:, 6 + t % 2, 0:D], rs4[:, t - 2:t - 1], X[:, t - 2, :], ALU.mult, ALU.add)\
                        .then_inc(x_done, 1)

        @block.tensor
        def _(pe):
            def mm(dst, lhsT, rhs, start=True, stop=True):
                return pe.matmul(dst, lhsT=lhsT, rhs=rhs, start=start, stop=stop)

            def ln_transposes(L):
                for g in range(NG):
                    pe.wait_ge(ln_xn, NG * L + g + 1)
                    if g >= 2:
                        pe.wait_ge(ln_xnT, NG * L + g - 1)
                    for j in range(4):
                        last = pe.transpose(psum[:, 6 + g % 2, P * j:P * j + P], xn[:, 4 * g + j, :], ident[:, :])
                    last.then_inc(ln_tp, 1)

            pe.wait_ge(w_l0, 16 * N_L0)
            mm(bank(0), wk0[:, :], ctxT[:, :])
            for b in range(B):
                last = mm(psum[:, 1, HD * b:HD * b + HD], ctxTd[:, P * b:P * b + P], wv0[:, :])
            last.then_inc(kv_mm, 1)
            pe.wait_ge(consts, 1)
            ln_transposes(0)
            for g in range(NG):
                pe.wait_ge(ln_xnT, g + 1)
                mm(bank(2 + g), wq0[:, :], xnT[:, 512 * g:512 * g + 512]).then_inc(q_mm, 1)
            pe.wait_ge(vaug_done, 1)
            for t in range(NT + 2):
                if t < NT:
                    b = t // TB
                    pe.wait_ge(q_sb, max(t // 4 + 1, 2))
                    pe.wait_ge(kbd_done[b % 2], b // 2 + 1)
                    if t >= 2:
                        pe.wait_ge(sim_used, t - 1)
                    for hf in range(2):
                        last = mm(bank(2 * (t % 2) + hf), qT[:, P * t:P * t + P],
                                  kbd[:, b, 8 * hf:8 * hf + 8, :].rearrange("p h k -> p (h k)"))
                    last.then_inc(sim_ready, 1)
                if t == 1:
                    pe.wait_ge(se_n, 2)
                    pe.wait_ge(ln_xnT, NG)
                    for g in range(2):
                        for j in range(4):
                            last = pe.transpose(psum[:, 6 + g, P * j:P * j + P], slot_n[:, 4 * g + j, :], ident[:, :])
                        last.then_inc(se_tp, 1)
                    pe.wait_ge(se_T, 2)
                if t >= 2:
                    pe.wait_ge(y_ready, t - 1)
                    pe.transpose(psum[:, 6, 256:384], y0[:, t % 2].rearrange("p h k -> p (h k)"), ident[:, :]).then_inc(yT_ready, 1)
                if 1 <= t <= NT:
                    b = (t - 1) // TB
                    pe.wait_ge(exp_done, t)
                    pe.wait_ge(et_sb, t - 1) if t >= 2 else pe.wait_ge(q_sb, 4)
                    for j in range(H0 // 2):
                        last = pe.transpose(psum[:, 4 + j // 4, P * (j % 4):P * (j % 4) + P], simE[:, (t - 1) % 2, P * j:P * j + P], ident[:, :])
                    last.then_inc(et_ready, 1)
                    pe.wait_ge(et_sb, t)
                    if t >= 2:
                        pe.wait_ge(yT_sb, t - 1)
                    for j in range(H0 // 2):
                        w = 2 * (HD + 1)
                        last = mm(psum[:, 6, w * j:w * j + w], simET[:, (t - 1) % 2, P * j:P * j + P],
                                  vaug[:, b].rearrange("p h k -> p (h k)"))
                    last.then_inc(av_ready, 1)
                if t >= 2:
                    pe.wait_ge(yT_sb, t - 1)
                    if t >= 3:
                        pe.wait_ge(x_done, t - 2)
                    mm(psum[:, 7, 0:D], y0T[:, t % 2, :], wo0[:, :]).then_inc(out_ready, 1)

            pe.wait_ge(x_done, NT)
            ln_transposes(1)

            def logits_slots(k):
                b, j = k // 4, k % 4
                pe.wait_ge(ln_xnT, NG + b // 2 + 1)
                if k >= 2:
                    pe.wait_ge(bexp_done, k - 1)
                for c in range(2):
                    ch = 2 * j + c
                    last = mm(psum[:, k % 2, N * c:N * c + N], seT[:, P * ch:P * ch + P], xnT[:, N * b:N * b + N])
                last.then_inc(bl_ready, 1)

            def logits_tokens(t):
                if t >= 1:
                    pe.wait_ge(aexp_done, t)
                for hf in range(2):
                    last = mm(bank(2 + hf), xnT[:, P * t:P * t + P], seT[:, 512 * hf:512 * hf + 512])
                last.then_inc(al_ready, 1)

            def dispatch_T(k):
                b, j = k // 4, k % 4
                pe.wait_ge(bnorm_done, k + 1)
                if j < 2:
                    if b:
                        pe.wait_ge(pt_sb, 2 * b)
                else:
                    pe.wait_ge(pt_sb, 2 * b + 1)
                for a in range(TB):
                    for c in range(2):
                        last = pe.transpose(psum[:, 4 + j % 2, N * a + P * c:N * a + P * c + P], qb[:, k % 2, c, P * a:P * a + P], ident[:, :])
                last.then_inc(bT_ready, 1)

            def combine_T(t):
                pe.wait_ge(aexp_done, t + 1)
                pe.wait_ge(qt_sb, 2 * t + 2)
                for c in range(NC0):
                    last = pe.transpose(psum[:, 4 + c // 4, P * (c % 4):P * (c % 4) + P], pbuf[:, t % 2, P * c:P * c + P], ident[:, :])
                last.then_inc(pT_ready, 1)

            for b in range(B):
                k = 4 * b
                logits_slots(k)
                logits_slots(k + 1)
                logits_tokens(2 * b)
                dispatch_T(k)
                logits_slots(k + 2)
                dispatch_T(k + 1)
                logits_slots(k + 3)
                combine_T(2 * b)
                dispatch_T(k + 2)
                logits_tokens(2 * b + 1)
                dispatch_T(k + 3)
                combine_T(2 * b + 1)
                pe.wait_ge(qt_sb, k + 4)
                for hf in range(2):
                    if b:
                        pe.wait_ge(slots_sb, 2 * (b - 1) + hf + 1)
                    else:
                        pe.wait_ge(ln_xnT, 2 * NG)
                    for a in range(TB):
                        last = mm(bank(6 + hf), xn[:, 2 * b + a, :], qt[:, b % 2, a, 512 * hf:512 * hf + 512], a == 0, a == TB - 1)
                    last.then_inc(slots_mm, 1)

            pe.wait_ge(slots_sb, 2 * B)
            pe.wait_ge(pt_sb, NT)

            def gate_up0(e, f, k, first):
                n = 2 * e + f
                moving = slotsT[:, bass.ds(e, 1), :, :].rearrange("p a b s -> p (a b s)")
                if f == 0:
                    if first:
                        pe.wait_ge(ew_in[k], 16)
                if not first or k:
                    pe.wait_ge(gelu_done, n - 1)
                mm(bank(f), ew[:, k, P * f:P * f + P], moving).then_inc(eg_ready, 1)
                if not first or k:
                    pe.wait_ge(h0_done, n - 1)
                mm(bank(2 + f), ew[:, k, F0 + P * f:F0 + P * f + P], moving).then_inc(eu_ready, 1)

            def down0(e, k, first):
                pe.wait_ge(h0_done, e * 2 + 2)
                if not first:
                    pe.wait_ge(eo_sb, e - 1)
                for f in range(2):
                    last = mm(bank(4 + k), ew[:, k, 2 * F0 + P * f:2 * F0 + P * f + P], h0[:, k, f, :], f == 0, f == 1)
                last.then_inc(ed_ready, 1)

            def expert_pair(i, first):
                for k in range(2):
                    if not first:
                        pe.wait_ge(ew_in[k], i * 16 + 16)
                    gate_up0(i * 2 + k, 0, k, first)
                    if not (first and k == 0):
                        down0(i * 2 + (k - 1), 1 - k, first)
                    gate_up0(i * 2 + k, 1, k, first)

            expert_pair(0, True)
            with pe.Fori(1, E0 // 2) as i:
                expert_pair(i, False)
            down0(E0 - 1, 1, False)
            pe.wait_ge(eo_sb, E0)
            for q in range(2 * B):
                if q >= 4:
                    pe.wait_ge(eo_tok[q % 2], (q - 4) // 2 + 1)
                for j in range(4):
                    c = 4 * (q % 2) + j
                    last = pe.transpose(psum[:, q % 4, P * j:P * j + P],
                                        eoT[:, q // 2, 2 * c:2 * c + 2, :].rearrange("p e s -> p (e s)"), ident[:, :])
                last.then_inc(eoT_tp, 1)
            for t in range(NT):
                b = t // TB
                for k in range(2):
                    pe.wait_ge(eo_tok[k], b + 1)
                if t >= 4:
                    pe.wait_ge(x_done, NT + t - 3)
                for c in range(NC0):
                    last = mm(psum[:, 4 + t % 4, 0:D], PT[:, c, P * t:P * t + P], eo[:, b, c, :], c == 0, c == NC0 - 1)
                last.then_inc(comb_ready, 1)

            pe.wait_ge(x_done, 2 * NT)
            pe.wait_ge(w_rest, 16 * (len(REST) + 2))
            mm(psum[0:1, 0, :], cols[:, COL["w_sim2"]:COL["w_sim2"] + 1], ctxT[:, :]).then_inc(dw2_mm, 1)
            ln_transposes(2)
            pe.wait_ge(dw2_sb, 1)
            pe.wait_ge(cw_done, 1)
            for t in range(NT):
                b = t // TB
                if t % 4 == 0:
                    pe.wait_ge(ln_xnT, 2 * NG + t // 4 + 1)
                dst = psum[:, t // 8, C * (t % 8):C * (t % 8) + C]
                mm(dst, xnT[:, P * t:P * t + P], cw[:, C * b:C * b + C], True, False)
                last = mm(dst, ones[0:1, :], dw2[0:1, C * b:C * b + C], False, True)
                if t % 8 == 7:
                    last.then_inc(s1_mm, 1)
            pe.wait_ge(s1_sub, 2)
            for a in range(TB):
                last = pe.transpose(psum[0:B, 7, P * a:P * a + P], mx1[:, a:NT:TB], ident[:, :])
            last.then_inc(bt_tp, 1)
            for t in range(NT):
                pe.wait_ge(e1_norm, t // 8 + 1)
                last = pe.transpose(psum[0:C, 2 + t // 4, P * (t % 4):P * (t % 4) + P], e1n[:, t, :], ident[:, :])
                if t % 4 == 3:
                    last.then_inc(aT_tp, 1)
            pe.wait_ge(bt_norm, 1)
            for a in range(TB):
                last = pe.transpose(psum[:, 7, 256 + B * a:256 + B * a + B], btn[0:B, P * a:P * a + P], ident[0:B, 0:B])
            last.then_inc(btT_tp, 1)
            pe.wait_ge(btT_sb, 1)
            for b in range(B):
                for a in range(TB):
                    last = mm(psum[:, 7, 288 + b:289 + b], xn[:, TB * b + a, :], btT[:, a, b:b + 1], a == 0, a == TB - 1)
            last.then_inc(hc_mm, 1)
            for b in range(B):
                g = b // 2
                pe.wait_ge(aT_sb, g + 1)
                last = mm(psum[:, (6, 0, 1, 2)[g], N * (b % 2):N * (b % 2) + N], ctx_tok[:, b, :], aT[0:C, N * b:N * b + N])
                if b % 2:
                    last.then_inc(hq_mm, 1)
            pe.wait_ge(xc_done, 1)
            pe.wait_ge(aT_sb, 4)
            for t in range(NT):
                pe.wait_ge(xh_done, t // 4 + 1)
                if t >= 3:
                    pe.wait_ge(x_done, 2 * NT + t - 2)
                for k, feat in enumerate((xnT, hqT, xhT, xcT)):
                    last = mm(psum[:, 3 + t % 3, 0:D], feat[:, P * t:P * t + P], wqv[:, k, :], k == 0, k == 3)
                last.then_inc(qv_ready, 1)

            pe.wait_ge(x_done, 3 * NT)
            ln_transposes(3)
            for t in range(NT):
                pe.wait_ge(ln_xnT, 3 * NG + t // 4 + 1)
                last = mm(psum[:, t // 8, E1 * (t % 8):E1 * (t % 8) + E1], xnT[:, P * t:P * t + P], gw1[:, :])
                if t % 8 == 7:
                    last.then_inc(rl_mm, 1)
            def shared_gate_up(m):
                g, c = m // 2, m % 2
                if m >= 2:
                    pe.wait_ge(hs_done, m - 1)
                mm(psum[0:I1, 2 + c, :], sgT[:, I1 * c:I1 * c + I1], xnT[:, 512 * g:512 * g + 512])
                mm(psum[0:I1, 4 + c, :], suT[:, I1 * c:I1 * c + I1], xnT[:, 512 * g:512 * g + 512]).then_inc(sg_ready, 1)

            for g in range(NG):
                shared_gate_up(2 * g)
                shared_gate_up(2 * g + 1)
                pe.wait_ge(hs_done, 2 * g + 2)
                if g >= 2:
                    pe.wait_ge(osh_done, g - 1)
                for c in range(SH1):
                    last = mm(bank(6 + g % 2), sdT[:, c, :], h1[0:I1, c, :], c == 0, c == SH1 - 1)
                last.then_inc(sd_ready, 1)
            pe.wait_ge(rw_done, 1)
            for q in range(4):
                src = (rwp, rwl)[q // 2]
                half = psum[:, q, :].bitcast(BF16)
                for j in range(8):
                    last = pe.transpose(half[:, P * j:P * j + P], src[:, 8 * (q % 2) + j, :], identb[:, :])
                last.then_inc(rw_tp, 1)
            pe.wait_ge(rw_sb, 4)
            pe.wait_ge(osh_done, NG)

            def gate_up1(n, c, k, slot, hf, first):
                tok = slice(1024 * hf + 512 * k, 1024 * hf + 512 * k + 512)
                if not first:
                    pe.wait_ge(sil1_done, n - 1)
                mm(bank(k), w1ring[:, slot, 0:P], xnT[:, tok]).then_inc(g1_ready, 1)
                if not first:
                    pe.wait_ge(h1_done, n - 1)
                mm(bank(2 + k), w1ring[:, slot, P:2 * P], xnT[:, tok])
                pick = sel1[:, bass.ds(c * P, P)]
                mm(bank(4 + k), pick, rwT1[:, tok], True, False)
                mm(bank(4 + k), pick, rwT2[:, tok], False, True).then_inc(u1_ready, 1)

            def down1(n, k, slot, start, stop):
                pe.wait_ge(h1_done, n + 1)
                mm(bank(6 + k), w1ring[:, slot, 2 * P:3 * P], h1[:, k, :], start, stop).then_inc(d1_done, 1)

            def chunk_pair(i, hf, first, last):
                base = 2 * NC1 * hf
                for s in range(4):
                    slot, k = s // 2, s % 2
                    if k == 0:
                        pe.wait_ge(w1_in[slot], i * 16 + (16 + 16 * (NC1 // 2) * hf))
                    gate_up1(i * 4 + (base + s), i * 2 + slot, k, slot, hf, first and hf == 0 and s < 2)
                    if not (first and s == 0):
                        down1(i * 4 + (base + s - 1), 1 - k, (slot + (k == 0)) % 2, first and s in (1, 2), last and s == 3)

            for hf in range(2):
                if hf:
                    pe.wait_ge(o1_done, 2)
                chunk_pair(0, hf, True, False)
                with pe.Fori(1, NC1 // 2 - 1) as i:
                    chunk_pair(i, hf, False, False)
                chunk_pair(NC1 // 2 - 1, hf, False, True)
                down1(2 * NC1 * (hf + 1) - 1, 1, 1, False, True)
            pe.wait_ge(o1_done, 4)
            for t in range(NT):
                if t >= 4:
                    pe.wait_ge(x_done, 3 * NT + t - 3)
                pe.transpose(psum[:, t % 4, 0:D], osh[:, P * t:P * t + P], ident[:, :]).then_inc(o1_tp, 1)

            def project(L, wq_, wk_, wv_):
                mm(bank(0), wk_[:, :], ctxT[:, :]).then_inc(qk2_mm, 1)
                for b in range(B):
                    last = mm(psum[0:C, 6 + b // 4, D * (b % 4):D * (b % 4) + D], ctxT[:, C * b:C * b + C], wv_[:, :])
                last.then_inc(v2_mm, 1)
                ln_transposes(L)
                for g in range(NG):
                    pe.wait_ge(ln_xnT, NG * L + g + 1)
                    mm(bank(2 + g), wq_[:, :], xnT[:, 512 * g:512 * g + 512]).then_inc(qk2_mm, 1)

            def scores(base):
                pe.wait_ge(v2_sb, base // 2 + 1)
                for t in range(NT):
                    b = t // TB
                    pe.wait_ge(qk2_sb, 5 * base // 2 + t // 4 + 2)
                    last = mm(psum[:, t // 8, C * (t % 8):C * (t % 8) + C], q2T[:, P * t:P * t + P], k2T[:, C * b:C * b + C])
                    if t % 8 == 7:
                        last.then_inc(s2_mm, 1)
                pe.wait_ge(qk2_sb, 5 * base // 2 + 5)
                for t in range(NT):
                    pe.wait_ge(e2_exp, base + t // 8 + 1)
                    last = pe.transpose(psum[0:C, 2 + t // 4, P * (t % 4):P * (t % 4) + P], e2[:, t, :], ident[:, :])
                    if t % 4 == 3:
                        last.then_inc(e2_tp, 1)

            pe.wait_ge(x_done, 4 * NT)
            project(4, wq2, wk2, wv2)
            scores(0)
            for t in range(NT):
                b = t // TB
                pe.wait_ge(e2_sb, t // 4 + 1)
                if t >= 4:
                    pe.wait_ge(x_done, 4 * NT + t - 3)
                mm(psum[:, (6, 7, 0, 1)[t % 4], 0:D], e2T[0:C, P * t:P * t + P], v2[0:C, b, :]).then_inc(av2_ready, 1)

            pe.wait_ge(x_done, 5 * NT)
            ln_transposes(5)
            for t in range(NT):
                pe.wait_ge(ln_xnT, 5 * NG + t // 4 + 1)
                last = mm(psum[:, 0, E2 * t:E2 * t + E2], xnT[:, P * t:P * t + P], rw2[:, :])
            last.then_inc(rl_mm, 1)
            pe.wait_ge(rw_done, 2)
            for q in range(2):
                half = psum[:, 1 + q, :].bitcast(BF16)
                for j in range(8):
                    last = pe.transpose(half[:, P * j:P * j + P], cpk[:, 8 * q + j, :], identb[:, :])
                last.then_inc(rw_tp, 1)
            pe.wait_ge(rw_sb, 6)

            def up2(n, c, k, q, slot, first):
                tok = slice(512 * q, 512 * q + 512)
                if not first:
                    pe.wait_ge(h2_done, n - 1)
                mm(bank(k), w2ring[:, slot, 0:P], xnT[:, tok])
                mm(bank(2 + k), sel2[:, bass.ds(c, 1), :].rearrange("p a n -> p (a n)"), cT[:, tok]).then_inc(h2_ready, 1)

            def down2(n, k, q, slot, start, stop):
                pe.wait_ge(h2_done, n + 1)
                mm(bank(4 + q), w2ring[:, slot, P:2 * P], h2[:, k, :], start, stop).then_inc(d2_done, 1)

            def chunk_pair2(i, first, last):
                for s in range(8):
                    slot, q, k = s // 4, s % 4, s % 2
                    if q == 0:
                        pe.wait_ge(w2_in[slot], i * 16 + 16)
                    up2(i * 8 + s, i * 2 + slot, k, q, slot, first and s < 2)
                    if not (first and s == 0):
                        down2(i * 8 + (s - 1), 1 - k, (q - 1) % 4, (slot + (q == 0)) % 2, first and 1 <= s <= 4, last and s >= 5)

            chunk_pair2(0, True, False)
            with pe.Fori(1, NC2 // 2 - 1) as i:
                chunk_pair2(i, False, False)
            chunk_pair2(NC2 // 2 - 1, False, True)
            down2(4 * NC2 - 1, 1, 3, 1, False, True)
            for t in range(NT):
                pe.wait_ge(o2_sb, t // 4 + 1)
                if t >= 4:
                    pe.wait_ge(x_done, 5 * NT + t - 3)
                pe.transpose(psum[:, t % 4, 0:D], o2T[:, P * t:P * t + P], ident[:, :]).then_inc(o2_tp, 1)

            pe.wait_ge(x_done, 6 * NT)
            project(6, wq3, wk3, wv3)
            scores(2)
            for b in range(B):
                g = b // 2
                pe.wait_ge(e2_sb, NG + max(g, 2) + 1 if g >= 2 else NG + g + 1)
                if g >= 2:
                    pe.wait_ge(e2_sb, 2 * NG)
                last = mm(psum[:, (0, 1, 2, 3)[g], N * (b % 2):N * (b % 2) + N], v2[0:C, b, :], e2T[0:C, N * b:N * b + N])
                if b % 2:
                    last.then_inc(c3_mm, 1)
            for t in range(NT):
                pe.wait_ge(c3_sb, t // 4 + 1)
                if t >= 4:
                    pe.wait_ge(x_done, 6 * NT + t - 3)
                mm(psum[:, 4 + t % 4, 0:D], c3T[:, P * t:P * t + P], wo3[:, :]).then_inc(av2_ready, 1)

            pe.wait_ge(x_done, 7 * NT)
            pe.wait_ge(wsum_done, 1)
            mm(psum[:, 7, 0:2], ones[:, :], wsum).then_inc(wsum_mm, 1)
            pe.wait_ge(rs3_done, 1)
            for t in range(NT):
                last = mm(psum[:, 2 + t // 4, P * (t % 4):P * (t % 4) + P], wide(rs3[:, t:t + 1], P), ident[:, :])
                if t % 4 == 3:
                    last.then_inc(rsB_mm, 1)
            pe.wait_ge(xi_done, 1)
            for g in range(2):
                half = psum[:, g, :].bitcast(BF16)
                for j in range(8):
                    last = pe.transpose(half[:, P * j:P * j + P], xi[:, 8 * g + j, :], identb[:, :])
                last.then_inc(xi_tp, 1)
            pe.wait_ge(wq_done, 1)
            pe.wait_ge(rsB_sb, NG)
            for n in range(NC3 * NG):
                c, g = n // NG, n % NG
                pe.wait_ge(xi_sb, g // 2 + 1 if n >= 2 else 2)
                if n >= 8:
                    pe.wait_ge(hpad_done, n - 7)
                mm(bank(n % 8), w1q[:, P * c:P * c + P], xiT[:, 512 * g:512 * g + 512]).then_inc(l1_ready, 1)
            pe.wait_ge(hpad_done, NC3 * NG)
            pe.wait_ge(g3_done, NC3)

            def hidden_T(t):
                if t >= 4:
                    pe.wait_ge(ga_done, t - 3)
                for c in range(NC3):
                    last = pe.transpose(psum[:, t % 4, P * c:P * c + P], g3[:, c, P * t:P * t + P], ident[:, :])
                last.then_inc(g3_tp, 1)

            hidden_T(0)
            hidden_T(1)
            for t in range(NT + 1):
                if t + 2 < NT:
                    hidden_T(t + 2)
                if t < NT:
                    pe.wait_ge(gi_done, t + 1)
                    if t >= 2:
                        pe.wait_ge(gi_sb, t - 1)
                    half = psum[:, 4 + t % 2, 0:NC3 * P // 2].bitcast(BF16)
                    for c in range(NC3):
                        last = pe.transpose(half[:, P * c:P * c + P], gi[:, t % 2, P * c:P * c + P], identb[:, :])
                    last.then_inc(gi_tp, 1)
                if t >= 1:
                    pe.wait_ge(gi_sb, t)
                    if t >= 3:
                        pe.wait_ge(x_done, 7 * NT + t - 2)
                    for c in range(NC3):
                        last = mm(psum[:, 6 + (t - 1) % 2, 0:D], giT[:, (t - 1) % 2, c, :], w2q[:, c, :], c == 0, c == NC3 - 1)
                    last.then_inc(l2_ready, 1)


def kernel(**inputs):
    import numpy as np
    import concourse.bacc as _bacc
    from concourse import mybir as _mybir
    from concourse.bass_utils import run_bass_kernel_spmd as _run

    v = {k: np.asarray(a) for k, a in inputs.items()}

    def columns(a, n):
        return a.reshape(a.shape[0], n, P).transpose(2, 0, 1)

    ctx = v["ctx_1024"].reshape(B * C, D)
    ctxT = ctx.T
    conv = np.concatenate([v["L3_ffn_conv_w"].reshape(HID3, 3), v["L3_ffn_conv_b"].reshape(HID3, 1)], axis=1)
    w_sim = v["L1_xattn_w_sim"].reshape(3, D)
    cols = np.concatenate([
        np.stack([v["L0_ffn_norm_g"], v["L0_ffn_norm_b"], v["L0_ffn_slot_g"], v["L0_ffn_slot_b"], w_sim[0], w_sim[1], w_sim[2],
                  v["L2_xattn_Wq_b"], v["L2_xattn_Wk_b"], v["L3_xattn_bq"]], axis=1),
        conv.reshape(NC3, P, 4).transpose(1, 0, 2).reshape(P, 4 * NC3)], axis=1)
    ew = np.concatenate([
        v["L0_ffn_Wg"], v["L0_ffn_Wu"],
        v["L0_ffn_Wd"].reshape(E0, 2, P, D).transpose(0, 2, 1, 3).reshape(E0, P, 2 * D),
        v["L0_ffn_bg"].reshape(E0, 2, P).transpose(0, 2, 1), v["L0_ffn_bu"].reshape(E0, 2, P).transpose(0, 2, 1),
        v["L0_ffn_bd"].reshape(E0, P, 1)], axis=2)
    w1 = np.concatenate([
        v["L1_ffn_Wg"].reshape(NC1, P, D).transpose(0, 2, 1), v["L1_ffn_Wu"].reshape(NC1, P, D).transpose(0, 2, 1),
        v["L1_ffn_Wd"].transpose(0, 2, 1).reshape(NC1, P, D)], axis=2)
    w2 = np.concatenate([v["L2_ffn_w1"].reshape(D, NC2, P).transpose(1, 0, 2), v["L2_ffn_w2"].reshape(NC2, P, D)], axis=2)
    laid = {
        "x": v["x"].reshape(T, D),
        "ctx": ctx,
        "ctxT": ctxT,
        "ctxTd": np.repeat(ctxT.reshape(D, B, 1, C), 2, axis=2).reshape(D, B * 2 * C),
        "cols": cols,
        "rows": np.stack([v["L1_xattn_b_qv"], v["L2_xattn_Wv_b"], v["L3_xattn_bv"], v["L3_xattn_bo"]]),
        "scal": np.concatenate([v["L0_ffn_scale"], v["L1_xattn_b_sim"]]),
        "gbias": v["L1_ffn_gate_bias"],
        "wq0": v["L0_xattn_Wq"],
        "wk0": np.tile(v["L0_xattn_Wkv"][:, 0:HD], (1, H0)),
        "wv0": v["L0_xattn_Wkv"][:, HD:2 * HD],
        "wo0": v["L0_xattn_Wo"],
        "slots": v["L0_ffn_slot_embeds"].reshape(ES, D),
        "ew": ew,
        "w1": w1,
        "w2": w2,
        "wqv": v["L1_xattn_W_qv"].reshape(4, P, D).transpose(1, 0, 2),
        "gw1": v["L1_ffn_gate_w"].T,
        "sgT": v["L1_ffn_Sg"].T,
        "suT": v["L1_ffn_Su"].T,
        "sdT": v["L1_ffn_Sd"].T.reshape(SH1, I1, D).transpose(1, 0, 2),
        "wq2": v["L2_xattn_Wq_w"].T,
        "wk2": v["L2_xattn_Wk_w"].T,
        "wv2": v["L2_xattn_Wv_w"].T,
        "rw2": v["L2_ffn_router_w"].T,
        "wq3": v["L3_xattn_Wq"].T,
        "wk3": v["L3_xattn_Wk"].T,
        "wv3": v["L3_xattn_Wv"].T,
        "wo3": v["L3_xattn_Wo"].T,
        "w1f": v["L3_ffn_w1"].T,
        "w2f": v["L3_ffn_w2"].T.reshape(NC3, P, D).transpose(1, 0, 2),
    }
    nc = _bacc.Bacc("TRN2", target_bir_lowering=False, num_devices=1)
    arrays, args = {}, {}
    for name, a in laid.items():
        a = np.ascontiguousarray(a)
        arrays[f"in_{name}"] = a
        args[name] = nc.dram_tensor(f"in_{name}", a.shape, _mybir.dt.from_np(a.dtype), kind="ExternalInput").ap()
    out = nc.dram_tensor("out", (T, D), F32, kind="ExternalOutput").ap()
    build_program(nc, args, out)
    r = _run(nc, [arrays], core_ids=[0])
    return r.results[0]["out"].reshape(B, N, D)
```

```python
from contextlib import ExitStack

import concourse.bass as bass
from concourse import mybir

ALU = mybir.AluOpType
ACT = mybir.ActivationFunctionType
AX = mybir.AxisListType
F32 = mybir.dt.float32
BF16 = mybir.dt.bfloat16
F32R = mybir.dt.float32r

P = 128
B, N, D = 8, 256, 128
C = 64
T = B * N
NT = T // P
TB = N // P
NG = NT // 4
H0, HD = 16, D // 16
E0, S0, F0 = 16, 64, 256
ES = E0 * S0
NC0 = ES // P
E1, I1 = 64, 88
NC1 = E1 * I1 // P
G1 = 8
SH1 = 2
E2 = 8
W2 = 4 * 128 + 4 * 256
NC2 = W2 // P
HID3 = 512
NC3 = HID3 // P
EPS = 1e-5
MAGIC = 1.5 * 2.0 ** 23
LAYERS = 8

COLS = ["norm_g", "norm_b", "slot_g", "slot_b", "w_sim1", "w_sim2", "w_sim3", "q2_b", "k2_b", "q3_b"]
COL = {name: k for k, name in enumerate(COLS)}
CONV = len(COLS)
NCOL = CONV + 4 * NC3
ROWS = ["qv1_b", "v2_b", "v3_b", "o3_b"]
ROW = {name: k for k, name in enumerate(ROWS)}
EGU = 2 * F0 + 4
EDN = F0 + 1


def build_program(nc, A, out):
    with ExitStack() as ctx:
        def sb(name, shape, dt=F32):
            return ctx.enter_context(nc.sbuf_tensor(name, shape, dt))

        def sem(name):
            return ctx.enter_context(nc.semaphore(name))

        psum = ctx.enter_context(nc.psum_tensor("psum", [P, 8, 512], F32))

        X = sb("X", [P, NT, D])
        xn = sb("xn", [P, NT, D])
        xnT = sb("xnT", [P, T])
        ctxT = sb("ctxT", [P, B * C])
        ident = sb("ident", [P, P])
        identb = sb("identb", [P, P], BF16)
        ones = sb("ones", [P, P])
        cols = sb("cols", [P, NCOL])
        rows = sb("rows", [P, len(ROWS), D])
        scal = sb("scal", [P, 2])
        stats = sb("stats", [P, NT, 6])
        mv = sb("mv", [P, NT, 2])
        veps = sb("veps", [P, NT])
        rstd = sb("rstd", [P, NT])
        rtmp = sb("rtmp", [P, NT])
        neghalf = sb("neghalf", [P, NT])
        epst = sb("epst", [P, NT])
        wq0 = sb("wq0", [P, D])
        wk0 = sb("wk0", [P, D])
        wv0 = sb("wv0", [P, HD])
        wo0 = sb("wo0", [P, D])
        headmask = sb("headmask", [P, H0])
        seT = sb("seT", [P, ES])
        slot_gs = sb("slot_gs", [P, 2])
        egu = sb("egu", [P, 2, EGU])
        edn = sb("edn", [P, 2, EDN])
        wqv = sb("wqv", [P, 4, D])
        gw1 = sb("gw1", [P, E1])
        gbias = sb("gbias", [P, E1])
        sgT = sb("sgT", [P, SH1 * I1])
        suT = sb("suT", [P, SH1 * I1])
        sdT = sb("sdT", [I1, SH1, D])
        w1ring = sb("w1ring", [P, 2, 3 * P])
        w2ring = sb("w2ring", [P, 2, 2 * P])
        wq2 = sb("wq2", [P, D])
        wk2 = sb("wk2", [P, D])
        wv2 = sb("wv2", [P, D])
        rw2 = sb("rw2", [P, E2])
        wq3 = sb("wq3", [P, D])
        wk3 = sb("wk3", [P, D])
        wv3 = sb("wv3", [P, D])
        wo3 = sb("wo3", [P, D])
        w1f = sb("w1f", [P, HID3])
        w2f = sb("w2f", [P, NC3, D])
        ltmask = sb("ltmask", [P, 8, 8])
        xh = sb("xh", [P, 2, T // 2], F32R)
        wgu = sb("wgu", [P, 2, 2, 2 * P], F32R)
        wdn = sb("wdn", [P, 2, 2, P], F32R)
        hh = sb("hh", [P, 2, 2, 512], F32R)
        selr = sb("selr", [P, 2, P], F32R)
        rwr = sb("rwr", [P, T], F32R)

        ARENA = 29900
        arena = sb("arena", [P, ARENA])
        taken = [0]

        def carve(*shape, dt=F32):
            n = 1
            for k in shape:
                n *= k
            words = n if dt == F32 else (n + 1) // 2
            v = arena[:, taken[0]:taken[0] + words]
            taken[0] += words
            assert taken[0] <= ARENA, taken[0]
            if dt != F32:
                v = v.bitcast(dt)
            if len(shape) == 2:
                v = v.rearrange("p (a b) -> p a b", a=shape[0])
            elif len(shape) == 3:
                v = v.rearrange("p (a b c) -> p a b c", a=shape[0], b=shape[1])
            elif len(shape) == 4:
                v = v.rearrange("p (a b c d) -> p a b c d", a=shape[0], b=shape[1], c=shape[2])
            return v

        def bank(k):
            return psum[:, k, :]

        kbd = carve(B, H0, C)
        qT = carve(T)
        simS = carve(2, H0, C)
        simE = carve(2, H0 * C)
        simET = carve(2, H0 * C)
        krep = carve(B * C)
        vaug = carve(B, 2, HD + 1)
        y0 = carve(2, H0, HD)
        y0T = carve(2, P)
        mx0 = carve(2, H0)
        rden0 = carve(2, H0)
        ctxTd = carve(B * 2 * C)
        slot_raw = carve(ES // P, D)
        slot_n = carve(ES // P, D)
        smv = carve(ES // P, 2)
        sstats = carve(ES // P, 6)
        srstd = carve(3, ES // P)
        taken[0] = 0
        PT = carve(NC0, T)
        slotsT = carve(E0, B, S0)
        eo = slotsT.rearrange("p e b s -> p (e b s)").rearrange("p (c b o) -> p c b o", b=B, c=NC0)
        nmA = carve(NT)
        rsumA = carve(NT)
        rinvA = carve(NT)
        at_experts = taken[0]
        qb = carve(2, 2, N)
        qt = carve(TB, ES)
        pbuf = carve(2, ES)
        nmB = carve(2, 2)
        sumB = carve(2, 2)
        recB = carve(2, 2)
        taken[0] = at_experts
        eoT = carve(B, 2, S0)
        gel = carve(2, 512)
        h0 = carve(2, 2, 512)
        taken[0] = 0
        cw = carve(B * C)
        dw2 = carve(B * C)
        mx1 = carve(NT)
        s1 = carve(NT, C)
        e1 = carve(NT, C)
        e1n = carve(NT, C)
        den1 = carve(NT)
        rden1 = carve(NT)
        aT = carve(T)
        hqT = carve(T)
        xhT = carve(T)
        xcT = carve(T)
        bt = carve(N)
        btn = carve(N)
        bsm = carve(4)
        btT = carve(TB, B)
        hcT = carve(B)
        ctx_tok = carve(B, D)
        sel1 = carve(NC1 * P, dt=BF16)
        sc1 = carve(NT, E1)
        sfc = carve(NT, E1)
        t1 = carve(NT, E1)
        t2 = carve(NT, E1)
        t3 = carve(NT, E1)
        gs = carve(NT, G1)
        rank = carve(NT, G1)
        top8 = carve(NT, 8)
        rsum1 = carve(2, NT)
        rwp = carve(NT, 2, E1)
        osh = carve(T)
        sil = carve(2, 512)
        u1 = carve(2, 512)
        h1 = carve(2, 512)
        taken[0] = 0
        q2T = carve(T)
        k2T = carve(B * C)
        v2 = carve(B, D)
        s2 = carve(NT, C)
        e2 = carve(NT, C)
        mx2 = carve(NT)
        den2 = carve(NT)
        rden2 = carve(NT)
        e2T = carve(T)
        c3T = carve(T)
        xtmp = carve(2, D)
        taken[0] = 0
        sel2 = carve(NC2, P, dt=BF16)
        pr2 = carve(NT, E2)
        g2a = carve(NT, 8, 8)
        g2b = carve(NT, 8, 8)
        rank2 = carve(NT, 8)
        rs2 = carve(2, NT)
        cpk = carve(NT, P, dt=BF16)
        cT = carve(T, dt=BF16)
        r2 = carve(2, 512)
        u2 = carve(2, 512)
        h2 = carve(2, 512)
        o2T = carve(T)
        taken[0] = 0
        am3 = carve(NT)
        qs3 = carve(NT)
        rs3 = carve(NT)
        qa = carve(NT, D)
        xi = carve(NT, D, dt=BF16)
        xiT = carve(T, dt=BF16)
        rsB = carve(T)
        wa = carve(HID3)
        w1q = carve(HID3, dt=BF16)
        w2q = carve(NC3, D, dt=BF16)
        wsum = carve(2)
        wm = carve(2)
        wr = carve(2)
        hpad = carve(2, B, N + 2)
        yc = carve(2, T)
        g3 = carve(NC3, T)
        am4 = carve(NT)
        qs4 = carve(NT)
        rs4 = carve(NT)
        ga = carve(2, HID3)
        gi = carve(2, HID3, dt=BF16)
        giT = carve(2, NC3, P, dt=BF16)

        x_in = [sem(f"x_in{g}") for g in range(NG)]
        w_l0 = sem("w_l0")
        w_slots = sem("w_slots")
        w_rest = sem("w_rest")
        ctx_in = sem("ctx_in")
        egu_in = [sem(f"egu_in{k}") for k in range(2)]
        edn_in = [sem(f"edn_in{k}") for k in range(2)]
        w1_in = [sem(f"w1_in{k}") for k in range(2)]
        w2_in = [sem(f"w2_in{k}") for k in range(2)]
        out_done = sem("out_done")
        consts = sem("consts")
        pool_step = sem("pool_step")
        dve_step = sem("dve_step")
        act_step = sem("act_step")
        xh_hi = sem("xh_hi")
        xh_lo = sem("xh_lo")
        wgu_hi = sem("wgu_hi")
        wgu_lo = sem("wgu_lo")
        wdn_hi = sem("wdn_hi")
        wdn_lo = sem("wdn_lo")
        hh_hi = sem("hh_hi")
        hh_lo = sem("hh_lo")
        rwr_hi = sem("rwr_hi")
        rwr_lo = sem("rwr_lo")
        x_done = sem("x_done")
        ln_var = sem("ln_var")
        ln_rstd = sem("ln_rstd")
        ln_xn = sem("ln_xn")
        ln_tp = sem("ln_tp")
        ln_xnT = sem("ln_xnT")
        se_var = sem("se_var")
        se_rstd = sem("se_rstd")
        se_n = sem("se_n")
        se_tp = sem("se_tp")
        se_T = sem("se_T")
        kv_mm = sem("kv_mm")
        krep_done = sem("krep_done")
        vaug_done = sem("vaug_done")
        kbd_done = [sem("kbd_even"), sem("kbd_odd")]
        q_mm = sem("q_mm")
        q_sb = sem("q_sb")
        sim_ready = sem("sim_ready")
        sim_used = sem("sim_used")
        exp_done = sem("exp_done")
        et_ready = sem("et_ready")
        et_sb = sem("et_sb")
        av_ready = sem("av_ready")
        y_ready = sem("y_ready")
        yT_ready = sem("yT_ready")
        yT_sb = sem("yT_sb")
        out_ready = sem("out_ready")
        bl_ready = sem("bl_ready")
        bmax_done = sem("bmax_done")
        bexp_done = sem("bexp_done")
        brec_done = sem("brec_done")
        bnorm_done = sem("bnorm_done")
        bT_ready = sem("bT_ready")
        qt_sb = sem("qt_sb")
        al_ready = sem("al_ready")
        amax_done = sem("amax_done")
        aexp_done = sem("aexp_done")
        pT_ready = sem("pT_ready")
        pt_sb = sem("pt_sb")
        slots_mm = sem("slots_mm")
        slots_sb = sem("slots_sb")
        eg_ready = sem("eg_ready")
        eu_ready = sem("eu_ready")
        gelu_done = sem("gelu_done")
        h0_done = sem("h0_done")
        ed_ready = sem("ed_ready")
        eo_sb = sem("eo_sb")
        eoT_tp = [sem("eoT_tp_low"), sem("eoT_tp_high")]
        eo_tok = [sem("eo_tok_act"), sem("eo_tok_dve")]
        comb_ready = sem("comb_ready")
        cw_done = sem("cw_done")
        dw2_mm = sem("dw2_mm")
        dw2_sb = sem("dw2_sb")
        sim_mm = sem("sim_mm")
        sim_sub = sem("sim_sub")
        sim_exp = sem("sim_exp")
        e1_norm = sem("e1_norm")
        aT_tp = sem("aT_tp")
        aT_sb = sem("aT_sb")
        hq_mm = sem("hq_mm")
        hq_sb = sem("hq_sb")
        xh_done = sem("xh_done")
        bt_tp = sem("bt_tp")
        bt_max = sem("bt_max")
        bt_exp = sem("bt_exp")
        bt_norm = sem("bt_norm")
        btT_tp = sem("btT_tp")
        btT_sb = sem("btT_sb")
        hc_mm = sem("hc_mm")
        hc_sb = sem("hc_sb")
        xc_done = sem("xc_done")
        xbias_done = sem("xbias_done")
        qv_ready = sem("qv_ready")
        rl_mm = sem("rl_mm")
        rl_sig = sem("rl_sig")
        rw_done = sem("rw_done")
        rw_tp = sem("rw_tp")
        rw_sb = sem("rw_sb")
        sg_ready = sem("sg_ready")
        sil_s = sem("sil_s")
        hs_done = sem("hs_done")
        sd_ready = sem("sd_ready")
        osh_done = sem("osh_done")
        pool_made = sem("pool_made")
        gate_ready = sem("gate_ready")
        up_ready = sem("up_ready")
        nl_done = sem("nl_done")
        prod_done = sem("prod_done")
        hid_done = sem("hid_done")
        down_done = sem("down_done")
        o1_done = sem("o1_done")
        ffn_tp = sem("ffn_tp")
        qk2_mm = sem("qk2_mm")
        qk2_sb = sem("qk2_sb")
        v2_mm = sem("v2_mm")
        v2_sb = sem("v2_sb")
        rden2_done = sem("rden2_done")
        e2_tp = sem("e2_tp")
        e2_sb = sem("e2_sb")
        av2_ready = sem("av2_ready")
        c3_mm = sem("c3_mm")
        c3_sb = sem("c3_sb")
        o2_sb = sem("o2_sb")
        wsum_done = sem("wsum_done")
        wsum_mm = sem("wsum_mm")
        wq_done = sem("wq_done")
        rs3_done = sem("rs3_done")
        xi_done = sem("xi_done")
        xi_tp = sem("xi_tp")
        xi_sb = sem("xi_sb")
        rsB_mm = sem("rsB_mm")
        rsB_sb = sem("rsB_sb")
        l1_ready = sem("l1_ready")
        hpad_done = sem("hpad_done")
        conv_done = sem("conv_done")
        g3_done = sem("g3_done")
        g3_tp = sem("g3_tp")
        qs4_done = sem("qs4_done")
        ga_done = sem("ga_done")
        gi_done = sem("gi_done")
        gi_tp = sem("gi_tp")
        gi_sb = sem("gi_sb")
        l2_ready = sem("l2_ready")

        block = ctx.enter_context(nc.Block())

        def wide(ap, *shape):
            return ap.broadcast_to([P, *shape])

        def later(step, k):
            return not isinstance(step, int) or step >= k

        N_L0 = 9
        REST = ["wqv", "gw1", "sgT", "suT", "sdT", "wq2", "wk2", "wv2", "rw2", "wq3", "wk3", "wv3", "wo3", "w1f", "w2f"]

        @block.sync
        def _(sp):
            xt = A["x"].rearrange("(t p) d -> p t d", p=P)
            for g in range(NG):
                sp.dma_start(X[:, 4 * g:4 * g + 4, :], xt[:, 4 * g:4 * g + 4, :]).then_inc(x_in[g], 16)
            for dst, src in ((ctxT[:, :], A["ctxT"]), (ctxTd, A["ctxTd"]), (wk0[:, :], A["wk0"]), (wv0[:, :], A["wv0"]),
                             (wq0[:, :], A["wq0"]), (cols[:, :], A["cols"]), (scal[:, :], A["scal"].partition_broadcast(P)),
                             (wo0[:, :], A["wo0"]), (rows[:, :, :], A["rows"].partition_broadcast(P))):
                sp.dma_start(dst, src).then_inc(w_l0, 16)
            sp.dma_start(slot_raw, A["slots"].rearrange("(t p) d -> p t d", p=P)).then_inc(w_slots, 16)
            for k in range(2):
                sp.dma_start(egu[:, k, :], A["egu"][k, :, :]).then_inc(egu_in[k], 16)
                sp.dma_start(edn[:, k, :], A["edn"][k, :, :]).then_inc(edn_in[k], 16)
                sp.dma_start(w1ring[:, k, :], A["w1"][k, :, :]).then_inc(w1_in[k], 16)
                sp.dma_start(w2ring[:, k, :], A["w2"][k, :, :]).then_inc(w2_in[k], 16)
            sp.dma_start(gbias[:, :], A["gbias"].partition_broadcast(P)).then_inc(w_rest, 16)
            for dst, name in ((wqv, "wqv"), (gw1, "gw1"), (sgT, "sgT"), (suT, "suT"), (sdT, "sdT"), (wq2, "wq2"), (wk2, "wk2"),
                              (wv2, "wv2"), (rw2, "rw2"), (wq3, "wq3"), (wk3, "wk3"), (wv3, "wv3"), (wo3, "wo3"), (w1f, "w1f"),
                              (w2f, "w2f")):
                whole = dst[:, :, :] if len(A[name].shape) == 3 else dst[:, :]
                sp.dma_start(whole, A[name]).then_inc(w_rest, 16)
            with sp.Fori(0, E0 // 2 - 1) as i:
                for k in range(2):
                    sp.wait_ge(h0_done, i * 4 + 2 * (k + 1))
                    sp.dma_start(egu[:, k, :], A["egu"][bass.ds(i * 2 + (k + 2), 1), :, :].rearrange("a p n -> (a p) n")).then_inc(egu_in[k], 16)
                    sp.wait_ge(eo_sb, i * 2 + (k + 1))
                    sp.dma_start(edn[:, k, :], A["edn"][bass.ds(i * 2 + (k + 2), 1), :, :].rearrange("a p n -> (a p) n")).then_inc(edn_in[k], 16)
            sp.wait_ge(x_done, 2 * NT)
            sp.dma_start(ctx_tok[0:C], A["ctx"].rearrange("(b j) d -> j b d", j=C)).then_inc(ctx_in, 16)
            with sp.Fori(0, NC1 // 2 - 1) as i:
                for k in range(2):
                    sp.wait_ge(wdn_lo, i * 2 + (k + 1))
                    sp.dma_start(w1ring[:, k, :], A["w1"][bass.ds(i * 2 + (k + 2), 1), :, :].rearrange("a p n -> (a p) n")).then_inc(w1_in[k], 16)
            for k in range(2):
                sp.wait_ge(wdn_lo, NC1 - 2 + k + 1)
                sp.dma_start(w1ring[:, k, :], A["w1"][k, :, :]).then_inc(w1_in[k], 16)
            with sp.Fori(0, NC1 // 2 - 1) as i:
                for k in range(2):
                    sp.wait_ge(wdn_lo, i * 2 + (NC1 + k + 1))
                    sp.dma_start(w1ring[:, k, :], A["w1"][bass.ds(i * 2 + (k + 2), 1), :, :].rearrange("a p n -> (a p) n")).then_inc(w1_in[k], 16)
            with sp.Fori(0, NC2 // 2 - 1) as i:
                for k in range(2):
                    sp.wait_ge(wdn_lo, i * 2 + (2 * NC1 + k + 1))
                    sp.dma_start(w2ring[:, k, :], A["w2"][bass.ds(i * 2 + (k + 2), 1), :, :].rearrange("a p n -> (a p) n")).then_inc(w2_in[k], 16)
            for k in range(2):
                sp.wait_ge(wdn_lo, 2 * NC1 + NC2 - 2 + k + 1)
                sp.dma_start(w2ring[:, k, :], A["w2"][k, :, :]).then_inc(w2_in[k], 16)
            with sp.Fori(0, NC2 // 2 - 1) as i:
                for k in range(2):
                    sp.wait_ge(wdn_lo, i * 2 + (2 * NC1 + NC2 + k + 1))
                    sp.dma_start(w2ring[:, k, :], A["w2"][bass.ds(i * 2 + (k + 2), 1), :, :].rearrange("a p n -> (a p) n")).then_inc(w2_in[k], 16)
            ot = out.rearrange("(t p) d -> p t d", p=P)
            for g in range(NG):
                sp.wait_ge(x_done, 7 * NT + 4 * g + 4)
                sp.dma_start(ot[:, 4 * g:4 * g + 4, :], X[:, 4 * g:4 * g + 4, :]).then_inc(out_done, 16)
            sp.wait_ge(out_done, 16 * NG)

        @block.gpsimd
        def _(pool):
            step = [0]

            def then(ins):
                step[0] += 1
                ins.then_inc(pool_step, 1)
                pool.wait_ge(pool_step, step[0])

            pool.memset(neghalf[:, :], -0.5)
            pool.memset(epst[:, :], EPS)
            pool.memset(ones[:, :], 1.0)
            then(pool.memset(ident[:, :], 0.0))
            then(pool.affine_select(out=ident[:, :], in_=ident[:, :], compare_op=ALU.not_equal, fill=1.0, base=0,
                                    pattern=[[-1, P]], channel_multiplier=1))
            pool.memset(headmask[:, :], 1.0)
            then(pool.memset(ltmask[:, :, :], 1.0))
            then(pool.affine_select(out=headmask[:, :], in_=headmask[:, :], compare_op=ALU.is_ge, fill=0.0, base=0,
                                    pattern=[[-HD, H0]], channel_multiplier=1))
            then(pool.affine_select(out=headmask[:, :], in_=headmask[:, :], compare_op=ALU.is_ge, fill=0.0, base=HD - 1,
                                    pattern=[[HD, H0]], channel_multiplier=-1))
            then(pool.affine_select(out=ltmask[:, :, :], in_=ltmask[:, :, :], compare_op=ALU.is_ge, fill=0.0, base=-1,
                                    pattern=[[1, 8], [-1, 8]], channel_multiplier=0))
            then(pool.memset(vaug, 0.0))
            pool.memset(vaug[0:C, :, 0, HD:HD + 1], 1.0)
            then(pool.memset(vaug[C:P, :, 1, HD:HD + 1], 1.0))
            pool.tensor_copy(identb[:, :], ident[:, :]).then_inc(consts, 1)

            def ln_power(L, g):
                s = slice(4 * g, 4 * g + 4)
                pool.wait_ge(ln_var, NG * L + g + 1)
                if L != 1:
                    pool.tensor_tensor(rstd[:, s], veps[:, s], neghalf[:, s], ALU.pow).then_inc(ln_rstd, 1)
                    return
                then(pool.tensor_tensor(rtmp[:, s], veps[:, s], neghalf[:, s], ALU.pow))
                then(pool.tensor_tensor(rstd[:, s], rtmp[:, s], rtmp[:, s], ALU.mult))
                then(pool.tensor_tensor(rstd[:, s], rstd[:, s], mv[:, s, 1], ALU.mult))
                then(pool.tensor_tensor(rstd[:, s], rstd[:, s], epst[:, s], ALU.add))
                then(pool.tensor_tensor(rstd[:, s], rstd[:, s], neghalf[:, s], ALU.pow))
                pool.tensor_tensor(rstd[:, s], rstd[:, s], rtmp[:, s], ALU.mult).then_inc(ln_rstd, 1)

            def norm_low(layer, hf):
                for q in range(2):
                    pool.wait_ge(xh_hi, 4 * layer + 2 * hf + q + 1)
                    r = slice(512 * q, 512 * q + 512)
                    pool.tensor_tensor(xh[:, 1, r], xnT[:, 1024 * hf + 512 * q:1024 * hf + 512 * q + 512], xh[:, 0, r].bitcast(F32),
                                       ALU.subtract).then_inc(xh_lo, 1)

            def gate_up1_low(c, slot):
                pool.wait_ge(wgu_hi, c + 1)
                pool.tensor_tensor(wgu[:, slot, 1, :], w1ring[:, slot, 0:2 * P], wgu[:, slot, 0, :].bitcast(F32), ALU.subtract).then_inc(wgu_lo, 1)

            def down1_low(c, slot):
                pool.wait_ge(wdn_hi, c + 1)
                pool.tensor_tensor(wdn[:, slot, 1, :], w1ring[:, slot, 2 * P:3 * P], wdn[:, slot, 0, :].bitcast(F32), ALU.subtract).then_inc(wdn_lo, 1)

            def hidden1_low(n, k):
                pool.wait_ge(hh_hi, n + 1)
                pool.tensor_tensor(hh[:, k, 1, :], h1[:, k, :], hh[:, k, 0, :].bitcast(F32), ALU.subtract).then_inc(hh_lo, 1)

            def experts1_low():
                norm_low(0, 0)
                gate_up1_low(0, 0)

                def chunk_pair(i, last=False):
                    for slot in range(2):
                        if later(i, 1) or slot:
                            hidden1_low(i * 4 + (2 * slot - 1), 1)
                        down1_low(i * 2 + slot, slot)
                        if not (last and slot):
                            gate_up1_low(i * 2 + (slot + 1), 1 - slot)
                        hidden1_low(i * 4 + 2 * slot, 0)

                chunk_pair(0)
                with pool.Fori(1, NC1 // 2) as i:
                    chunk_pair(i)
                norm_low(0, 1)
                with pool.Fori(NC1 // 2, NC1 - 1) as i:
                    chunk_pair(i)
                chunk_pair(NC1 - 1, True)
                hidden1_low(4 * NC1 - 1, 1)

            def up2_low(c, slot):
                pool.wait_ge(wgu_hi, c + 1)
                pool.tensor_tensor(wgu[:, slot, 1, 0:P], w2ring[:, slot, 0:P], wgu[:, slot, 0, 0:P].bitcast(F32), ALU.subtract).then_inc(wgu_lo, 1)

            def down2_low(c, slot):
                pool.wait_ge(wdn_hi, c + 1)
                pool.tensor_tensor(wdn[:, slot, 1, :], w2ring[:, slot, P:2 * P], wdn[:, slot, 0, :].bitcast(F32), ALU.subtract).then_inc(wdn_lo, 1)

            def hidden2_low(n, k):
                pool.wait_ge(hh_hi, n + 1)
                pool.tensor_tensor(hh[:, k, 1, :], h2[:, k, :], hh[:, k, 0, :].bitcast(F32), ALU.subtract).then_inc(hh_lo, 1)

            def experts2_low():
                norm_low(1, 0)
                up2_low(2 * NC1, 0)

                def chunk_pair(i, first=False, last=False):
                    for slot in range(2):
                        if slot or not first:
                            hidden2_low(i * 4 + (2 * slot - 1), 1)
                        down2_low(i * 2 + slot, slot)
                        if not (last and slot):
                            up2_low(i * 2 + (slot + 1), 1 - slot)
                        hidden2_low(i * 4 + 2 * slot, 0)

                chunk_pair(NC1, first=True)
                with pool.Fori(NC1 + 1, NC1 + NC2 // 2) as i:
                    chunk_pair(i)
                norm_low(1, 1)
                with pool.Fori(NC1 + NC2 // 2, NC1 + NC2 - 1) as i:
                    chunk_pair(i)
                chunk_pair(NC1 + NC2 - 1, last=True)
                hidden2_low(4 * (NC1 + NC2) - 1, 1)

            for L in range(LAYERS):
                for g in range(NG):
                    ln_power(L, g)
                if L == 0:
                    pool.wait_ge(krep_done, 1)
                    for b in range(1, B, 2):
                        pool.tensor_tensor(kbd[:, b], wide(krep[:, b * C:(b + 1) * C].unsqueeze(1), H0, C),
                                           wide(headmask[:, :].unsqueeze(2), H0, C), ALU.mult).then_inc(kbd_done[1], 1)
                    pool.wait_ge(se_var, 1)
                    pool.tensor_tensor(srstd[:, 1, :], srstd[:, 0, :], neghalf[:, 0:ES // P], ALU.pow).then_inc(se_rstd, 1)
                if L == 1:
                    for k in range(4 * B):
                        pool.wait_ge(brec_done, k + 1)
                        pool.tensor_tensor(qb[:, k % 2], qb[:, k % 2], wide(recB[:, k % 2].unsqueeze(2), 2, N), ALU.mult)\
                            .then_inc(bnorm_done, 1)
                if L == 2:
                    pool.wait_ge(ln_xn, NG * L + NG)
                    pool.tensor_tensor(X[:, :, :], X[:, :, :], wide(rows[:, ROW["qv1_b"], :].unsqueeze(1), NT, D), ALU.add)\
                        .then_inc(xbias_done, 1)
                    then(pool.memset(sel1, 0.0))
                    per_expert = sel1.rearrange("p (e i) -> p e i", i=I1)
                    then(pool.affine_select(out=per_expert, in_=per_expert, compare_op=ALU.not_equal, fill=1.0, base=0,
                                            pattern=[[-1, E1], [0, I1]], channel_multiplier=1))
                    pool.affine_select(out=per_expert, in_=per_expert, compare_op=ALU.not_equal, fill=1.0, base=-E1,
                                       pattern=[[-1, E1], [0, I1]], channel_multiplier=1).then_inc(pool_made, 1)
                if L == 3:
                    experts1_low()
                if L == 5:
                    pool.wait_ge(x_done, NT * L)
                    pool.memset(cpk, 0.0)
                    then(pool.memset(sel2, 0.0))
                    wide2 = sel2[:, 4:12, :].rearrange("p (e c) n -> p e (c n)", c=2)
                    for part in range(3):
                        then(pool.affine_select(out=sel2[:, 0:4, :], in_=sel2[:, 0:4, :], compare_op=ALU.not_equal, fill=1.0,
                                                base=-E2 * part, pattern=[[-1, 4], [0, P]], channel_multiplier=1))
                        last = pool.affine_select(out=wide2, in_=wide2, compare_op=ALU.not_equal, fill=1.0,
                                                  base=-E2 * part - 4, pattern=[[-1, 4], [0, 2 * P]], channel_multiplier=1)
                        if part < 2:
                            then(last)
                    last.then_inc(pool_made, 1)
                    experts2_low()
                if L == 6:
                    pool.wait_ge(ln_xn, NG * L + NG)
                    pool.tensor_tensor(X[:, :, :], X[:, :, :], wide(rows[:, ROW["o3_b"], :].unsqueeze(1), NT, D), ALU.add)\
                        .then_inc(xbias_done, 1)
                if L == 7:
                    pool.wait_ge(x_done, NT * L)
                    pool.memset(hpad, 0.0).then_inc(pool_made, 1)

        @block.scalar
        def _(act):
            def copy(dst, src):
                return act.activation(dst, src, ACT.Copy)

            def ln_evac(L):
                for g in range(NG):
                    act.wait_ge(ln_tp, NG * L + g + 1)
                    dst = xnT[:, 512 * g:512 * g + 512]
                    if L == 1:
                        ins = act.activation(dst, bank(6 + g % 2), ACT.Identity, scale=cols[:, COL["norm_g"]:COL["norm_g"] + 1],
                                             bias=cols[:, COL["norm_b"]:COL["norm_b"] + 1])
                    else:
                        ins = copy(dst, bank(6 + g % 2))
                    ins.then_inc(ln_xnT, 1)

            act.wait_ge(kv_mm, 1)
            copy(krep, bank(0)).then_inc(krep_done, 1)
            act.wait_ge(consts, 1)
            vps = psum[:, 1, 0:B * HD].rearrange("p (b d) -> p b d", b=B)
            copy(vaug[0:C, :, 0, 0:HD], vps[0:C])
            copy(vaug[C:P, :, 1, 0:HD], vps[C:P]).then_inc(vaug_done, 1)
            ln_evac(0)
            for g in range(NG):
                act.wait_ge(q_mm, g + 1)
                act.activation(qT[:, 512 * g:512 * g + 512], bank(2 + g), ACT.Copy, scale=float(HD) ** -0.5).then_inc(q_sb, 1)
            act.wait_ge(se_n, 2)
            for g in range(2):
                act.wait_ge(se_tp, g + 1)
                act.activation(seT[:, 512 * g:512 * g + 512], bank(6 + g), ACT.Identity, scale=slot_gs[:, 0:1], bias=slot_gs[:, 1:2])\
                    .then_inc(se_T, 1)
            for t in range(NT + 3):
                if t >= 3:
                    u = t - 3
                    act.wait_ge(yT_ready, u + 1)
                    if u >= 2:
                        act.wait_ge(out_ready, u - 1)
                    copy(y0T[:, u % 2, :], psum[:, 7, 256:384]).then_inc(yT_sb, 1)
                if 1 <= t <= NT:
                    u = t - 1
                    act.wait_ge(et_ready, u + 1)
                    if u >= 2:
                        act.wait_ge(av_ready, u - 1)
                    copy(simET[:, u % 2, :], psum[:, 4:6, :].rearrange("p a n -> p (a n)")).then_inc(et_sb, 1)
                if t < NT:
                    act.wait_ge(sim_used, t + 1)
                    if t >= 2:
                        act.wait_ge(et_ready, t - 1)
                    act.activation(simE[:, t % 2, :], simS[:, t % 2].rearrange("p h k -> p (h k)"), ACT.Exp).then_inc(exp_done, 1)

            act.wait_ge(x_done, NT)
            ln_evac(1)

            def bexp(k):
                act.wait_ge(bmax_done, k + 1)
                if k >= 2:
                    act.wait_ge(bT_ready, k - 1)
                for c in range(2):
                    last = act.activation(qb[:, k % 2, c, :], psum[:, k % 2, c * N:(c + 1) * N], ACT.Exp,
                                          bias=nmB[:, k % 2, c:c + 1], accum_out=sumB[:, k % 2, c:c + 1])
                last.then_inc(bexp_done, 1)

            def aexp(t):
                act.wait_ge(amax_done, t + 1)
                if t >= 2:
                    act.wait_ge(pT_ready, t - 1)
                act.activation(pbuf[:, t % 2, :], psum[:, 2:4, :].rearrange("p a n -> p (a n)"), ACT.Exp, bias=nmA[:, t:t + 1],
                               accum_out=rsumA[:, t:t + 1]).then_inc(aexp_done, 1)

            def pt_evac(t):
                act.wait_ge(pT_ready, t + 1)
                copy(PT[:, :, t * P:(t + 1) * P], psum[:, 4:6, :].rearrange("p a (c n) -> p (a c) n", c=4)).then_inc(pt_sb, 1)

            def slots_evac(b, hf):
                act.wait_ge(slots_mm, 2 * b + hf + 1)
                act.activation(slotsT[:, 8 * hf:8 * hf + 8, b, :], bank(6 + hf).rearrange("p (e s) -> p e s", s=S0), ACT.Identity,
                               scale=cols[:, COL["norm_g"]:COL["norm_g"] + 1], bias=cols[:, COL["norm_b"]:COL["norm_b"] + 1])\
                    .then_inc(slots_sb, 1)

            bexp(0)
            bexp(1)
            for q in range(4 * B + 2):
                if q % 2 == 0:
                    if q >= 2:
                        pt_evac(q // 2 - 1)
                    if q < 4 * B:
                        aexp(q // 2)
                if q + 2 < 4 * B:
                    bexp(q + 2)
                if q >= 4 and q % 4 == 1:
                    slots_evac(q // 4 - 1, 1)
                if q % 4 == 3:
                    slots_evac(q // 4, 0)

            def gelu(e, f, k):
                n = 2 * e + f
                act.wait_ge(eg_ready, n + 1)
                if not isinstance(n, int) or n >= 2:
                    act.wait_ge(h0_done, n - 1)
                act.activation(gel[:, f, :], bank(f), ACT.Gelu, bias=egu[:, k, 2 * F0 + f:2 * F0 + f + 1]).then_inc(gelu_done, 1)

            def eo_evac(e, k):
                act.wait_ge(ed_ready, e + 1)
                act.activation(eoT[:, :, k, :], bank(4 + k).rearrange("p (b s) -> p b s", s=S0), ACT.Identity,
                               bias=edn[:, k, F0:F0 + 1]).then_inc(eo_sb, 1)

            def eo_low(c):
                act.wait_ge(eoT_tp[0], c + 1)
                copy(eo[:, bass.ds(c, 1), 0:4, :].rearrange("p a b o -> p (a b o)"), bank(6)).then_inc(eo_tok[0], 1)

            def expert_pair(i, first):
                for k in range(2):
                    gelu(i * 2 + k, 0, k)
                    if not (first and k == 0):
                        eo_evac(i * 2 + (k - 1), 1 - k)
                    gelu(i * 2 + k, 1, k)
                    if not first and k == 0:
                        eo_low(i + (-1))

            expert_pair(0, True)
            with act.Fori(1, E0 // 2) as i:
                expert_pair(i, False)
            eo_evac(E0 - 1, 1)
            eo_low(E0 // 2 - 1)

            act.wait_ge(x_done, 2 * NT)
            act.wait_ge(dw2_mm, 1)
            act.activation(dw2[0:1, :], psum[0:1, 0, :], ACT.Identity, bias=scal[0:1, 1:2]).then_inc(dw2_sb, 1)
            ln_evac(2)
            for hf in range(2):
                act.wait_ge(sim_sub, hf + 1)
                act.activation(e1[:, 8 * hf:8 * hf + 8, :], s1[:, 8 * hf:8 * hf + 8, :], ACT.Exp).then_inc(sim_exp, 1)
            act.wait_ge(bt_max, 1)
            act.activation(bt[0:B, :], psum[0:B, 7, 0:N], ACT.Exp, bias=bsm[0:B, 0:1], accum_out=bsm[0:B, 1:2]).then_inc(bt_exp, 1)
            for g in range(NG):
                act.wait_ge(aT_tp, g + 1)
                copy(aT[0:C, 512 * g:512 * g + 512], psum[0:C, 2 + g, :]).then_inc(aT_sb, 1)
            act.wait_ge(btT_tp, 1)
            copy(btT, psum[:, 7, 256:256 + TB * B].rearrange("p (k b) -> p k b", k=TB)).then_inc(btT_sb, 1)
            act.wait_ge(hc_mm, 1)
            copy(hcT, psum[:, 7, 288:288 + B]).then_inc(hc_sb, 1)
            for g in range(NG):
                act.wait_ge(hq_mm, g + 1)
                copy(hqT[:, 512 * g:512 * g + 512], bank((6, 0, 1, 2)[g])).then_inc(hq_sb, 1)

            act.wait_ge(x_done, 3 * NT)
            ln_evac(3)
            for hf in range(2):
                act.wait_ge(rl_mm, hf + 1)
                act.activation(sc1[:, 8 * hf:8 * hf + 8, :], bank(hf).rearrange("p (t e) -> p t e", e=E1), ACT.Sigmoid).then_inc(rl_sig, 1)
            def norm_high(layer, hf):
                for q in range(2):
                    copy(xh[:, 0, 512 * q:512 * q + 512], xnT[:, 1024 * hf + 512 * q:1024 * hf + 512 * q + 512]).then_inc(xh_hi, 1)

            def shared_sum(g):
                act.wait_ge(sd_ready, g + 1)
                copy(osh[:, 512 * g:512 * g + 512], bank(6 + g % 2)).then_inc(osh_done, 1)

            norm_high(0, 0)
            for m in range(2 * NG):
                act.wait_ge(sg_ready, m + 1)
                if m >= 2:
                    act.wait_ge(hs_done, m - 1)
                act.activation(sil[0:I1, m % 2, :], psum[0:I1, 2 + m % 2, :], ACT.Silu).then_inc(sil_s, 1)
                if m % 2 and m >= 3:
                    shared_sum(m // 2 - 1)
            shared_sum(NG - 1)
            for g in range(NG):
                act.wait_ge(rw_tp, g + 1)
                copy(rwr[:, 512 * g:512 * g + 512], bank(g)).then_inc(rwr_hi, 1)

            def gate_up1_high(i, slot, local):
                act.wait_ge(w1_in[slot], i * 16 + 16)
                if later(i, 1):
                    act.wait_ge(up_ready, i * 4 + (2 * slot - 2))
                copy(selr[:, slot, :], sel1[:, bass.ds(local, P)])
                copy(wgu[:, slot, 0, :], w1ring[:, slot, 0:2 * P]).then_inc(wgu_hi, 1)

            def down1_high(i, slot):
                if later(i, 1):
                    act.wait_ge(down_done, i * 4 + (2 * slot - 2))
                copy(wdn[:, slot, 0, :], w1ring[:, slot, 2 * P:3 * P]).then_inc(wdn_hi, 1)

            def silu1(n, k):
                act.wait_ge(gate_ready, n + 1)
                if later(n, 2):
                    act.wait_ge(prod_done, n - 1)
                act.activation(sil[:, k, :], bank(k), ACT.Silu).then_inc(nl_done, 1)

            def hidden1_high(n, k):
                act.wait_ge(hid_done, n + 1)
                if later(n, 2):
                    act.wait_ge(down_done, n - 1)
                copy(hh[:, k, 0, :], h1[:, k, :]).then_inc(hh_hi, 1)

            def chunk_pair1(i, hf, last=False):
                for slot in range(2):
                    silu1(i * 4 + 2 * slot, 0)
                    if later(i, 1) or slot:
                        hidden1_high(i * 4 + (2 * slot - 1), 1)
                    down1_high(i, slot)
                    if slot == 0:
                        gate_up1_high(i, 1, i * 2 * P + (P - NC1 * P * hf))
                    elif not last:
                        gate_up1_high(i + 1, 0, 0 if last is None else i * 2 * P + (2 * P - NC1 * P * hf))
                    silu1(i * 4 + (2 * slot + 1), 1)
                    hidden1_high(i * 4 + 2 * slot, 0)

            act.wait_ge(pool_made, 1)
            gate_up1_high(0, 0, 0)
            chunk_pair1(0, 0)
            with act.Fori(1, NC1 // 2 - 1) as i:
                chunk_pair1(i, 0)
            chunk_pair1(NC1 // 2 - 1, 0, None)
            act.wait_ge(up_ready, 2 * NC1)
            norm_high(0, 1)
            with act.Fori(NC1 // 2, NC1 - 1) as i:
                chunk_pair1(i, 1)
            chunk_pair1(NC1 - 1, 1, True)
            hidden1_high(4 * NC1 - 1, 1)

            def attention_tail(L, base):
                act.wait_ge(sim_sub, base + 3)
                for hf in range(2):
                    act.wait_ge(sim_sub, base + hf + 3)
                    act.activation(e2[:, 8 * hf:8 * hf + 8, :], s2[:, 8 * hf:8 * hf + 8, :], ACT.Exp).then_inc(sim_exp, 1)
                for g in range(NG):
                    act.wait_ge(e2_tp, 2 * base + g + 1)
                    copy(e2T[0:C, 512 * g:512 * g + 512], psum[0:C, 2 + g, :]).then_inc(e2_sb, 1)

            act.wait_ge(x_done, 4 * NT)
            ln_evac(4)
            attention_tail(4, 0)

            act.wait_ge(x_done, 5 * NT)
            ln_evac(5)
            act.wait_ge(rl_mm, 3)
            act.activation(pr2, psum[:, 0, 0:NT * E2].rearrange("p (t e) -> p t e", e=E2), ACT.Sigmoid).then_inc(rl_sig, 1)
            norm_high(1, 0)
            for q in range(2):
                act.wait_ge(rw_tp, NG + q + 1)
                copy(cT[:, 1024 * q:1024 * q + 1024], bank(1 + q).bitcast(BF16)).then_inc(rw_sb, 1)

            def up2_high(i, slot):
                act.wait_ge(w2_in[slot], i * 16 + (16 - 16 * NC1))
                act.wait_ge(up_ready, i * 4 + (2 * slot - 2))
                copy(wgu[:, slot, 0, 0:P], w2ring[:, slot, 0:P]).then_inc(wgu_hi, 1)

            def down2_high(i, slot):
                act.wait_ge(down_done, i * 4 + (2 * slot - 2))
                copy(wdn[:, slot, 0, :], w2ring[:, slot, P:2 * P]).then_inc(wdn_hi, 1)

            def relu2(n, k):
                act.wait_ge(up_ready, n + 1)
                act.wait_ge(hid_done, n - 1)
                act.activation(r2[:, k, :], bank(k), ACT.Relu).then_inc(nl_done, 1)

            def hidden2_high(n, k):
                act.wait_ge(hid_done, n + 1)
                act.wait_ge(down_done, n - 1)
                copy(hh[:, k, 0, :], h2[:, k, :]).then_inc(hh_hi, 1)

            def chunk_pair2(i, first=False, last=False):
                for slot in range(2):
                    relu2(i * 4 + 2 * slot, 0)
                    if slot or not first:
                        hidden2_high(i * 4 + (2 * slot - 1), 1)
                    down2_high(i, slot)
                    if slot == 0:
                        up2_high(i, 1)
                    elif not last:
                        up2_high(i + 1, 0)
                    relu2(i * 4 + (2 * slot + 1), 1)
                    hidden2_high(i * 4 + 2 * slot, 0)

            up2_high(NC1, 0)
            chunk_pair2(NC1, first=True)
            with act.Fori(NC1 + 1, NC1 + NC2 // 2) as i:
                chunk_pair2(i)
            act.wait_ge(up_ready, 4 * NC1 + 2 * NC2)
            norm_high(1, 1)
            with act.Fori(NC1 + NC2 // 2, NC1 + NC2 - 1) as i:
                chunk_pair2(i)
            chunk_pair2(NC1 + NC2 - 1, last=True)
            hidden2_high(4 * (NC1 + NC2) - 1, 1)
            act.wait_ge(down_done, 4 * (NC1 + NC2))
            for q in range(NG):
                copy(o2T[:, 512 * q:512 * q + 512], bank(4 + q)).then_inc(o2_sb, 1)

            act.wait_ge(x_done, 6 * NT)
            ln_evac(6)
            attention_tail(6, 2)
            for g in range(NG):
                act.wait_ge(c3_mm, g + 1)
                copy(c3T[:, 512 * g:512 * g + 512], bank((0, 1, 2, 3)[g])).then_inc(c3_sb, 1)

            act.wait_ge(x_done, 7 * NT)
            for g in range(2):
                act.wait_ge(xi_tp, g + 1)
                copy(xiT[:, 1024 * g:1024 * g + 1024], bank(g).bitcast(BF16)).then_inc(xi_sb, 1)
            act.wait_ge(wq_done, 1)
            for g in range(NG):
                act.wait_ge(rsB_mm, g + 1)
                act.activation(rsB[:, 512 * g:512 * g + 512], bank(2 + g), ACT.Copy, scale=wm[:, 0:1]).then_inc(rsB_sb, 1)
            for c in range(NC3):
                act.wait_ge(conv_done, c + 1)
                act.activation(g3[:, c, :], yc[:, c % 2, :], ACT.Silu).then_inc(g3_done, 1)
            for t in range(NT + 1):
                if t < NT:
                    act.wait_ge(qs4_done, t + 1)
                    if t >= 2:
                        act.wait_ge(gi_done, t - 1)
                    act.activation(ga[:, t % 2, :], bank(t % 4), ACT.Copy, scale=qs4[:, t:t + 1]).then_inc(ga_done, 1)
                if t >= 1:
                    act.wait_ge(gi_tp, t)
                    if t >= 3:
                        act.wait_ge(l2_ready, t - 2)
                    copy(giT[:, (t - 1) % 2], psum[:, 4 + (t - 1) % 2, 0:NC3 * P // 2].bitcast(BF16).rearrange("p (c n) -> p c n", c=NC3))\
                        .then_inc(gi_sb, 1)

        @block.vector
        def _(dve):
            step = [0]

            def then(ins):
                step[0] += 1
                ins.then_inc(dve_step, 1)
                dve.wait_ge(dve_step, step[0])

            def ln_stats(L, g):
                ts = range(4 * g, 4 * g + 4)
                if L == 0:
                    dve.wait_ge(x_in[g], 16)
                if L > 0:
                    dve.wait_ge(x_done, NT * L)
                for t in ts:
                    last = dve.bn_stats(stats[:, t, :], X[:, t, :])
                then(last)
                for t in ts:
                    last = dve.bn_aggr(mv[:, t, :], stats[:, t, :])
                then(last)
                s = slice(4 * g, 4 * g + 4)
                dve.tensor_scalar(veps[:, s], mv[:, s, 1], EPS, None, ALU.add).then_inc(ln_var, 1)

            def ln_apply(L, g):
                dve.wait_ge(ln_rstd, NG * L + g + 1)
                for t in range(4 * g, 4 * g + 4):
                    last = dve.tensor_scalar(xn[:, t, :], X[:, t, :], mv[:, t, 0:1], rstd[:, t:t + 1], ALU.subtract, ALU.mult)
                last.then_inc(ln_xn, 1)

            def layer_norm(L):
                ln_stats(L, 0)
                for g in range(1, NG):
                    ln_stats(L, g)
                    ln_apply(L, g - 1)
                ln_apply(L, NG - 1)

            layer_norm(0)
            dve.wait_ge(krep_done, 1)
            dve.wait_ge(consts, 1)
            for b in range(0, B, 2):
                dve.tensor_tensor(kbd[:, b], wide(krep[:, b * C:(b + 1) * C].unsqueeze(1), H0, C),
                                  wide(headmask[:, :].unsqueeze(2), H0, C), ALU.mult).then_inc(kbd_done[0], 1)
            dve.wait_ge(w_slots, 16)
            for t in range(ES // P):
                last = dve.bn_stats(sstats[:, t, :], slot_raw[:, t, :])
            then(last)
            for t in range(ES // P):
                last = dve.bn_aggr(smv[:, t, :], sstats[:, t, :])
            then(last)
            dve.tensor_scalar(srstd[:, 0, :], smv[:, :, 1], EPS, None, ALU.add).then_inc(se_var, 1)
            dve.wait_ge(w_l0, 16 * N_L0)
            dve.tensor_scalar(slot_gs[:, :], cols[:, COL["slot_g"]:COL["slot_g"] + 2], scal[:, 0:1], None, ALU.mult).then_inc(se_n, 1)
            dve.wait_ge(se_rstd, 1)
            for t in range(ES // P):
                last = dve.tensor_scalar(slot_n[:, t, :], slot_raw[:, t, :], smv[:, t, 0:1], srstd[:, 1, t:t + 1], ALU.subtract, ALU.mult)
            last.then_inc(se_n, 1)
            for t in range(NT + 3):
                if t < NT:
                    dve.wait_ge(sim_ready, t + 1)
                    sim = psum[:, 2 * (t % 2):2 * (t % 2) + 2, :].rearrange("p a (h k) -> p (a h) k", k=C)
                    then(dve.tensor_reduce(mx0[:, t % 2, :], sim, AX.X, ALU.max))
                    if t >= 2:
                        dve.wait_ge(exp_done, t - 1)
                    dve.tensor_tensor(simS[:, t % 2], sim, wide(mx0[:, t % 2, :].unsqueeze(2), H0, C), ALU.subtract).then_inc(sim_used, 1)
                if t >= 3:
                    u = t - 3
                    dve.wait_ge(out_ready, u + 1)
                    dve.tensor_tensor(X[:, u, :], X[:, u, :], psum[:, 7, 0:D], ALU.add).then_inc(x_done, 1)
                if 2 <= t <= NT + 1:
                    u = t - 2
                    dve.wait_ge(av_ready, u + 1)
                    av = psum[:, 6, 0:H0 * (HD + 1)].rearrange("p (h k) -> p h k", k=HD + 1)
                    then(dve.reciprocal(rden0[:, u % 2, :], av[:, :, HD]))
                    if u >= 2:
                        dve.wait_ge(yT_ready, u - 1)
                    dve.tensor_tensor(y0[:, u % 2], av[:, :, 0:HD], wide(rden0[:, u % 2, :].unsqueeze(2), H0, HD), ALU.mult)\
                        .then_inc(y_ready, 1)

            layer_norm(1)

            def bmax(k):
                dve.wait_ge(bl_ready, k + 1)
                if k >= 2:
                    dve.wait_ge(bexp_done, k - 1)
                dve.tensor_reduce(nmB[:, k % 2, :], bank(k % 2).rearrange("p (c n) -> p c n", c=2), AX.X, ALU.max, negate=True)\
                    .then_inc(bmax_done, 1)

            def brec(k):
                dve.wait_ge(bexp_done, k + 1)
                if k >= 2:
                    dve.wait_ge(bnorm_done, k - 1)
                dve.reciprocal(recB[:, k % 2, :], sumB[:, k % 2, :]).then_inc(brec_done, 1)

            def amax(t):
                dve.wait_ge(al_ready, t + 1)
                dve.tensor_reduce(nmA[:, t:t + 1], psum[:, 2:4, :].rearrange("p a n -> p (a n)"), AX.X, ALU.max, negate=True)\
                    .then_inc(amax_done, 1)

            def qt_evac(b, j):
                k = 4 * b + j
                dve.wait_ge(bT_ready, k + 1)
                if b >= 1:
                    dve.wait_ge(slots_mm, 2 * b - 1 + j // 2)
                dve.tensor_copy(qt[:, :, N * j:N * j + N], bank(4 + j % 2).rearrange("p (a n) -> p a n", a=TB)).then_inc(qt_sb, 1)

            bmax(0)
            bmax(1)
            brec(0)
            for q in range(4 * B):
                if q + 1 < 4 * B:
                    brec(q + 1)
                if q % 2 == 0:
                    amax(q // 2)
                qt_evac(q // 4, q % 4)
                if q + 2 < 4 * B:
                    bmax(q + 2)
            dve.wait_ge(aexp_done, NT)
            dve.reciprocal(rinvA, rsumA)

            def hidden0(e, f, k, first):
                n = 2 * e + f
                dve.wait_ge(eu_ready, n + 1)
                dve.wait_ge(gelu_done, n + 1)
                if not first:
                    dve.wait_ge(ed_ready, e - 1)
                dve.scalar_tensor_tensor(h0[:, k, f, :], bank(2 + f), egu[:, k, 2 * F0 + 2 + f:2 * F0 + 3 + f], gel[:, f, :],
                                         ALU.add, ALU.mult).then_inc(h0_done, 1)

            def eo_high(c):
                dve.wait_ge(eoT_tp[1], c + 1)
                dve.tensor_copy(eo[:, bass.ds(c, 1), 4:8, :].rearrange("p a b o -> p (a b o)"), bank(7)).then_inc(eo_tok[1], 1)

            for e in range(2):
                for f in range(2):
                    hidden0(e, f, e, True)
            with dve.Fori(1, E0 // 2) as i:
                for k in range(2):
                    for f in range(2):
                        hidden0(i * 2 + k, f, k, False)
                    if k == 0:
                        eo_high(i + (-1))
            eo_high(E0 // 2 - 1)
            for t in range(NT):
                dve.wait_ge(comb_ready, t + 1)
                dve.scalar_tensor_tensor(X[:, t, :], psum[:, 2 + t % 4, 0:D], rinvA[:, t:t + 1], X[:, t, :], ALU.mult, ALU.add)\
                    .then_inc(x_done, 1)

            dve.wait_ge(w_rest, 16 * (len(REST) + 1))
            dve.tensor_scalar(cw, ctxT[:, :], cols[:, COL["w_sim3"]:COL["w_sim3"] + 1], cols[:, COL["w_sim1"]:COL["w_sim1"] + 1],
                              ALU.mult, ALU.add).then_inc(cw_done, 1)
            layer_norm(2)
            for hf in range(2):
                r = slice(8 * hf, 8 * hf + 8)
                sim = bank(hf).rearrange("p (t j) -> p t j", j=C)
                dve.wait_ge(sim_mm, hf + 1)
                then(dve.tensor_reduce(mx1[:, r], sim, AX.X, ALU.max))
                dve.tensor_tensor(s1[:, r, :], sim, wide(mx1[:, r].unsqueeze(2), 8, C), ALU.subtract).then_inc(sim_sub, 1)
            for hf in range(2):
                r = slice(8 * hf, 8 * hf + 8)
                dve.wait_ge(sim_exp, hf + 1)
                then(dve.tensor_reduce(den1[:, r], e1[:, r, :], AX.X, ALU.add))
                then(dve.reciprocal(rden1[:, r], den1[:, r]))
                dve.tensor_tensor(e1n[:, r, :], e1[:, r, :], wide(rden1[:, r].unsqueeze(2), 8, C), ALU.mult).then_inc(e1_norm, 1)
                if hf == 0:
                    dve.wait_ge(bt_tp, 1)
                    dve.tensor_reduce(bsm[0:B, 0:1], psum[0:B, 7, 0:N], AX.X, ALU.max, negate=True).then_inc(bt_max, 1)
            dve.wait_ge(bt_exp, 1)
            then(dve.reciprocal(bsm[0:B, 2:3], bsm[0:B, 1:2]))
            dve.tensor_scalar(btn[0:B, :], bt[0:B, :], bsm[0:B, 2:3], None, ALU.mult).then_inc(bt_norm, 1)
            dve.wait_ge(hc_sb, 1)
            for b in range(B):
                last = dve.tensor_scalar(xcT[:, N * b:N * b + N], xnT[:, N * b:N * b + N], hcT[:, b:b + 1], None, ALU.mult)
            last.then_inc(xc_done, 1)
            for g in range(NG):
                r = slice(512 * g, 512 * g + 512)
                dve.wait_ge(hq_sb, g + 1)
                dve.tensor_tensor(xhT[:, r], hqT[:, r], xnT[:, r], ALU.mult).then_inc(xh_done, 1)
            dve.wait_ge(xbias_done, 1)
            for t in range(NT):
                dve.wait_ge(qv_ready, t + 1)
                dve.tensor_tensor(X[:, t, :], psum[:, 3 + t % 3, 0:D], X[:, t, :], ALU.add).then_inc(x_done, 1)

            def rank_of(dst, v, a, b2, n):
                own = wide(v.unsqueeze(3), n, 8, 8)
                other = wide(v.unsqueeze(2), n, 8, 8)
                dve.tensor_tensor(b2, other, own, ALU.is_equal)
                then(dve.tensor_tensor(a, other, own, ALU.is_gt))
                then(dve.tensor_tensor(b2, b2, wide(ltmask[:, :, :].unsqueeze(1), n, 8, 8), ALU.mult))
                then(dve.tensor_tensor(a, a, b2, ALU.add))
                then(dve.tensor_reduce(dst, a, AX.X, ALU.add))

            layer_norm(3)

            def routing():
                dve.wait_ge(rl_sig, 2)
                then(dve.tensor_tensor(sfc, sc1, wide(gbias[:, :].unsqueeze(1), NT, E1), ALU.add))
                v = sfc.rearrange("p t (g j) -> p (t g) j", j=8)
                hi = t1.rearrange("p t (g j) -> p (t g) j", j=8)
                lo = t2.rearrange("p t (g j) -> p (t g) j", j=8)
                tmp = t3.rearrange("p t (g j) -> p (t g) j", j=8)
                dve.tensor_tensor(hi[:, :, 0:4], v[:, :, 0:4], v[:, :, 4:8], ALU.max)
                then(dve.tensor_tensor(lo[:, :, 0:4], v[:, :, 0:4], v[:, :, 4:8], ALU.min))
                at = 0
                for k in (2, 1):
                    x0, x1, y = slice(at, at + k), slice(at + k, at + 2 * k), slice(at + 2 * k, at + 3 * k)
                    dve.tensor_tensor(tmp[:, :, 0:k], hi[:, :, x0], hi[:, :, x1], ALU.min)
                    dve.tensor_tensor(tmp[:, :, 4:4 + k], lo[:, :, x0], lo[:, :, x1], ALU.max)
                    then(dve.tensor_tensor(hi[:, :, y], hi[:, :, x0], hi[:, :, x1], ALU.max))
                    then(dve.tensor_tensor(lo[:, :, y], tmp[:, :, 0:k], tmp[:, :, 4:4 + k], ALU.max))
                    at += 2 * k
                then(dve.tensor_tensor(gs.rearrange("p t g -> p (t g)"), hi[:, :, at], lo[:, :, at], ALU.add))
                rank_of(rank, gs, t1.rearrange("p t (g j) -> p t g j", j=8), t2.rearrange("p t (g j) -> p t g j", j=8), NT)
                then(dve.tensor_scalar(rank, rank, 3.5, None, ALU.is_lt))
                then(dve.tensor_tensor(t1.rearrange("p t (g j) -> p t g j", j=8), sfc.rearrange("p t (g j) -> p t g j", j=8),
                                       wide(rank.unsqueeze(3), NT, 8, 8), ALU.mult))
                for t in range(NT):
                    last = dve.max(top8[:, t, :], t1[:, t, :])
                then(last)
                for t in range(NT):
                    last = dve.match_replace(t2[:, t, :], top8[:, t, :], t1[:, t, :], -3.0e38)
                then(last)
                then(dve.tensor_tensor(t3, t1, t2, ALU.not_equal))
                then(dve.tensor_tensor(t3, t3, sc1, ALU.mult))
                then(dve.tensor_reduce(rsum1[:, 0, :], t3, AX.X, ALU.add))
                then(dve.tensor_scalar(rsum1[:, 0, :], rsum1[:, 0, :], 1e-20, None, ALU.add))
                then(dve.reciprocal(rsum1[:, 1, :], rsum1[:, 0, :]))
                then(dve.tensor_scalar(rsum1[:, 1, :], rsum1[:, 1, :], 2.5, None, ALU.mult))
                for k in range(2):
                    last = dve.tensor_tensor(rwp[:, :, k, :], t3, wide(rsum1[:, 1, :].unsqueeze(2), NT, E1), ALU.mult)
                last.then_inc(rw_done, 1)

            def shared_hidden(m):
                dve.wait_ge(sil_s, m + 1)
                if m >= 2:
                    dve.wait_ge(sd_ready, m // 2)
                dve.tensor_tensor(h1[0:I1, m % 2, :], psum[0:I1, 4 + m % 2, :], sil[0:I1, m % 2, :], ALU.mult).then_inc(hs_done, 1)

            for m in range(2 * NG):
                shared_hidden(m)
            routing()

            for g in range(NG):
                r = slice(512 * g, 512 * g + 512)
                dve.wait_ge(rwr_hi, g + 1)
                dve.tensor_tensor(rwr[E1:P, r], psum[E1:P, g, :], rwr[E1:P, r].bitcast(F32), ALU.subtract).then_inc(rwr_lo, 1)

            def hidden1(n, k):
                dve.wait_ge(up_ready, n + 1)
                dve.wait_ge(nl_done, n + 1)
                dve.tensor_tensor(u1[:, k, :], bank(2 + k), sil[:, k, :], ALU.mult).then_inc(prod_done, 1)
                dve.wait_ge(prod_done, n + 1)
                if later(n, 2):
                    dve.wait_ge(hh_hi, n - 1)
                    dve.wait_ge(hh_lo, n - 1)
                dve.tensor_tensor(h1[:, k, :], bank(4 + k), u1[:, k, :], ALU.mult).then_inc(hid_done, 1)

            def sum1(hf):
                dve.wait_ge(down_done, 2 * NC1 * (hf + 1))
                for q in range(2):
                    r = slice(1024 * hf + 512 * q, 1024 * hf + 512 * q + 512)
                    dve.tensor_tensor(osh[:, r], osh[:, r], bank(6 + q), ALU.add).then_inc(o1_done, 1)

            for s in range(4):
                hidden1(s, s % 2)
            with dve.Fori(1, NC1 // 2) as i:
                for s in range(4):
                    hidden1(i * 4 + s, s % 2)
            for s in range(4):
                hidden1(2 * NC1 + s, s % 2)
                if s == 1:
                    sum1(0)
            with dve.Fori(NC1 // 2 + 1, NC1) as i:
                for s in range(4):
                    hidden1(i * 4 + s, s % 2)
            sum1(1)
            for t in range(NT):
                dve.wait_ge(ffn_tp, t + 1)
                dve.tensor_tensor(X[:, t, :], psum[:, t % 4, 0:D], X[:, t, :], ALU.add).then_inc(x_done, 1)

            def project(L, base, qb_, kb_, vrow, mm):
                dve.wait_ge(qk2_mm, mm + 1)
                if kb_ is None:
                    dve.tensor_copy(k2T, bank(0)).then_inc(qk2_sb, 1)
                else:
                    dve.tensor_scalar(k2T, bank(0), cols[:, kb_:kb_ + 1], None, ALU.add).then_inc(qk2_sb, 1)
                dve.wait_ge(v2_mm, mm // 5 + 1)
                dve.tensor_tensor(v2[0:C], psum[0:C, 6:8, :].rearrange("p a (b d) -> p (a b) d", d=D),
                                  rows[0:C, vrow, :].unsqueeze(1).broadcast_to([C, B, D]), ALU.add).then_inc(v2_sb, 1)
                layer_norm(L)
                for g in range(NG):
                    dve.wait_ge(qk2_mm, mm + g + 2)
                    dve.tensor_scalar(q2T[:, 512 * g:512 * g + 512], bank(2 + g), cols[:, qb_:qb_ + 1], float(D) ** -0.5, ALU.add, ALU.mult)\
                        .then_inc(qk2_sb, 1)

            def softmax(base):
                for hf in range(2):
                    r = slice(8 * hf, 8 * hf + 8)
                    sim = bank(hf).rearrange("p (t j) -> p t j", j=C)
                    dve.wait_ge(sim_mm, base + hf + 3)
                    then(dve.tensor_reduce(mx2[:, r], sim, AX.X, ALU.max))
                    dve.tensor_tensor(s2[:, r, :], sim, wide(mx2[:, r].unsqueeze(2), 8, C), ALU.subtract).then_inc(sim_sub, 1)
                for hf in range(2):
                    r = slice(8 * hf, 8 * hf + 8)
                    dve.wait_ge(sim_exp, base + hf + 3)
                    then(dve.tensor_reduce(den2[:, r], e2[:, r, :], AX.X, ALU.add))
                    then(dve.reciprocal(rden2[:, r], den2[:, r]))

            project(4, 0, COL["q2_b"], COL["k2_b"], ROW["v2_b"], 0)
            softmax(0)
            for t in range(NT):
                dve.wait_ge(av2_ready, t + 1)
                dve.scalar_tensor_tensor(X[:, t, :], psum[:, (6, 7, 0, 1)[t % 4], 0:D], rden2[:, t:t + 1], X[:, t, :], ALU.mult, ALU.add)\
                    .then_inc(x_done, 1)

            layer_norm(5)
            dve.wait_ge(rl_sig, 3)
            rank_of(rank2, pr2, g2a, g2b, NT)
            then(dve.tensor_scalar(rank2, rank2, 1.5, None, ALU.is_lt))
            then(dve.tensor_tensor(rank2, rank2, pr2, ALU.mult))
            then(dve.tensor_reduce(rs2[:, 0, :], rank2, AX.X, ALU.add))
            then(dve.tensor_scalar(rs2[:, 0, :], rs2[:, 0, :], 1e-20, None, ALU.add))
            then(dve.reciprocal(rs2[:, 1, :], rs2[:, 0, :]))
            then(dve.tensor_tensor(rank2, rank2, wide(rs2[:, 1, :].unsqueeze(2), NT, E2), ALU.mult))
            dve.wait_ge(pool_made, 2)
            then(dve.tensor_copy(cpk[:, :, 0:E2], rank2))
            then(dve.tensor_tensor(rank2, rank2, cpk[:, :, 0:E2], ALU.subtract))
            then(dve.tensor_copy(cpk[:, :, E2:2 * E2], rank2))
            then(dve.tensor_tensor(rank2, rank2, cpk[:, :, E2:2 * E2], ALU.subtract))
            dve.tensor_copy(cpk[:, :, 2 * E2:3 * E2], rank2).then_inc(rw_done, 1)

            def hidden2(n, k):
                dve.wait_ge(nl_done, n + 1)
                dve.tensor_tensor(u2[:, k, :], bank(2 + k), r2[:, k, :], ALU.mult).then_inc(prod_done, 1)
                dve.wait_ge(prod_done, n + 1)
                dve.wait_ge(hh_hi, n - 1)
                dve.wait_ge(hh_lo, n - 1)
                dve.tensor_tensor(h2[:, k, :], u2[:, k, :], r2[:, k, :], ALU.mult).then_inc(hid_done, 1)

            with dve.Fori(NC1, NC1 + NC2) as i:
                for s in range(4):
                    hidden2(i * 4 + s, s % 2)
            for t in range(NT):
                dve.wait_ge(ffn_tp, NT + t + 1)
                dve.tensor_tensor(X[:, t, :], psum[:, t % 4, 0:D], X[:, t, :], ALU.add).then_inc(x_done, 1)

            project(6, 2, COL["q3_b"], None, ROW["v3_b"], 5)
            softmax(2)
            dve.wait_ge(xbias_done, 2)
            for t in range(NT):
                dve.wait_ge(av2_ready, NT + t + 1)
                dve.scalar_tensor_tensor(X[:, t, :], psum[:, 4 + t % 4, 0:D], rden2[:, t:t + 1], X[:, t, :], ALU.mult, ALU.add)\
                    .then_inc(x_done, 1)

            dve.wait_ge(x_done, 7 * NT)
            dve.tensor_reduce(wsum[:, 0:1], w1f[:, :], AX.X, ALU.add, apply_absolute_value=True)
            dve.tensor_reduce(wsum[:, 1:2], w2f[:, :, :].rearrange("p c o -> p (c o)"), AX.X, ALU.add, apply_absolute_value=True)\
                .then_inc(wsum_done, 1)
            layer_norm(7)
            dve.wait_ge(wsum_mm, 1)
            then(dve.tensor_scalar(wm, psum[:, 7, 0:2], 1.0 / (D * HID3), 1e-5, ALU.mult, ALU.max))
            then(dve.reciprocal(wr, wm))
            for k, (w, q) in enumerate(((w1f[:, :], w1q), (w2f[:, :, :].rearrange("p c o -> p (c o)"), w2q.rearrange("p c o -> p (c o)")))):
                then(dve.tensor_scalar(wa, w, wr[:, k:k + 1], MAGIC, ALU.mult, ALU.add))
                then(dve.tensor_scalar(wa, wa, MAGIC + 1.0, MAGIC - 1.0, ALU.min, ALU.max))
                last = dve.tensor_scalar(q, wa, MAGIC, None, ALU.subtract)
                if k == 0:
                    then(last)
            last.then_inc(wq_done, 1)
            dve.wait_ge(ln_xn, NG * 8)
            then(dve.tensor_reduce(am3, xn[:, :, :], AX.X, ALU.max, apply_absolute_value=True))
            then(dve.tensor_scalar(am3, am3, 1e-5, None, ALU.max))
            dve.tensor_scalar(rs3, am3, 1.0 / 127.0, None, ALU.mult).then_inc(rs3_done, 1)
            then(dve.reciprocal(qs3, am3))
            then(dve.tensor_scalar(qs3, qs3, 127.0, None, ALU.mult))
            for t in range(NT):
                last = dve.tensor_scalar(qa[:, t, :], xn[:, t, :], qs3[:, t:t + 1], MAGIC, ALU.mult, ALU.add)
            then(last)
            then(dve.tensor_scalar(qa, qa, MAGIC + 127.0, MAGIC - 128.0, ALU.min, ALU.max))
            dve.tensor_scalar(xi, qa, MAGIC, None, ALU.subtract).then_inc(xi_done, 1)
            dve.wait_ge(pool_made, 3)
            dve.wait_ge(rsB_sb, NG)
            for c in range(NC3):
                w = CONV + 4 * c
                for g in range(NG):
                    dve.wait_ge(l1_ready, NG * c + g + 1)
                    last = dve.tensor_tensor(hpad[:, c % 2, 2 * g:2 * g + 2, 1:N + 1],
                                             bank((NG * c + g) % 8).rearrange("p (b n) -> p b n", b=2),
                                             rsB[:, 512 * g:512 * g + 512].rearrange("p (b n) -> p b n", b=2), ALU.mult)
                    last.then_inc(hpad_done, 1)
                dve.wait_ge(hpad_done, NG * (c + 1))
                if c >= 2:
                    dve.wait_ge(g3_done, c - 1)
                y = yc[:, c % 2, :].rearrange("p (b n) -> p b n", b=B)
                then(dve.tensor_scalar(y, hpad[:, c % 2, :, 1:N + 1], cols[:, w + 1:w + 2], cols[:, w + 3:w + 4], ALU.mult, ALU.add))
                then(dve.scalar_tensor_tensor(y, hpad[:, c % 2, :, 0:N], cols[:, w:w + 1], y, ALU.mult, ALU.add))
                dve.scalar_tensor_tensor(y, hpad[:, c % 2, :, 2:N + 2], cols[:, w + 2:w + 3], y, ALU.mult, ALU.add).then_inc(conv_done, 1)

            def quant_scale(t):
                dve.wait_ge(g3_tp, t + 1)
                then(dve.tensor_reduce(am4[:, t:t + 1], bank(t % 4), AX.X, ALU.max, apply_absolute_value=True))
                then(dve.tensor_scalar(am4[:, t:t + 1], am4[:, t:t + 1], 1e-5, None, ALU.max))
                then(dve.reciprocal(qs4[:, t:t + 1], am4[:, t:t + 1]))
                dve.tensor_scalar(rs4[:, t:t + 1], am4[:, t:t + 1], wm[:, 1:2], 1.0 / 127.0, ALU.mult, ALU.mult)
                dve.tensor_scalar(qs4[:, t:t + 1], qs4[:, t:t + 1], 127.0, None, ALU.mult).then_inc(qs4_done, 1)

            for t in range(NT + 2):
                if t < NT:
                    quant_scale(t)
                if 1 <= t <= NT:
                    k = (t - 1) % 2
                    dve.wait_ge(ga_done, t)
                    then(dve.tensor_scalar(ga[:, k, :], ga[:, k, :], MAGIC, MAGIC + 127.0, ALU.add, ALU.min))
                    if t >= 3:
                        dve.wait_ge(gi_tp, t - 2)
                    dve.tensor_scalar(gi[:, k, :], ga[:, k, :], MAGIC - 128.0, MAGIC, ALU.max, ALU.subtract).then_inc(gi_done, 1)
                if t >= 2:
                    dve.wait_ge(l2_ready, t - 1)
                    dve.scalar_tensor_tensor(X[:, t - 2, :], psum[:, 6 + t % 2, 0:D], rs4[:, t - 2:t - 1], X[:, t - 2, :], ALU.mult, ALU.add)\
                        .then_inc(x_done, 1)

        @block.tensor
        def _(pe):
            def mm(dst, lhsT, rhs, start=True, stop=True):
                return pe.matmul(dst, lhsT=lhsT, rhs=rhs, start=start, stop=stop)

            def ln_transposes(L):
                for g in range(NG):
                    pe.wait_ge(ln_xn, NG * L + g + 1)
                    if g >= 2:
                        pe.wait_ge(ln_xnT, NG * L + g - 1)
                    for j in range(4):
                        last = pe.transpose(psum[:, 6 + g % 2, P * j:P * j + P], xn[:, 4 * g + j, :], ident[:, :])
                    last.then_inc(ln_tp, 1)

            pe.wait_ge(w_l0, 16 * N_L0)
            mm(bank(0), wk0[:, :], ctxT[:, :])
            for b in range(B):
                last = mm(psum[:, 1, HD * b:HD * b + HD], ctxTd[:, P * b:P * b + P], wv0[:, :])
            last.then_inc(kv_mm, 1)
            pe.wait_ge(consts, 1)
            ln_transposes(0)
            for g in range(NG):
                pe.wait_ge(ln_xnT, g + 1)
                mm(bank(2 + g), wq0[:, :], xnT[:, 512 * g:512 * g + 512]).then_inc(q_mm, 1)
            pe.wait_ge(vaug_done, 1)
            for t in range(NT + 3):
                if t < NT:
                    b = t // TB
                    pe.wait_ge(q_sb, max(t // 4 + 1, 2))
                    pe.wait_ge(kbd_done[b % 2], b // 2 + 1)
                    if t >= 2:
                        pe.wait_ge(sim_used, t - 1)
                    for hf in range(2):
                        last = mm(bank(2 * (t % 2) + hf), qT[:, P * t:P * t + P],
                                  kbd[:, b, 8 * hf:8 * hf + 8, :].rearrange("p h k -> p (h k)"))
                    last.then_inc(sim_ready, 1)
                if t == 1:
                    pe.wait_ge(se_n, 2)
                    pe.wait_ge(ln_xnT, NG)
                    for g in range(2):
                        for j in range(4):
                            last = pe.transpose(psum[:, 6 + g, P * j:P * j + P], slot_n[:, 4 * g + j, :], ident[:, :])
                        last.then_inc(se_tp, 1)
                    pe.wait_ge(se_T, 2)
                if t >= 3:
                    u = t - 3
                    pe.wait_ge(y_ready, u + 1)
                    if u >= 1:
                        pe.wait_ge(x_done, u)
                    pe.transpose(psum[:, 7, 256:384], y0[:, u % 2].rearrange("p h k -> p (h k)"), ident[:, :]).then_inc(yT_ready, 1)
                if 1 <= t <= NT:
                    u = t - 1
                    pe.wait_ge(exp_done, u + 1)
                    pe.wait_ge(et_sb, u) if u >= 1 else pe.wait_ge(q_sb, 4)
                    for j in range(H0 // 2):
                        last = pe.transpose(psum[:, 4 + j // 4, P * (j % 4):P * (j % 4) + P], simE[:, u % 2, P * j:P * j + P], ident[:, :])
                    last.then_inc(et_ready, 1)
                if t >= 3:
                    u = t - 3
                    pe.wait_ge(yT_sb, u + 1)
                    mm(psum[:, 7, 0:D], y0T[:, u % 2, :], wo0[:, :]).then_inc(out_ready, 1)
                if 2 <= t <= NT + 1:
                    u = t - 2
                    b = u // TB
                    pe.wait_ge(et_sb, u + 1)
                    if u >= 1:
                        pe.wait_ge(y_ready, u)
                    for j in range(H0 // 2):
                        w = 2 * (HD + 1)
                        last = mm(psum[:, 6, w * j:w * j + w], simET[:, u % 2, P * j:P * j + P],
                                  vaug[:, b].rearrange("p h k -> p (h k)"))
                    last.then_inc(av_ready, 1)

            pe.wait_ge(x_done, NT)
            ln_transposes(1)

            def logits_slots(k):
                b, j = k // 4, k % 4
                pe.wait_ge(ln_xnT, NG + b // 2 + 1)
                if k >= 2:
                    pe.wait_ge(bexp_done, k - 1)
                for c in range(2):
                    ch = 2 * j + c
                    last = mm(psum[:, k % 2, N * c:N * c + N], seT[:, P * ch:P * ch + P], xnT[:, N * b:N * b + N])
                last.then_inc(bl_ready, 1)

            def logits_tokens(t):
                if t >= 1:
                    pe.wait_ge(aexp_done, t)
                for hf in range(2):
                    last = mm(bank(2 + hf), xnT[:, P * t:P * t + P], seT[:, 512 * hf:512 * hf + 512])
                last.then_inc(al_ready, 1)

            def dispatch_T(k):
                b, j = k // 4, k % 4
                pe.wait_ge(bnorm_done, k + 1)
                if k >= 2:
                    pe.wait_ge(pt_sb, k // 2)
                    pe.wait_ge(qt_sb, k - 1)
                for a in range(TB):
                    for c in range(2):
                        last = pe.transpose(psum[:, 4 + j % 2, N * a + P * c:N * a + P * c + P], qb[:, k % 2, c, P * a:P * a + P], ident[:, :])
                last.then_inc(bT_ready, 1)

            def combine_T(t):
                pe.wait_ge(aexp_done, t + 1)
                pe.wait_ge(qt_sb, 2 * t + 2)
                for c in range(NC0):
                    last = pe.transpose(psum[:, 4 + c // 4, P * (c % 4):P * (c % 4) + P], pbuf[:, t % 2, P * c:P * c + P], ident[:, :])
                last.then_inc(pT_ready, 1)

            def slots_part(b, hf, a):
                if a == 0:
                    pe.wait_ge(qt_sb, 4 * b + 2 * hf + 2)
                    if b:
                        pe.wait_ge(slots_sb, 2 * (b - 1) + hf + 1)
                    else:
                        pe.wait_ge(ln_xnT, 2 * NG)
                last = mm(bank(6 + hf), xn[:, 2 * b + a, :], qt[:, a, 512 * hf:512 * hf + 512], a == 0, a == TB - 1)
                if a == TB - 1:
                    last.then_inc(slots_mm, 1)

            logits_slots(0)
            logits_slots(1)
            for q in range(4 * B + 2):
                if q < 4 * B:
                    if q % 2 == 0:
                        logits_tokens(q // 2)
                    dispatch_T(q)
                    if q + 2 < 4 * B:
                        logits_slots(q + 2)
                if q >= 2:
                    slots_part((q - 2) // 4, (q - 2) % 4 // 2, q % 2)
                if q % 2 and q < 4 * B:
                    combine_T(q // 2)

            pe.wait_ge(slots_sb, 2 * B)
            pe.wait_ge(pt_sb, NT)

            def gate_up0(e, f, k, first):
                n = 2 * e + f
                moving = slotsT[:, bass.ds(e, 1), :, :].rearrange("p a b s -> p (a b s)")
                if f == 0:
                    if first:
                        pe.wait_ge(egu_in[k], 16)
                if not first or k:
                    pe.wait_ge(gelu_done, n - 1)
                mm(bank(f), egu[:, k, P * f:P * f + P], moving).then_inc(eg_ready, 1)
                if not first or k:
                    pe.wait_ge(h0_done, n - 1)
                mm(bank(2 + f), egu[:, k, F0 + P * f:F0 + P * f + P], moving).then_inc(eu_ready, 1)

            def down0(e, k, first):
                pe.wait_ge(h0_done, e * 2 + 2)
                if not first:
                    pe.wait_ge(eo_sb, e - 1)
                for f in range(2):
                    last = mm(bank(4 + k), edn[:, k, P * f:P * f + P], h0[:, k, f, :], f == 0, f == 1)
                last.then_inc(ed_ready, 1)

            def outputs_T(c, first):
                pe.wait_ge(eo_sb, c * 2 + 2)
                for hf in range(2):
                    if not first:
                        pe.wait_ge(eo_tok[hf], c)
                    for j in range(4):
                        last = pe.transpose(psum[:, 6 + hf, P * j:P * j + P], eoT[:, 4 * hf + j].rearrange("p e s -> p (e s)"), ident[:, :])
                    last.then_inc(eoT_tp[hf], 1)

            def expert_pair(i, first, second=False):
                for k in range(2):
                    if not first:
                        pe.wait_ge(egu_in[k], i * 16 + 16)
                    gate_up0(i * 2 + k, 0, k, first)
                    if not (first and k == 0):
                        if k == 1:
                            pe.wait_ge(edn_in[0], i * 16 + 16)
                        else:
                            pe.wait_ge(edn_in[1], i * 16)
                        down0(i * 2 + (k - 1), 1 - k, first)
                    gate_up0(i * 2 + k, 1, k, first)
                    if k == 0 and not first:
                        outputs_T(i + (-1), second)

            expert_pair(0, True)
            expert_pair(1, False, True)
            with pe.Fori(2, E0 // 2) as i:
                expert_pair(i, False)
            pe.wait_ge(edn_in[1], 16 * (E0 // 2))
            down0(E0 - 1, 1, False)
            outputs_T(E0 // 2 - 1, False)
            for t in range(NT):
                b = t // TB
                pe.wait_ge(eo_tok[b // 4], E0 // 2)
                if t >= 4:
                    pe.wait_ge(x_done, NT + t - 3)
                for c in range(NC0):
                    last = mm(psum[:, 2 + t % 4, 0:D], PT[:, c, P * t:P * t + P], eo[:, c, b, :], c == 0, c == NC0 - 1)
                last.then_inc(comb_ready, 1)

            pe.wait_ge(x_done, 2 * NT)
            pe.wait_ge(w_rest, 16 * (len(REST) + 1))
            mm(psum[0:1, 0, :], cols[:, COL["w_sim2"]:COL["w_sim2"] + 1], ctxT[:, :]).then_inc(dw2_mm, 1)
            ln_transposes(2)
            pe.wait_ge(dw2_sb, 1)
            pe.wait_ge(cw_done, 1)
            for t in range(NT):
                b = t // TB
                if t % 4 == 0:
                    pe.wait_ge(ln_xnT, 2 * NG + t // 4 + 1)
                dst = psum[:, t // 8, C * (t % 8):C * (t % 8) + C]
                mm(dst, xnT[:, P * t:P * t + P], cw[:, C * b:C * b + C], True, False)
                last = mm(dst, ones[0:1, :], dw2[0:1, C * b:C * b + C], False, True)
                if t % 8 == 7:
                    last.then_inc(sim_mm, 1)
            pe.wait_ge(sim_sub, 2)
            for a in range(TB):
                last = pe.transpose(psum[0:B, 7, P * a:P * a + P], mx1[:, a:NT:TB], ident[:, :])
            last.then_inc(bt_tp, 1)
            for t in range(NT):
                pe.wait_ge(e1_norm, t // 8 + 1)
                last = pe.transpose(psum[0:C, 2 + t // 4, P * (t % 4):P * (t % 4) + P], e1n[:, t, :], ident[:, :])
                if t % 4 == 3:
                    last.then_inc(aT_tp, 1)
            pe.wait_ge(bt_norm, 1)
            for a in range(TB):
                last = pe.transpose(psum[:, 7, 256 + B * a:256 + B * a + B], btn[0:B, P * a:P * a + P], ident[0:B, 0:B])
            last.then_inc(btT_tp, 1)
            pe.wait_ge(btT_sb, 1)
            for b in range(B):
                for a in range(TB):
                    last = mm(psum[:, 7, 288 + b:289 + b], xn[:, TB * b + a, :], btT[:, a, b:b + 1], a == 0, a == TB - 1)
            last.then_inc(hc_mm, 1)
            pe.wait_ge(ctx_in, 16)
            for b in range(B):
                g = b // 2
                pe.wait_ge(aT_sb, g + 1)
                last = mm(psum[:, (6, 0, 1, 2)[g], N * (b % 2):N * (b % 2) + N], ctx_tok[0:C, b, :], aT[0:C, N * b:N * b + N])
                if b % 2:
                    last.then_inc(hq_mm, 1)
            pe.wait_ge(xc_done, 1)
            pe.wait_ge(aT_sb, 4)
            for t in range(NT):
                pe.wait_ge(xh_done, t // 4 + 1)
                if t >= 3:
                    pe.wait_ge(x_done, 2 * NT + t - 2)
                for k, feat in enumerate((xnT, hqT, xhT, xcT)):
                    last = mm(psum[:, 3 + t % 3, 0:D], feat[:, P * t:P * t + P], wqv[:, k, :], k == 0, k == 3)
                last.then_inc(qv_ready, 1)

            pe.wait_ge(x_done, 3 * NT)
            ln_transposes(3)
            for t in range(NT):
                pe.wait_ge(ln_xnT, 3 * NG + t // 4 + 1)
                last = mm(psum[:, t // 8, E1 * (t % 8):E1 * (t % 8) + E1], xnT[:, P * t:P * t + P], gw1[:, :])
                if t % 8 == 7:
                    last.then_inc(rl_mm, 1)
            def shared_gate_up(m):
                g, c = m // 2, m % 2
                if m >= 2:
                    pe.wait_ge(hs_done, m - 1)
                mm(psum[0:I1, 2 + c, :], sgT[:, I1 * c:I1 * c + I1], xnT[:, 512 * g:512 * g + 512])
                mm(psum[0:I1, 4 + c, :], suT[:, I1 * c:I1 * c + I1], xnT[:, 512 * g:512 * g + 512]).then_inc(sg_ready, 1)

            for g in range(NG):
                shared_gate_up(2 * g)
                shared_gate_up(2 * g + 1)
                pe.wait_ge(hs_done, 2 * g + 2)
                if g >= 2:
                    pe.wait_ge(osh_done, g - 1)
                for c in range(SH1):
                    last = mm(bank(6 + g % 2), sdT[:, c, :], h1[0:I1, c, :], c == 0, c == SH1 - 1)
                last.then_inc(sd_ready, 1)
            pe.wait_ge(rw_done, 1)
            for g in range(NG):
                if g >= 2:
                    pe.wait_ge(hs_done, 2 * NG)
                for j in range(4):
                    last = pe.transpose(psum[:, g, P * j:P * j + P], rwp[:, 4 * g + j].rearrange("p k e -> p (k e)"), ident[:, :])
                last.then_inc(rw_tp, 1)
            pe.wait_ge(rwr_lo, NG)
            pe.wait_ge(osh_done, NG)
            pe.wait_ge(xh_lo, 2)

            def product(dst, w, x):
                mm(dst, w(0), x(0), True, False)
                mm(dst, w(0), x(1), False, False)
                return mm(dst, w(1), x(0), False, True)

            def gate_up1(n, k, slot, hf):
                tok = slice(512 * k, 512 * k + 512)
                if later(n, 2):
                    pe.wait_ge(nl_done, n - 1)
                product(bank(k), lambda h: wgu[:, slot, h, 0:P], lambda h: xh[:, h, tok]).then_inc(gate_ready, 1)
                if later(n, 2):
                    pe.wait_ge(hid_done, n - 1)
                product(bank(2 + k), lambda h: wgu[:, slot, h, P:2 * P], lambda h: xh[:, h, tok])
                mm(bank(4 + k), selr[:, slot, :], rwr[:, 1024 * hf + 512 * k:1024 * hf + 512 * k + 512]).then_inc(up_ready, 1)

            def down1(n, k, slot, start=False, stop=False):
                pe.wait_ge(hh_lo, n + 1)
                mm(bank(6 + k), wdn[:, slot, 0, :], hh[:, k, 0, :], start, False)
                mm(bank(6 + k), wdn[:, slot, 0, :], hh[:, k, 1, :], False, False)
                mm(bank(6 + k), wdn[:, slot, 1, :], hh[:, k, 0, :], False, stop).then_inc(down_done, 1)

            def chunk_pair1(i, hf, first=False):
                for slot in range(2):
                    pe.wait_ge(wgu_lo, i * 2 + (slot + 1))
                    for k in range(2):
                        if first and hf and slot == 0:
                            pe.wait_ge(xh_lo, 2 + k + 1)
                        gate_up1(i * 4 + (2 * slot + k), k, slot, hf)
                        if later(i, 1) or slot:
                            if k == 0:
                                pe.wait_ge(wdn_lo, i * 2 + slot)
                            if first and hf and slot:
                                pe.wait_ge(o1_done, k + 1)
                            down1(i * 4 + (2 * slot + k - 2), k, 1 - slot, first and slot == 1, first and slot == 0)

            for hf in range(2):
                chunk_pair1(NC1 // 2 * hf, hf, True)
                with pe.Fori(NC1 // 2 * hf + 1, NC1 // 2 * (hf + 1)) as i:
                    chunk_pair1(i, hf)
            pe.wait_ge(wdn_lo, 2 * NC1)
            for k in range(2):
                down1(4 * NC1 - 2 + k, k, 1, False, True)
            pe.wait_ge(o1_done, 4)
            for t in range(NT):
                if t >= 4:
                    pe.wait_ge(x_done, 3 * NT + t - 3)
                pe.transpose(psum[:, t % 4, 0:D], osh[:, P * t:P * t + P], ident[:, :]).then_inc(ffn_tp, 1)

            def project(L, wq_, wk_, wv_):
                mm(bank(0), wk_[:, :], ctxT[:, :]).then_inc(qk2_mm, 1)
                for b in range(B):
                    last = mm(psum[0:C, 6 + b // 4, D * (b % 4):D * (b % 4) + D], ctxT[:, C * b:C * b + C], wv_[:, :])
                last.then_inc(v2_mm, 1)
                ln_transposes(L)
                for g in range(NG):
                    pe.wait_ge(ln_xnT, NG * L + g + 1)
                    mm(bank(2 + g), wq_[:, :], xnT[:, 512 * g:512 * g + 512]).then_inc(qk2_mm, 1)

            def scores(base):
                pe.wait_ge(v2_sb, base // 2 + 1)
                for t in range(NT):
                    b = t // TB
                    pe.wait_ge(qk2_sb, 5 * base // 2 + t // 4 + 2)
                    last = mm(psum[:, t // 8, C * (t % 8):C * (t % 8) + C], q2T[:, P * t:P * t + P], k2T[:, C * b:C * b + C])
                    if t % 8 == 7:
                        last.then_inc(sim_mm, 1)
                pe.wait_ge(qk2_sb, 5 * base // 2 + 5)
                for t in range(NT):
                    pe.wait_ge(sim_exp, base + t // 8 + 3)
                    last = pe.transpose(psum[0:C, 2 + t // 4, P * (t % 4):P * (t % 4) + P], e2[:, t, :], ident[:, :])
                    if t % 4 == 3:
                        last.then_inc(e2_tp, 1)

            pe.wait_ge(x_done, 4 * NT)
            project(4, wq2, wk2, wv2)
            scores(0)
            for t in range(NT):
                b = t // TB
                pe.wait_ge(e2_sb, t // 4 + 1)
                if t >= 4:
                    pe.wait_ge(x_done, 4 * NT + t - 3)
                mm(psum[:, (6, 7, 0, 1)[t % 4], 0:D], e2T[0:C, P * t:P * t + P], v2[0:C, b, :]).then_inc(av2_ready, 1)

            pe.wait_ge(x_done, 5 * NT)
            ln_transposes(5)
            for t in range(NT):
                pe.wait_ge(ln_xnT, 5 * NG + t // 4 + 1)
                last = mm(psum[:, 0, E2 * t:E2 * t + E2], xnT[:, P * t:P * t + P], rw2[:, :])
            last.then_inc(rl_mm, 1)
            pe.wait_ge(rw_done, 2)
            for q in range(2):
                half = psum[:, 1 + q, :].bitcast(BF16)
                for j in range(8):
                    last = pe.transpose(half[:, P * j:P * j + P], cpk[:, 8 * q + j, :], identb[:, :])
                last.then_inc(rw_tp, 1)
            pe.wait_ge(rw_sb, 2)

            pe.wait_ge(xh_lo, 6)

            def up2(n, local, k, slot, hf):
                tok = slice(512 * k, 512 * k + 512)
                pe.wait_ge(prod_done, n - 1)
                product(bank(k), lambda h: wgu[:, slot, h, 0:P], lambda h: xh[:, h, tok])
                mm(bank(2 + k), sel2[:, bass.ds(local, 1), :].rearrange("p a n -> p (a n)"),
                   cT[:, 1024 * hf + 512 * k:1024 * hf + 512 * k + 512]).then_inc(up_ready, 1)

            def down2(n, k, slot, hf, start=False, stop=False):
                pe.wait_ge(hh_lo, n + 1)
                acc = bank(4 + 2 * hf + k)
                mm(acc, wdn[:, slot, 0, :], hh[:, k, 0, :], start, False)
                mm(acc, wdn[:, slot, 0, :], hh[:, k, 1, :], False, False)
                mm(acc, wdn[:, slot, 1, :], hh[:, k, 0, :], False, stop).then_inc(down_done, 1)

            def chunk_pair2(i, hf, first=False):
                for slot in range(2):
                    pe.wait_ge(wgu_lo, i * 2 + (slot + 1))
                    for k in range(2):
                        if first and hf and slot == 0:
                            pe.wait_ge(xh_lo, 6 + k + 1)
                        up2(i * 4 + (2 * slot + k), i * 2 + (slot - 2 * NC1 - NC2 * hf), k, slot, hf)
                        if not (first and hf == 0 and slot == 0):
                            if k == 0:
                                pe.wait_ge(wdn_lo, i * 2 + slot)
                            ends = first and slot == 0
                            down2(i * 4 + (2 * slot + k - 2), k, 1 - slot, hf - ends, first and slot == 1, ends)

            for hf in range(2):
                start = NC1 + NC2 // 2 * hf
                chunk_pair2(start, hf, True)
                with pe.Fori(start + 1, start + NC2 // 2) as i:
                    chunk_pair2(i, hf)
            pe.wait_ge(wdn_lo, 2 * (NC1 + NC2))
            for k in range(2):
                down2(4 * (NC1 + NC2) - 2 + k, k, 1, 1, False, True)
            for t in range(NT):
                pe.wait_ge(o2_sb, t // 4 + 1)
                if t >= 4:
                    pe.wait_ge(x_done, 5 * NT + t - 3)
                pe.transpose(psum[:, t % 4, 0:D], o2T[:, P * t:P * t + P], ident[:, :]).then_inc(ffn_tp, 1)

            pe.wait_ge(x_done, 6 * NT)
            project(6, wq3, wk3, wv3)
            scores(2)
            for b in range(B):
                g = b // 2
                pe.wait_ge(e2_sb, NG + max(g, 2) + 1 if g >= 2 else NG + g + 1)
                if g >= 2:
                    pe.wait_ge(e2_sb, 2 * NG)
                last = mm(psum[:, (0, 1, 2, 3)[g], N * (b % 2):N * (b % 2) + N], v2[0:C, b, :], e2T[0:C, N * b:N * b + N])
                if b % 2:
                    last.then_inc(c3_mm, 1)
            for t in range(NT):
                pe.wait_ge(c3_sb, t // 4 + 1)
                if t >= 4:
                    pe.wait_ge(x_done, 6 * NT + t - 3)
                mm(psum[:, 4 + t % 4, 0:D], c3T[:, P * t:P * t + P], wo3[:, :]).then_inc(av2_ready, 1)

            pe.wait_ge(x_done, 7 * NT)
            pe.wait_ge(wsum_done, 1)
            mm(psum[:, 7, 0:2], ones[:, :], wsum).then_inc(wsum_mm, 1)
            pe.wait_ge(rs3_done, 1)
            for t in range(NT):
                last = mm(psum[:, 2 + t // 4, P * (t % 4):P * (t % 4) + P], wide(rs3[:, t:t + 1], P), ident[:, :])
                if t % 4 == 3:
                    last.then_inc(rsB_mm, 1)
            pe.wait_ge(xi_done, 1)
            for g in range(2):
                half = psum[:, g, :].bitcast(BF16)
                for j in range(8):
                    last = pe.transpose(half[:, P * j:P * j + P], xi[:, 8 * g + j, :], identb[:, :])
                last.then_inc(xi_tp, 1)
            pe.wait_ge(wq_done, 1)
            pe.wait_ge(rsB_sb, NG)
            for n in range(NC3 * NG):
                c, g = n // NG, n % NG
                pe.wait_ge(xi_sb, g // 2 + 1 if n >= 2 else 2)
                if n >= 8:
                    pe.wait_ge(hpad_done, n - 7)
                mm(bank(n % 8), w1q[:, P * c:P * c + P], xiT[:, 512 * g:512 * g + 512]).then_inc(l1_ready, 1)
            pe.wait_ge(hpad_done, NC3 * NG)
            pe.wait_ge(g3_done, NC3)

            def hidden_T(t):
                if t >= 4:
                    pe.wait_ge(ga_done, t - 3)
                for c in range(NC3):
                    last = pe.transpose(psum[:, t % 4, P * c:P * c + P], g3[:, c, P * t:P * t + P], ident[:, :])
                last.then_inc(g3_tp, 1)

            hidden_T(0)
            hidden_T(1)
            for t in range(NT + 1):
                if t + 2 < NT:
                    hidden_T(t + 2)
                if t < NT:
                    pe.wait_ge(gi_done, t + 1)
                    if t >= 2:
                        pe.wait_ge(gi_sb, t - 1)
                    half = psum[:, 4 + t % 2, 0:NC3 * P // 2].bitcast(BF16)
                    for c in range(NC3):
                        last = pe.transpose(half[:, P * c:P * c + P], gi[:, t % 2, P * c:P * c + P], identb[:, :])
                    last.then_inc(gi_tp, 1)
                if t >= 1:
                    pe.wait_ge(gi_sb, t)
                    if t >= 3:
                        pe.wait_ge(x_done, 7 * NT + t - 2)
                    for c in range(NC3):
                        last = mm(psum[:, 6 + (t - 1) % 2, 0:D], giT[:, (t - 1) % 2, c, :], w2q[:, c, :], c == 0, c == NC3 - 1)
                    last.then_inc(l2_ready, 1)


def kernel(**inputs):
    import numpy as np
    import concourse.bacc as _bacc
    from concourse import mybir as _mybir
    from concourse.bass_utils import run_bass_kernel_spmd as _run

    v = {k: np.asarray(a) for k, a in inputs.items()}

    def columns(a, n):
        return a.reshape(a.shape[0], n, P).transpose(2, 0, 1)

    ctx = v["ctx_1024"].reshape(B * C, D)
    ctxT = ctx.T
    conv = np.concatenate([v["L3_ffn_conv_w"].reshape(HID3, 3), v["L3_ffn_conv_b"].reshape(HID3, 1)], axis=1)
    w_sim = v["L1_xattn_w_sim"].reshape(3, D)
    cols = np.concatenate([
        np.stack([v["L0_ffn_norm_g"], v["L0_ffn_norm_b"], v["L0_ffn_slot_g"], v["L0_ffn_slot_b"], w_sim[0], w_sim[1], w_sim[2],
                  v["L2_xattn_Wq_b"], v["L2_xattn_Wk_b"], v["L3_xattn_bq"]], axis=1),
        conv.reshape(NC3, P, 4).transpose(1, 0, 2).reshape(P, 4 * NC3)], axis=1)
    egu = np.concatenate([v["L0_ffn_Wg"], v["L0_ffn_Wu"], v["L0_ffn_bg"].reshape(E0, 2, P).transpose(0, 2, 1),
                          v["L0_ffn_bu"].reshape(E0, 2, P).transpose(0, 2, 1)], axis=2)
    edn = np.concatenate([v["L0_ffn_Wd"].reshape(E0, 2, P, D).transpose(0, 2, 1, 3).reshape(E0, P, 2 * D),
                          v["L0_ffn_bd"].reshape(E0, P, 1)], axis=2)
    w1 = np.concatenate([
        v["L1_ffn_Wg"].reshape(NC1, P, D).transpose(0, 2, 1), v["L1_ffn_Wu"].reshape(NC1, P, D).transpose(0, 2, 1),
        v["L1_ffn_Wd"].transpose(0, 2, 1).reshape(NC1, P, D)], axis=2)
    w2 = np.concatenate([v["L2_ffn_w1"].reshape(D, NC2, P).transpose(1, 0, 2), v["L2_ffn_w2"].reshape(NC2, P, D)], axis=2)
    laid = {
        "x": v["x"].reshape(T, D),
        "ctx": ctx,
        "ctxT": ctxT,
        "ctxTd": np.repeat(ctxT.reshape(D, B, 1, C), 2, axis=2).reshape(D, B * 2 * C),
        "cols": cols,
        "rows": np.stack([v["L1_xattn_b_qv"], v["L2_xattn_Wv_b"], v["L3_xattn_bv"], v["L3_xattn_bo"]]),
        "scal": np.concatenate([v["L0_ffn_scale"], v["L1_xattn_b_sim"]]),
        "gbias": v["L1_ffn_gate_bias"],
        "wq0": v["L0_xattn_Wq"],
        "wk0": np.tile(v["L0_xattn_Wkv"][:, 0:HD], (1, H0)),
        "wv0": v["L0_xattn_Wkv"][:, HD:2 * HD],
        "wo0": v["L0_xattn_Wo"],
        "slots": v["L0_ffn_slot_embeds"].reshape(ES, D),
        "egu": egu,
        "edn": edn,
        "w1": w1,
        "w2": w2,
        "wqv": v["L1_xattn_W_qv"].reshape(4, P, D).transpose(1, 0, 2),
        "gw1": v["L1_ffn_gate_w"].T,
        "sgT": v["L1_ffn_Sg"].T,
        "suT": v["L1_ffn_Su"].T,
        "sdT": v["L1_ffn_Sd"].T.reshape(SH1, I1, D).transpose(1, 0, 2),
        "wq2": v["L2_xattn_Wq_w"].T,
        "wk2": v["L2_xattn_Wk_w"].T,
        "wv2": v["L2_xattn_Wv_w"].T,
        "rw2": v["L2_ffn_router_w"].T,
        "wq3": v["L3_xattn_Wq"].T,
        "wk3": v["L3_xattn_Wk"].T,
        "wv3": v["L3_xattn_Wv"].T,
        "wo3": v["L3_xattn_Wo"].T,
        "w1f": v["L3_ffn_w1"].T,
        "w2f": v["L3_ffn_w2"].T.reshape(NC3, P, D).transpose(1, 0, 2),
    }
    nc = _bacc.Bacc("TRN2", target_bir_lowering=False, num_devices=1)
    arrays, args = {}, {}
    for name, a in laid.items():
        a = np.ascontiguousarray(a)
        arrays[f"in_{name}"] = a
        args[name] = nc.dram_tensor(f"in_{name}", a.shape, _mybir.dt.from_np(a.dtype), kind="ExternalInput").ap()
    out = nc.dram_tensor("out", (T, D), F32, kind="ExternalOutput").ap()
    build_program(nc, args, out)
    r = _run(nc, [arrays], core_ids=[0])
    return r.results[0]["out"].reshape(B, N, D)
```

```python
from contextlib import ExitStack

import concourse.bass as bass
from concourse import mybir

ALU = mybir.AluOpType
ACT = mybir.ActivationFunctionType
AX = mybir.AxisListType
F32 = mybir.dt.float32
BF16 = mybir.dt.bfloat16
F32R = mybir.dt.float32r

P = 128
B, N, D = 8, 256, 128
C = 64
T = B * N
NT = T // P
TB = N // P
NG = NT // 4
H0, HD = 16, D // 16
E0, S0, F0 = 16, 64, 256
ES = E0 * S0
NC0 = ES // P
E1, I1 = 64, 88
NC1 = E1 * I1 // P
G1 = 8
SH1 = 2
E2 = 8
W2 = 4 * 128 + 4 * 256
NC2 = W2 // P
HID3 = 512
NC3 = HID3 // P
EPS = 1e-5
MAGIC = 1.5 * 2.0 ** 23
LAYERS = 8

COLS = ["norm_g", "norm_b", "slot_g", "slot_b", "w_sim1", "w_sim2", "w_sim3", "q2_b", "k2_b", "q3_b"]
COL = {name: k for k, name in enumerate(COLS)}
CONV = len(COLS)
NCOL = CONV + 4 * NC3
ROWS = ["qv1_b", "v2_b", "v3_b", "o3_b"]
ROW = {name: k for k, name in enumerate(ROWS)}
STEPS0 = 2 * E0


def build_program(nc, A, out):
    with ExitStack() as ctx:
        def sb(name, shape, dt=F32):
            return ctx.enter_context(nc.sbuf_tensor(name, shape, dt))

        def sem(name):
            return ctx.enter_context(nc.semaphore(name))

        psum = ctx.enter_context(nc.psum_tensor("psum", [P, 8, 512], F32))

        X = sb("X", [P, NT, D])
        xn = sb("xn", [P, NT, D])
        xnT = sb("xnT", [P, T])
        ctxT = sb("ctxT", [P, B * C])
        ident = sb("ident", [P, P])
        identb = sb("identb", [P, P], BF16)
        ones = sb("ones", [P, P])
        cols = sb("cols", [P, NCOL])
        rows = sb("rows", [P, len(ROWS), D])
        scal = sb("scal", [P, 2])
        stats = sb("stats", [P, NT, 6])
        mv = sb("mv", [P, NT, 2])
        veps = sb("veps", [P, NT])
        rstd = sb("rstd", [P, NT])
        rtmp = sb("rtmp", [P, NT])
        neghalf = sb("neghalf", [P, NT])
        unused = sb("unused", [P, 1])
        epst = sb("epst", [P, NT])
        wq0 = sb("wq0", [P, D])
        wk0 = sb("wk0", [P, D])
        wv0 = sb("wv0", [P, HD])
        wo0 = sb("wo0", [P, D])
        headmask = sb("headmask", [P, H0])
        seT = sb("seT", [P, ES])
        w1f = seT[:, 0:HID3]
        w2f = seT[:, HID3:2 * HID3].rearrange("p (c o) -> p c o", c=NC3)
        slot_gs = sb("slot_gs", [P, 2])
        egu = sb("egu", [P, 2, 2 * F0])
        edn = sb("edn", [P, 2, F0])
        ebias = sb("ebias", [P, E0, 5])
        wqv = sb("wqv", [P, 4, D])
        gw1 = sb("gw1", [P, E1])
        gbias = sb("gbias", [P, E1])
        sgT = sb("sgT", [P, SH1 * I1])
        suT = sb("suT", [P, SH1 * I1])
        sdT = sb("sdT", [I1, SH1, D])
        w1gu = sb("w1gu", [P, 2, 2 * P])
        w1dn = sb("w1dn", [P, 2, P])
        wq2 = sb("wq2", [P, D])
        wk2 = sb("wk2", [P, D])
        wv2 = sb("wv2", [P, D])
        rw2 = sb("rw2", [P, E2])
        wq3 = sb("wq3", [P, D])
        wk3 = sb("wk3", [P, D])
        wv3 = sb("wv3", [P, D])
        wo3 = sb("wo3", [P, D])
        ltmask = sb("ltmask", [P, 8, 8])
        xh = sb("xh", [P, 2, T // 2], F32R)
        xh2 = sb("xh2", [P, 2, 512], F32R)
        wgu = sb("wgu", [P, 2, 2, 2 * P], F32R)
        wdn = sb("wdn", [P, 2, 2, P], F32R)
        hh = sb("hh", [P, 2, 2, 512], F32R)
        selr = sb("selr", [P, 2, P], F32R)
        rwr = sb("rwr", [P, T], F32R)

        ARENA = 29900
        arena = sb("arena", [P, ARENA])
        taken = [0]

        def carve(*shape, dt=F32):
            n = 1
            for k in shape:
                n *= k
            words = n if dt == F32 else (n + 1) // 2
            v = arena[:, taken[0]:taken[0] + words]
            taken[0] += words
            assert taken[0] <= ARENA, taken[0]
            if dt != F32:
                v = v.bitcast(dt)
            if len(shape) == 2:
                v = v.rearrange("p (a b) -> p a b", a=shape[0])
            elif len(shape) == 3:
                v = v.rearrange("p (a b c) -> p a b c", a=shape[0], b=shape[1])
            elif len(shape) == 4:
                v = v.rearrange("p (a b c d) -> p a b c d", a=shape[0], b=shape[1], c=shape[2])
            return v

        def bank(k):
            return psum[:, k, :]

        kbd = carve(B, H0, C)
        qT = carve(T)
        simS = carve(2, H0, C)
        simE = carve(2, H0 * C)
        simET = carve(2, H0 * C)
        krep = carve(B * C)
        vaug = carve(B, 2, HD + 1)
        y0 = carve(2, H0, HD)
        y0T = carve(2, P)
        mx0 = carve(2, H0)
        rden0 = carve(2, H0)
        ctxTd = carve(B * 2 * C)
        slot_raw = carve(ES // P, D)
        slot_n = carve(ES // P, D)
        smv = carve(ES // P, 2)
        sstats = carve(ES // P, 6)
        srstd = carve(3, ES // P)
        taken[0] = 0
        PT = carve(NC0, T)
        slotsT = carve(E0, B, S0)
        eo = slotsT.rearrange("p e b s -> p (e b s)").rearrange("p (c b o) -> p c b o", b=B, c=NC0)
        nmA = carve(NT)
        rsumA = carve(NT)
        rinvA = carve(NT)
        at_experts = taken[0]
        qb = carve(2, 2, N)
        qt = carve(TB, ES)
        pbuf = carve(2, ES)
        nmB = carve(2, 2)
        sumB = carve(2, 2)
        recB = carve(2, 2)
        taken[0] = at_experts
        eoT = carve(B, 2, S0)
        gel = carve(2, 512)
        h0 = carve(2, 512)
        taken[0] = 0
        cw = carve(B * C)
        dw2T = carve(B // 2)
        simT = carve(B // 2, N)
        mx1 = carve(NT)
        mx1b = carve(NT)
        s1 = carve(NT, C)
        e1 = carve(NT, C)
        e1n = carve(NT, C)
        den1 = carve(NT)
        rden1 = carve(NT)
        aT = carve(B // 2, N)
        hqT = carve(T)
        xhT = carve(T)
        xcT = carve(T)
        bt = carve(N)
        btn = carve(N)
        bsm = carve(4)
        btT = carve(B * (2 * B + 1))
        hc = carve(D)
        hcT = carve(B)
        ctx_tok = carve(B // 2, D)
        sel1 = carve(NC1 * P, dt=BF16)
        sc1 = carve(NT, E1)
        sfc = carve(NT, E1)
        t1 = carve(NT, E1)
        t2 = carve(NT, E1)
        t3 = carve(NT, E1)
        gs = carve(NT, G1)
        rank = carve(NT, G1)
        top8 = carve(NT, 8)
        rsum1 = carve(2, NT)
        rwp = carve(NT, 2, E1)
        osh = carve(T)
        sil = carve(2, 512)
        u1 = carve(2, 512)
        h1 = carve(2, 512)
        taken[0] = 0
        q2T = carve(T)
        k2T = carve(B * C)
        v2 = carve(B, D)
        s2 = carve(NT, C)
        e2 = carve(NT, C)
        mx2 = carve(NT)
        den2 = carve(NT)
        rden2 = carve(NT)
        e2T = carve(T)
        c3T = carve(T)
        xtmp = carve(2, D)
        taken[0] = 0
        pr2 = carve(NT, E2)
        g2a = carve(NT, 8, 8)
        g2b = carve(NT, 8, 8)
        rank2 = carve(NT, 8)
        rs2 = carve(2, NT)
        cpk = carve(NT, P, dt=BF16)
        cT = carve(T, dt=BF16)
        r2 = carve(2, 512)
        u2 = carve(2, 512)
        h2 = carve(2, 512)
        o2T = carve(T)
        taken[0] = 0
        am3 = carve(NT)
        qs3 = carve(NT)
        rs3 = carve(NT)
        qa = carve(NT, D)
        cwm = carve(NC3)
        taken[0] = max(taken[0], 9776)
        hpad = carve(4, 2, N + 2)
        yc = carve(4, 512)
        g3 = carve(NC3, T)
        am4 = carve(NT)
        qs4 = carve(NT)
        rs4 = carve(NT)
        ga = carve(2, 2, HID3)
        gi = carve(2, 2 * NC3, P, dt=BF16)
        giT = carve(2, 2 * NC3, P, dt=BF16)
        taken[0] = max(taken[0], 26000)
        sel2 = carve(NC2, P, dt=BF16)
        wa = carve(2, HID3)
        w1q = carve(HID3, dt=BF16)
        w2q = carve(NC3, D, dt=BF16)
        wsum = carve(2)
        wm = carve(2)
        wr = carve(2)
        taken[0] = 12000
        w2all = carve(NC2 + 1, 2 * P)

        x_in = [sem(f"x_in{g}") for g in range(NG)]
        w_l0 = sem("w_l0")
        w_slots = sem("w_slots")
        w_rest = sem("w_rest")
        ctx_in = sem("ctx_in")
        egu_in = [sem(f"egu_in{k}") for k in range(2)]
        edn_in = [sem(f"edn_in{k}") for k in range(2)]
        w1gu_in = [sem(f"w1gu_in{k}") for k in range(2)]
        w1dn_in = [sem(f"w1dn_in{k}") for k in range(2)]
        w2_in = sem("w2_in")
        out_done = sem("out_done")
        consts = sem("consts")
        pool_step = sem("pool_step")
        dve_step = sem("dve_step")
        act_step = sem("act_step")
        xh_hi = sem("xh_hi")
        xh_lo = sem("xh_lo")
        wgu_hi = sem("wgu_hi")
        wgu_lo = sem("wgu_lo")
        wdn_hi = sem("wdn_hi")
        wdn_lo = sem("wdn_lo")
        hh_hi = sem("hh_hi")
        hh_lo = sem("hh_lo")
        hh_lo2 = sem("hh_lo2")
        rwr_hi = sem("rwr_hi")
        rwr_lo = sem("rwr_lo")
        x_done = sem("x_done")
        ln_var = sem("ln_var")
        ln_rstd = sem("ln_rstd")
        ln_xn = sem("ln_xn")
        ln_tp = sem("ln_tp")
        ln_xnT = sem("ln_xnT")
        se_var = sem("se_var")
        se_rstd = sem("se_rstd")
        se_n = sem("se_n")
        se_tp = sem("se_tp")
        se_T = sem("se_T")
        kv_mm = sem("kv_mm")
        krep_done = sem("krep_done")
        vaug_done = sem("vaug_done")
        kbd_done = [sem("kbd_even"), sem("kbd_odd")]
        q_mm = sem("q_mm")
        q_sb = sem("q_sb")
        sim_ready = sem("sim_ready")
        sim_used = sem("sim_used")
        exp_done = sem("exp_done")
        et_ready = sem("et_ready")
        et_sb = sem("et_sb")
        av_ready = sem("av_ready")
        y_ready = sem("y_ready")
        yT_ready = sem("yT_ready")
        yT_sb = sem("yT_sb")
        out_ready = sem("out_ready")
        bl_ready = sem("bl_ready")
        bmax_done = sem("bmax_done")
        bexp_done = sem("bexp_done")
        brec_done = sem("brec_done")
        bnorm_done = sem("bnorm_done")
        bT_ready = sem("bT_ready")
        qt_sb = sem("qt_sb")
        al_ready = sem("al_ready")
        amax_done = sem("amax_done")
        aexp_done = sem("aexp_done")
        pT_ready = sem("pT_ready")
        pt_sb = sem("pt_sb")
        slots_mm = sem("slots_mm")
        slots_sb = sem("slots_sb")
        eg_ready = sem("eg_ready")
        eu_ready = sem("eu_ready")
        gelu_done = sem("gelu_done")
        h0_done = sem("h0_done")
        ed_ready = sem("ed_ready")
        eo_sb = sem("eo_sb")
        eoT_tp = [sem("eoT_tp_low"), sem("eoT_tp_high")]
        eo_tok = [sem("eo_tok_act"), sem("eo_tok_dve")]
        comb_ready = sem("comb_ready")
        cw_done = sem("cw_done")
        simT_mm = sem("simT_mm")
        simT_sb = sem("simT_sb")
        sim_mm = sem("sim_mm")
        sim_sub = sem("sim_sub")
        sim_exp = sem("sim_exp")
        e1_norm = sem("e1_norm")
        aT_tp = sem("aT_tp")
        aT_sb = sem("aT_sb")
        hq_mm = sem("hq_mm")
        hq_sb = sem("hq_sb")
        xh_done = sem("xh_done")
        bt_tp = sem("bt_tp")
        bt_max = sem("bt_max")
        bt_exp = sem("bt_exp")
        bt_norm = sem("bt_norm")
        btT_sb = sem("btT_sb")
        hc_mm = sem("hc_mm")
        hc_sb = sem("hc_sb")
        xc_done = sem("xc_done")
        xbias_done = sem("xbias_done")
        qv_ready = sem("qv_ready")
        rl_mm = sem("rl_mm")
        rl_sig = sem("rl_sig")
        rw_done = sem("rw_done")
        rw_tp = sem("rw_tp")
        rw_sb = sem("rw_sb")
        sg_ready = sem("sg_ready")
        sil_s = sem("sil_s")
        hs_done = sem("hs_done")
        sd_ready = sem("sd_ready")
        osh_done = sem("osh_done")
        pool_made = sem("pool_made")
        gate_ready = sem("gate_ready")
        up_ready = sem("up_ready")
        nl_done = sem("nl_done")
        prod_done = sem("prod_done")
        hid_done = sem("hid_done")
        down_done = sem("down_done")
        o1_done = sem("o1_done")
        ffn_tp = sem("ffn_tp")
        qk2_mm = sem("qk2_mm")
        qk2_sb = sem("qk2_sb")
        v2_mm = sem("v2_mm")
        v2_sb = sem("v2_sb")
        rden2_done = sem("rden2_done")
        e2_tp = sem("e2_tp")
        e2_sb = sem("e2_sb")
        av2_ready = sem("av2_ready")
        c3_mm = sem("c3_mm")
        c3_sb = sem("c3_sb")
        o2_sb = sem("o2_sb")
        wsum_done = sem("wsum_done")
        wsum_mm = sem("wsum_mm")
        wq_done = sem("wq_done")
        qi_done = sem("qi_done")
        xq_done = sem("xq_done")
        xq_tp = sem("xq_tp")
        xq_hi = sem("xq_hi")
        xq_lo = sem("xq_lo")
        l1_ready = sem("l1_ready")
        hpad_done = sem("hpad_done")
        conv_done = sem("conv_done")
        g3_done = sem("g3_done")
        g3_tp = sem("g3_tp")
        qs4_done = sem("qs4_done")
        ga_done = sem("ga_done")
        gi_done = sem("gi_done")
        gi_tp = sem("gi_tp")
        gi_sb = sem("gi_sb")
        l2_ready = sem("l2_ready")

        block = ctx.enter_context(nc.Block())

        def wide(ap, *shape):
            return ap.broadcast_to([P, *shape])

        def later(step, k):
            return not isinstance(step, int) or step >= k

        def applied_behind(L, g):
            return (L == 5 and g < NG - 1) or (L in (4, 6) and g < 2)

        HQ_BANKS = (6, 0, 1, 2)

        def hq_part(ap, g):
            return ap.rearrange("p (i q r n) -> p i r q n", i=2, q=2, r=2)[:, g // 2, g % 2]

        LOW2 = 384

        def norm_half(hf, k, half):
            return xh2[:, half, :] if hf and k == 0 else xh[:, half, 512 * (k - hf):512 * (k - hf) + 512]

        def egu_part(k, f):
            return egu[:, k, :].rearrange("p (w f n) -> p f w n", w=2, f=2)[:, f]

        def wgu_pair(slot, half):
            return wgu[:, slot, half, :].rearrange("p (w n) -> p w n", w=2)

        LOW0 = 384

        def w2part(c, part):
            return w2all[:, bass.ds(c, 1), P * part:P * part + P].rearrange("p c n -> p (c n)")

        def hidden2_part(k, half):
            return hh[:, k, half, :] if k < 2 else rwr[:, 1024 * k - 2048 + 512 * half:1024 * k - 1536 + 512 * half]

        UNITS, PAIRS, TURNS3 = NC3 * NG, NT // 2, NT // 2 + 5
        xq_high = rwr[:, :]
        xq_low = xh[:, :, :].rearrange("p h n -> p (h n)")
        w1r = wgu[:, 0].rearrange("p h n -> p (h n)")

        N_L0, N_SLOTS = 5, 6
        REST = ["wqv", "gw1", "sgT", "suT", "sdT", "wq2", "wk2", "wv2", "rw2", "wq3", "wk3", "wv3", "wo3", "w1f", "w2f"]

        @block.sync
        def _(sp):
            xt = A["x"].rearrange("(t p) d -> p t d", p=P)
            for g in range(NG):
                sp.dma_start(X[:, 4 * g:4 * g + 4, :], xt[:, 4 * g:4 * g + 4, :]).then_inc(x_in[g], 16)
            for dst, src in ((ctxT[:, :], A["ctxT"]), (wk0[:, :], A["wk0"]), (ctxTd, A["ctxTd"]), (wv0[:, :], A["wv0"]),
                             (wq0[:, :], A["wq0"])):
                sp.dma_start(dst, src).then_inc(w_l0, 16)
            for dst, src in ((slot_raw, A["slots"].rearrange("(t p) d -> p t d", p=P)), (cols[:, :], A["cols"]),
                             (scal[:, :], A["scal"].partition_broadcast(P)), (wo0[:, :], A["wo0"]), (ebias[:, :, :], A["ebias"]),
                             (rows[:, :, :], A["rows"].partition_broadcast(P))):
                sp.dma_start(dst, src).then_inc(w_slots, 16)
            for k in range(2):
                sp.dma_start(egu[:, k, :], A["egu"][k, :, :]).then_inc(egu_in[k], 16)
                sp.dma_start(edn[:, k, :], A["edn"][k, :, :]).then_inc(edn_in[k], 16)
                sp.dma_start(w1gu[:, k, :], A["w1"][k, :, 0:2 * P]).then_inc(w1gu_in[k], 16)
                sp.dma_start(w1dn[:, k, :], A["w1"][k, :, 2 * P:3 * P]).then_inc(w1dn_in[k], 16)
            sp.dma_start(gbias[:, :], A["gbias"].partition_broadcast(P)).then_inc(w_rest, 16)
            for dst, name in ((wqv, "wqv"), (gw1, "gw1"), (sgT, "sgT"), (suT, "suT"), (sdT, "sdT"), (wq2, "wq2"), (wk2, "wk2"),
                              (wv2, "wv2"), (rw2, "rw2"), (wq3, "wq3"), (wk3, "wk3"), (wv3, "wv3"), (wo3, "wo3")):
                whole = dst[:, :, :] if len(A[name].shape) == 3 else dst[:, :]
                sp.dma_start(whole, A[name]).then_inc(w_rest, 16)
            def load_egu(e, k, free):
                sp.wait_ge(wgu_lo, free)
                sp.dma_start(egu[:, k, :], A["egu"][bass.ds(e, 1), :, :].rearrange("a p n -> (a p) n")).then_inc(egu_in[k], 16)

            def load_edn(e, k, free):
                sp.wait_ge(wdn_lo, free)
                sp.dma_start(edn[:, k, :], A["edn"][bass.ds(e, 1), :, :].rearrange("a p n -> (a p) n")).then_inc(edn_in[k], 16)

            load_egu(2, 0, 2)
            load_egu(3, 1, 4)
            load_edn(2, 0, 2)
            sp.wait_ge(eg_ready, 1)
            sp.dma_start(w1f, A["w1f"]).then_inc(w_rest, 16)
            sp.dma_start(w2f, A["w2f"]).then_inc(w_rest, 16)
            with sp.Fori(1, E0 // 2 - 1) as i:
                load_egu(i * 2 + 2, 0, i * 4 + 2)
                load_edn(i * 2 + 1, 1, i * 4)
                load_egu(i * 2 + 3, 1, i * 4 + 4)
                load_edn(i * 2 + 2, 0, i * 4 + 2)
            load_edn(E0 - 1, 1, STEPS0 - 4)
            sp.wait_ge(x_done, 2 * NT)
            sp.dma_start(ctx_tok, A["ctx"].rearrange("(q p) d -> p q d", p=P)).then_inc(ctx_in, 16)
            def load_gu(c, k, free):
                sp.wait_ge(wgu_lo, free + STEPS0)
                sp.dma_start(w1gu[:, k, :], A["w1"][bass.ds(c, 1), :, 0:2 * P].rearrange("a p n -> (a p) n")).then_inc(w1gu_in[k], 16)

            def load_dn(c, k, free):
                sp.wait_ge(wdn_lo, free + STEPS0)
                sp.dma_start(w1dn[:, k, :], A["w1"][bass.ds(c, 1), :, 2 * P:3 * P].rearrange("a p n -> (a p) n")).then_inc(w1dn_in[k], 16)

            load_gu(2, 0, 1)
            load_gu(3, 1, 2)
            load_dn(2, 0, 1)
            with sp.Fori(1, NC1 // 2 - 1) as i:
                load_gu(i * 2 + 2, 0, i * 2 + 1)
                load_dn(i * 2 + 1, 1, i * 2)
                load_gu(i * 2 + 3, 1, i * 2 + 2)
                load_dn(i * 2 + 2, 0, i * 2 + 1)
            load_gu(0, 0, NC1 - 1)
            load_dn(NC1 - 1, 1, NC1 - 2)
            load_gu(1, 1, NC1)
            load_dn(0, 0, NC1 - 1)
            with sp.Fori(0, NC1 // 2 - 1) as i:
                load_gu(i * 2 + 2, 0, i * 2 + (NC1 + 1))
                load_dn(i * 2 + 1, 1, i * 2 + NC1)
                load_gu(i * 2 + 3, 1, i * 2 + (NC1 + 2))
                load_dn(i * 2 + 2, 0, i * 2 + (NC1 + 1))
            load_dn(NC1 - 1, 1, 2 * NC1 - 2)
            sp.wait_ge(x_done, 4 * NT)
            sp.dma_start(w2all[:, 0:NC2, :], A["w2"]).then_inc(w2_in, 16)
            sp.dma_start(w2all[:, NC2, :], A["w2"][:, 0, :]).then_inc(w2_in, 16)
            ot = out.rearrange("(t p) d -> p t d", p=P)
            for g in range(NG):
                sp.wait_ge(x_done, 7 * NT + 4 * g + 4)
                sp.dma_start(ot[:, 4 * g:4 * g + 4, :], X[:, 4 * g:4 * g + 4, :]).then_inc(out_done, 16)
            sp.wait_ge(out_done, 16 * NG)

        @block.gpsimd
        def _(pool):
            step = [0]

            def then(ins):
                step[0] += 1
                ins.then_inc(pool_step, 1)
                pool.wait_ge(pool_step, step[0])

            pool.memset(neghalf[:, :], -0.5)
            pool.memset(epst[:, :], EPS)
            pool.memset(ones[:, :], 1.0)
            then(pool.memset(ident[:, :], 0.0))
            then(pool.affine_select(out=ident[:, :], in_=ident[:, :], compare_op=ALU.not_equal, fill=1.0, base=0,
                                    pattern=[[-1, P]], channel_multiplier=1))
            pool.memset(headmask[:, :], 1.0)
            then(pool.memset(ltmask[:, :, :], 1.0))
            then(pool.affine_select(out=headmask[:, :], in_=headmask[:, :], compare_op=ALU.is_ge, fill=0.0, base=0,
                                    pattern=[[-HD, H0]], channel_multiplier=1))
            then(pool.affine_select(out=headmask[:, :], in_=headmask[:, :], compare_op=ALU.is_ge, fill=0.0, base=HD - 1,
                                    pattern=[[HD, H0]], channel_multiplier=-1))
            then(pool.affine_select(out=ltmask[:, :, :], in_=ltmask[:, :, :], compare_op=ALU.is_ge, fill=0.0, base=-1,
                                    pattern=[[1, 8], [-1, 8]], channel_multiplier=0))
            then(pool.memset(vaug, 0.0))
            pool.memset(vaug[0:C, :, 0, HD:HD + 1], 1.0)
            then(pool.memset(vaug[C:P, :, 1, HD:HD + 1], 1.0))
            pool.tensor_copy(identb[:, :], ident[:, :]).then_inc(consts, 1)

            def ln_power(L, g):
                s = slice(4 * g, 4 * g + 4)
                pool.wait_ge(ln_var, NG * L + g + 1)
                if L != 1:
                    pool.tensor_tensor(rstd[:, s], veps[:, s], neghalf[:, s], ALU.pow).then_inc(ln_rstd, 1)
                    if applied_behind(L, g):
                        pool.wait_ge(ln_rstd, NG * L + g + 1)
                        if g >= 1 and not applied_behind(L, g - 1):
                            pool.wait_ge(ln_xn, NG * L + g)
                        then(pool.tensor_tensor(xn[:, s, :], X[:, s, :], wide(mv[:, s, 0:1], 4, D), ALU.subtract))
                        pool.tensor_tensor(xn[:, s, :], xn[:, s, :], wide(rstd[:, s].unsqueeze(2), 4, D), ALU.mult).then_inc(ln_xn, 1)
                    return
                then(pool.tensor_tensor(rtmp[:, s], veps[:, s], neghalf[:, s], ALU.pow))
                then(pool.tensor_tensor(rstd[:, s], rtmp[:, s], rtmp[:, s], ALU.mult))
                then(pool.tensor_tensor(rstd[:, s], rstd[:, s], mv[:, s, 1], ALU.mult))
                then(pool.tensor_tensor(rstd[:, s], rstd[:, s], epst[:, s], ALU.add))
                then(pool.tensor_tensor(rstd[:, s], rstd[:, s], neghalf[:, s], ALU.pow))
                pool.tensor_tensor(rstd[:, s], rstd[:, s], rtmp[:, s], ALU.mult).then_inc(ln_rstd, 1)

            def norm_low(layer, hf, k):
                pool.wait_ge(xh_hi, 4 * layer + 2 * hf + k + 1 + E0)
                r = slice(1024 * hf + 512 * k, 1024 * hf + 512 * k + 512)
                pool.tensor_tensor(norm_half(hf, k, 1), xnT[:, r], norm_half(hf, k, 0).bitcast(F32), ALU.subtract).then_inc(xh_lo, 1)

            def gate_up0_low(n, k, f):
                pool.wait_ge(wgu_hi, n + 1)
                pool.tensor_tensor(wgu_pair(f, 1), egu_part(k, f), wgu_pair(f, 0).bitcast(F32), ALU.subtract).then_inc(wgu_lo, 1)

            def hidden0_low(n, f):
                pool.wait_ge(hh_hi, n + 1)
                r = slice(0, LOW0)
                pool.tensor_tensor(hh[:, f, 1, r], h0[:, f, r], hh[:, f, 0, r].bitcast(F32), ALU.subtract).then_inc(hh_lo, 1)

            def experts0_low():
                gate_up0_low(0, 0, 0)

                def expert_pair(i, last=False):
                    for k in range(2):
                        for f in range(2):
                            n = i * 4 + (2 * k + f)
                            if not (last and k and f):
                                gate_up0_low(n + 1, k if f == 0 else 1 - k, 1 - f)
                            if later(i, 1) or k or f:
                                hidden0_low(n - 1, 1 - f)

                expert_pair(0)
                with pool.Fori(1, E0 // 2 - 1) as i:
                    expert_pair(i)
                expert_pair(E0 // 2 - 1, True)
                hidden0_low(STEPS0 - 1, 1)

            def gate_up1_low(c, slot):
                pool.wait_ge(wgu_hi, c + 1 + STEPS0)
                pool.tensor_tensor(wgu[:, slot, 1, :], w1gu[:, slot, :], wgu[:, slot, 0, :].bitcast(F32), ALU.subtract).then_inc(wgu_lo, 1)

            def down1_low(c, slot):
                pool.wait_ge(wdn_hi, c + 1 + STEPS0)
                pool.tensor_tensor(wdn[:, slot, 1, :], w1dn[:, slot, :], wdn[:, slot, 0, :].bitcast(F32), ALU.subtract).then_inc(wdn_lo, 1)

            def hidden1_low(n, k):
                pool.wait_ge(hh_hi, n + 1 + STEPS0)
                pool.tensor_tensor(hh[:, k, 1, :], h1[:, k, :], hh[:, k, 0, :].bitcast(F32), ALU.subtract).then_inc(hh_lo, 1)

            def experts1_low():
                norm_low(0, 1, 0)

                def chunk_pair(i, last=False):
                    for slot in range(2):
                        if later(i, 1) or slot:
                            hidden1_low(i * 4 + (2 * slot - 1), 1)
                        if not (last and slot):
                            gate_up1_low(i * 2 + (slot + 1), 1 - slot)
                        down1_low(i * 2 + slot, slot)
                        hidden1_low(i * 4 + 2 * slot, 0)

                chunk_pair(0)
                with pool.Fori(1, NC1 // 2) as i:
                    chunk_pair(i)
                norm_low(0, 1, 1)
                with pool.Fori(NC1 // 2, NC1 - 1) as i:
                    chunk_pair(i)
                chunk_pair(NC1 - 1, True)
                hidden1_low(4 * NC1 - 1, 1)

            def up2_low(c, slot, local):
                pool.wait_ge(wgu_hi, c + 1 + STEPS0)
                pool.tensor_tensor(wgu[:, slot, 1, 0:P], w2part(local, 0), wgu[:, slot, 0, 0:P].bitcast(F32), ALU.subtract).then_inc(wgu_lo, 1)

            def down2_low(c, slot, local):
                pool.wait_ge(wdn_hi, c + 1 + STEPS0)
                pool.tensor_tensor(wdn[:, slot, 1, :], w2part(local, 1), wdn[:, slot, 0, :].bitcast(F32), ALU.subtract).then_inc(wdn_lo, 1)

            def hidden2_low(n, k):
                pool.wait_ge(hh_hi, n + 1 + STEPS0)
                r = slice(0, LOW2)
                pool.tensor_tensor(hidden2_part(k, 1)[:, r], h2[:, k % 2, r], hidden2_part(k, 0)[:, r].bitcast(F32), ALU.subtract).then_inc(hh_lo, 1)

            def experts2_low():
                norm_low(1, 0, 0)
                norm_low(1, 0, 1)
                norm_low(1, 1, 0)
                up2_low(2 * NC1, 0, 0)

                def chunk_pair(i, hf, first=False, last=False, ends=False):
                    for slot in range(2):
                        if not (last and slot):
                            up2_low(i * 2 + (slot + 1), 1 - slot, i * 2 + (slot + 1 - 2 * NC1 - NC2 * hf))
                        if slot or not first:
                            hidden2_low(i * 4 + (2 * slot - 1), (2 * slot - 1) % 4)
                        down2_low(i * 2 + slot, slot, i * 2 + (slot - 2 * NC1 - NC2 * hf))
                        if ends and slot:
                            norm_low(1, 1, 1)
                        hidden2_low(i * 4 + 2 * slot, 2 * slot)

                chunk_pair(NC1, 0, first=True)
                with pool.Fori(NC1 + 1, NC1 + NC2 // 2 - 1) as i:
                    chunk_pair(i, 0)
                chunk_pair(NC1 + NC2 // 2 - 1, 0, ends=True)
                with pool.Fori(NC1 + NC2 // 2, NC1 + NC2 - 1) as i:
                    chunk_pair(i, 1)
                chunk_pair(NC1 + NC2 - 1, 1, last=True)
                hidden2_low(4 * (NC1 + NC2) - 1, 3)

            def quantised_norm():
                def scaled(g):
                    s = slice(4 * g, 4 * g + 4)
                    pool.wait_ge(qi_done, 2 * g + 1)
                    pool.tensor_tensor(qa[:, s, :], xn[:, s, :], wide(qs3[:, s].unsqueeze(2), 4, D), ALU.mult).then_inc(ln_rstd, 1)

                for g in range(NG):
                    s = slice(4 * g, 4 * g + 4)
                    pool.wait_ge(ln_var, NG * 7 + g + 1)
                    then(pool.tensor_tensor(rstd[:, s], veps[:, s], neghalf[:, s], ALU.pow))
                    then(pool.tensor_tensor(xn[:, s, :], X[:, s, :], wide(mv[:, s, 0:1], 4, D), ALU.subtract))
                    pool.tensor_tensor(xn[:, s, :], xn[:, s, :], wide(rstd[:, s].unsqueeze(2), 4, D), ALU.mult).then_inc(ln_xn, 1)
                    if g >= 1:
                        scaled(g - 1)
                scaled(NG - 1)

            for L in range(LAYERS):
                if L == 7:
                    pool.wait_ge(x_done, NT * 6)
                    pool.memset(hpad[:, :, :, 0:1], 0.0)
                    pool.memset(hpad[:, :, :, N + 1:N + 2], 0.0).then_inc(pool_made, 1)
                    quantised_norm()
                    continue
                for g in range(NG):
                    ln_power(L, g)
                if L == 0:
                    pool.wait_ge(krep_done, 1)
                    for b in range(1, B, 2):
                        pool.tensor_tensor(kbd[:, b], wide(krep[:, b * C:(b + 1) * C].unsqueeze(1), H0, C),
                                           wide(headmask[:, :].unsqueeze(2), H0, C), ALU.mult).then_inc(kbd_done[1], 1)
                    pool.wait_ge(se_var, 1)
                    pool.tensor_tensor(srstd[:, 1, :], srstd[:, 0, :], neghalf[:, 0:ES // P], ALU.pow).then_inc(se_rstd, 1)
                if L == 1:
                    for k in range(4 * B):
                        pool.wait_ge(brec_done, k + 1)
                        pool.tensor_tensor(qb[:, k % 2], qb[:, k % 2], wide(recB[:, k % 2].unsqueeze(2), 2, N), ALU.mult)\
                            .then_inc(bnorm_done, 1)
                    experts0_low()
                if L == 2:
                    pool.wait_ge(ln_xn, NG * L + NG)
                    pool.tensor_tensor(X[:, :, :], X[:, :, :], wide(rows[:, ROW["qv1_b"], :].unsqueeze(1), NT, D), ALU.add)\
                        .then_inc(xbias_done, 1)
                    then(pool.memset(sel1, 0.0))
                    per_expert = sel1.rearrange("p (e i) -> p e i", i=I1)
                    then(pool.affine_select(out=per_expert, in_=per_expert, compare_op=ALU.not_equal, fill=1.0, base=0,
                                            pattern=[[-1, E1], [0, I1]], channel_multiplier=1))
                    pool.affine_select(out=per_expert, in_=per_expert, compare_op=ALU.not_equal, fill=1.0, base=-E1,
                                       pattern=[[-1, E1], [0, I1]], channel_multiplier=1).then_inc(pool_made, 1)
                if L == 3:
                    for m in range(2 * NG):
                        pool.wait_ge(sil_s, m + 1)
                        if m >= 2:
                            pool.wait_ge(sd_ready, m // 2)
                        pool.tensor_tensor(h1[0:I1, m % 2, :], u1[0:I1, m % 2, :], sil[0:I1, m % 2, :], ALU.mult).then_inc(hs_done, 1)
                        if m in (1, 3):
                            norm_low(0, 0, m // 2)
                        if m == 5:
                            gate_up1_low(0, 0)
                    experts1_low()
                if L == 4:
                    pool.wait_ge(x_done, NT * L)
                    then(pool.memset(sel2, 0.0))
                    wide2 = sel2[:, 4:12, :].rearrange("p (e c) n -> p e (c n)", c=2)
                    for part in range(3):
                        then(pool.affine_select(out=sel2[:, 0:4, :], in_=sel2[:, 0:4, :], compare_op=ALU.not_equal, fill=1.0,
                                                base=-E2 * part, pattern=[[-1, 4], [0, P]], channel_multiplier=1))
                        last = pool.affine_select(out=wide2, in_=wide2, compare_op=ALU.not_equal, fill=1.0,
                                                  base=-E2 * part - 4, pattern=[[-1, 4], [0, 2 * P]], channel_multiplier=1)
                        if part < 2:
                            then(last)
                    last.then_inc(pool_made, 1)
                if L == 5:
                    pool.wait_ge(x_done, NT * L)
                    pool.memset(cpk, 0.0).then_inc(pool_made, 1)
                    experts2_low()
                if L == 6:
                    pool.wait_ge(ln_xn, NG * L + NG)
                    pool.tensor_tensor(X[:, :, :], X[:, :, :], wide(rows[:, ROW["o3_b"], :].unsqueeze(1), NT, D), ALU.add)\
                        .then_inc(xbias_done, 1)

        @block.scalar
        def _(act):
            def copy(dst, src):
                return act.activation(dst, src, ACT.Copy)

            def load_table(func):
                act.activation(unused[:, :], epst[:, 0:1], func)

            def ln_evac_group(L, g):
                act.wait_ge(ln_tp, NG * L + g + 1)
                dst = xnT[:, 512 * g:512 * g + 512]
                if L == 1:
                    ins = act.activation(dst, bank(6 + g % 2), ACT.Identity, scale=cols[:, COL["norm_g"]:COL["norm_g"] + 1],
                                         bias=cols[:, COL["norm_b"]:COL["norm_b"] + 1])
                else:
                    ins = copy(dst, bank(6 + g % 2))
                ins.then_inc(ln_xnT, 1)

            def ln_evac(L):
                for g in range(NG):
                    ln_evac_group(L, g)

            act.wait_ge(kv_mm, 1)
            copy(krep, bank(0)).then_inc(krep_done, 1)
            act.wait_ge(consts, 1)
            vps = psum[:, 1, 0:B * HD].rearrange("p (b d) -> p b d", b=B)
            copy(vaug[0:C, :, 0, 0:HD], vps[0:C])
            copy(vaug[C:P, :, 1, 0:HD], vps[C:P]).then_inc(vaug_done, 1)
            ln_evac(0)
            for g in range(NG):
                act.wait_ge(q_mm, g + 1)
                act.activation(qT[:, 512 * g:512 * g + 512], bank(2 + g), ACT.Copy, scale=float(HD) ** -0.5).then_inc(q_sb, 1)
            for t in range(NT + 3):
                if t >= 3:
                    u = t - 3
                    act.wait_ge(yT_ready, u + 1)
                    if u >= 2:
                        act.wait_ge(out_ready, u - 1)
                    copy(y0T[:, u % 2, :], psum[:, 7, 256:384]).then_inc(yT_sb, 1)
                if 1 <= t <= NT:
                    u = t - 1
                    act.wait_ge(et_ready, u + 1)
                    if u >= 2:
                        act.wait_ge(av_ready, u - 1)
                    copy(simET[:, u % 2, :], psum[:, 4:6, :].rearrange("p a n -> p (a n)")).then_inc(et_sb, 1)
                if t < NT:
                    act.wait_ge(sim_used, t + 1)
                    if t >= 2:
                        act.wait_ge(et_ready, t - 1)
                    act.activation(simE[:, t % 2, :], simS[:, t % 2].rearrange("p h k -> p (h k)"), ACT.Exp).then_inc(exp_done, 1)
                if t == NT:
                    act.wait_ge(se_n, 2)
                    for g in range(2):
                        act.wait_ge(se_tp, g + 1)
                        act.activation(seT[:, 512 * g:512 * g + 512], bank(g), ACT.Identity, scale=slot_gs[:, 0:1], bias=slot_gs[:, 1:2])\
                            .then_inc(se_T, 1)

            for g in range(NG - 1):
                ln_evac_group(1, g)
            act.wait_ge(x_done, NT)

            def bexp(k):
                act.wait_ge(bmax_done, k + 1)
                if k >= 2:
                    act.wait_ge(bT_ready, k - 1)
                for c in range(2):
                    last = act.activation(qb[:, k % 2, c, :], psum[:, k % 2, c * N:(c + 1) * N], ACT.Exp,
                                          bias=nmB[:, k % 2, c:c + 1], accum_out=sumB[:, k % 2, c:c + 1])
                last.then_inc(bexp_done, 1)

            def aexp(t):
                act.wait_ge(amax_done, t + 1)
                if t >= 2:
                    act.wait_ge(pT_ready, t - 1)
                act.activation(pbuf[:, t % 2, :], psum[:, 2:4, :].rearrange("p a n -> p (a n)"), ACT.Exp, bias=nmA[:, t:t + 1],
                               accum_out=rsumA[:, t:t + 1]).then_inc(aexp_done, 1)

            def pt_evac(t):
                act.wait_ge(pT_ready, t + 1)
                copy(PT[:, :, t * P:(t + 1) * P], psum[:, 4:6, :].rearrange("p a (c n) -> p (a c) n", c=4)).then_inc(pt_sb, 1)

            def slots_evac(b, hf):
                act.wait_ge(slots_mm, 2 * b + hf + 1)
                act.activation(slotsT[:, 8 * hf:8 * hf + 8, b, :], bank(6 + hf).rearrange("p (e s) -> p e s", s=S0), ACT.Identity,
                               scale=cols[:, COL["norm_g"]:COL["norm_g"] + 1], bias=cols[:, COL["norm_b"]:COL["norm_b"] + 1])\
                    .then_inc(slots_sb, 1)

            bexp(0)
            ln_evac_group(1, NG - 1)
            bexp(1)
            for q in range(4 * B + 2):
                if q % 2 == 0:
                    if q >= 2:
                        pt_evac(q // 2 - 1)
                    if q < 4 * B:
                        aexp(q // 2)
                if q + 2 < 4 * B:
                    bexp(q + 2)
                if q >= 4 and q % 4 == 1:
                    slots_evac(q // 4 - 1, 1)
                if q % 4 == 3:
                    slots_evac(q // 4, 0)

            def gate_up0_high(n, i, k, f):
                act.wait_ge(egu_in[k], i * 16 + 16)
                if later(n, 2):
                    act.wait_ge(eu_ready, n - 1)
                copy(wgu_pair(f, 0), egu_part(k, f)).then_inc(wgu_hi, 1)

            def hidden0_high(n, f):
                act.wait_ge(h0_done, n + 1)
                if later(n, 2):
                    act.wait_ge(ed_ready, n - 1)
                copy(hh[:, f, 0, :], h0[:, f, :]).then_inc(hh_hi, 1)

            def gelu(n, e, f):
                act.wait_ge(eg_ready, n + 1)
                if later(n, 2):
                    act.wait_ge(h0_done, n - 1)
                act.activation(gel[:, f, :], bank(f), ACT.Gelu, bias=ebias[:, bass.ds(e, 1), f:f + 1].rearrange("p a b -> p (a b)"))\
                    .then_inc(gelu_done, 1)

            def eo_evac(e, k, pairs_out=None):
                act.wait_ge(ed_ready, e * 2 + 2)
                if pairs_out is not None:
                    act.wait_ge(eoT_tp[1], pairs_out)
                act.activation(eoT[:, :, k, :], bank(4 + k).rearrange("p (b s) -> p b s", s=S0), ACT.Identity,
                               bias=ebias[:, bass.ds(e, 1), 4:5].rearrange("p a b -> p (a b)")).then_inc(eo_sb, 1)

            def eo_low(c):
                act.wait_ge(eoT_tp[0], c + 1)
                copy(eo[:, bass.ds(c, 1), 0:4, :].rearrange("p a b o -> p (a b o)"), bank(6)).then_inc(eo_tok[0], 1)

            def expert_pair(i, last=False):
                for k in range(2):
                    for f in range(2):
                        n = i * 4 + (2 * k + f)
                        if f == 0:
                            gate_up0_high(n + 1, i, k, 1)
                        elif k == 0:
                            gate_up0_high(n + 1, i, 1, 0)
                        elif not last:
                            gate_up0_high(n + 1, i + 1, 0, 0)
                        gelu(n, i * 2 + k, f)
                        if later(i, 1) or k or f:
                            hidden0_high(n - 1, 1 - f)
                        if f == 0 and later(i, 1):
                            eo_evac(i * 2 + (k - 2), k, i - 1 if k == 0 and later(i, 2) else None)
                        if f == 0 and k == 0 and later(i, 2):
                            eo_low(i - 2)

            gate_up0_high(0, 0, 0, 0)
            expert_pair(0)
            expert_pair(1)
            with act.Fori(2, E0 // 2 - 1) as i:
                expert_pair(i)
            expert_pair(E0 // 2 - 1, True)
            hidden0_high(STEPS0 - 1, 1)
            eo_evac(E0 - 2, 0, E0 // 2 - 1)
            eo_evac(E0 - 1, 1)
            eo_low(E0 // 2 - 2)
            eo_low(E0 // 2 - 1)

            load_table(ACT.Exp)
            act.wait_ge(simT_mm, 1)
            act.activation(dw2T, psum[:, 0, 0:B // 2], ACT.Identity, bias=scal[:, 1:2]).then_inc(simT_sb, 1)
            act.wait_ge(simT_sb, 1)
            ln_evac_group(2, 0)
            for q in range(B // 2):
                if q + 1 < NG:
                    ln_evac_group(2, q + 1)
                act.wait_ge(simT_mm, q + 2)
                for r in range(2):
                    own = slice(C * r, C * r + C)
                    last = act.activation(simT[own, q, :], psum[own, q, N * r:N * r + N], ACT.Identity, bias=dw2T[own, q:q + 1])
                last.then_inc(simT_sb, 1)
            for hf in range(2):
                act.wait_ge(sim_sub, hf + 1)
                act.activation(e1[:, 8 * hf:8 * hf + 8, :], s1[:, 8 * hf:8 * hf + 8, :], ACT.Exp).then_inc(sim_exp, 1)
            act.wait_ge(bt_max, 1)
            act.activation(bt[0:B, :], psum[0:B, 7, 0:N], ACT.Exp, bias=bsm[0:B, 0:1], accum_out=bsm[0:B, 1:2]).then_inc(bt_exp, 1)
            for hf in range(2):
                act.wait_ge(aT_tp, hf + 1)
                copy(aT[:, 2 * hf:2 * hf + 2, :], bank(2 + hf).rearrange("p (q n) -> p q n", q=2)).then_inc(aT_sb, 1)
            act.wait_ge(bt_tp, 2)
            copy(btT.rearrange("p (b w) -> p b w", b=B)[:, :, 0:2 * B:B],
                 psum[:, 7, 256:256 + TB * B].rearrange("p (k b) -> p b k", k=TB)).then_inc(btT_sb, 1)
            for g in range(NG):
                if g == 2:
                    act.wait_ge(hc_mm, 1)
                    copy(hc[0:B, :], psum[0:B, 7, 288:288 + D]).then_inc(hc_sb, 1)
                    act.wait_ge(hc_mm, 2)
                    copy(hcT, psum[:, 7, 416:416 + B]).then_inc(hc_sb, 1)
                act.wait_ge(hq_mm, g + 1)
                copy(hq_part(hqT, g), bank(HQ_BANKS[g]).rearrange("p (q n) -> p q n", q=2)).then_inc(hq_sb, 1)

            load_table(ACT.Sigmoid)
            ln_evac(3)
            act.wait_ge(x_done, 3 * NT)
            for hf in range(2):
                act.wait_ge(rl_mm, hf + 1)
                act.activation(sc1[:, 8 * hf:8 * hf + 8, :], bank(hf).rearrange("p (t e) -> p t e", e=E1), ACT.Sigmoid).then_inc(rl_sig, 1)
            def norm_high(hf, k):
                copy(norm_half(hf, k, 0), xnT[:, 1024 * hf + 512 * k:1024 * hf + 512 * k + 512]).then_inc(xh_hi, 1)

            def shared_sum(g):
                act.wait_ge(sd_ready, g + 1)
                copy(osh[:, 512 * g:512 * g + 512], bank(6 + g % 2)).then_inc(osh_done, 1)

            def gate_up1_high(i, slot, local):
                act.wait_ge(w1gu_in[slot], i * 16 + 16)
                if later(i, 1):
                    act.wait_ge(up_ready, i * 4 + (2 * slot - 2))
                copy(selr[:, slot, :], sel1[:, bass.ds(local, P)])
                copy(wgu[:, slot, 0, :], w1gu[:, slot, :]).then_inc(wgu_hi, 1)

            norm_high(0, 0)
            norm_high(0, 1)
            for m in range(2 * NG):
                act.wait_ge(sg_ready, m + 1)
                if m >= 2:
                    act.wait_ge(hs_done, m - 1)
                if m == 4:
                    act.wait_ge(pool_made, 1)
                    gate_up1_high(0, 0, 0)
                act.activation(sil[0:I1, m % 2, :], psum[0:I1, 2 + m % 2, :], ACT.Silu)
                copy(u1[0:I1, m % 2, :], psum[0:I1, 4 + m % 2, :]).then_inc(sil_s, 1)
                if m % 2 and m >= 5:
                    shared_sum(m // 2 - 2)
            shared_sum(NG - 2)
            shared_sum(NG - 1)
            def down1_high(i, slot):
                act.wait_ge(w1dn_in[slot], i * 16 + 16)
                if later(i, 1):
                    act.wait_ge(down_done, i * 4 + (2 * slot - 2))
                copy(wdn[:, slot, 0, :], w1dn[:, slot, :]).then_inc(wdn_hi, 1)

            def silu1(n, k):
                act.wait_ge(gate_ready, n + 1)
                if later(n, 2):
                    act.wait_ge(prod_done, n - 1)
                act.activation(sil[:, k, :], bank(k), ACT.Silu).then_inc(nl_done, 1)

            def hidden1_high(n, k):
                act.wait_ge(hid_done, n + 1)
                if later(n, 2):
                    act.wait_ge(down_done, n - 1)
                copy(hh[:, k, 0, :], h1[:, k, :]).then_inc(hh_hi, 1)

            def chunk_pair1(i, hf, last=False):
                for slot in range(2):
                    silu1(i * 4 + 2 * slot, 0)
                    if later(i, 1) or slot:
                        hidden1_high(i * 4 + (2 * slot - 1), 1)
                    if slot == 0:
                        gate_up1_high(i, 1, i * 2 * P + (P - NC1 * P * hf))
                    elif not last:
                        gate_up1_high(i + 1, 0, 0 if last is None else i * 2 * P + (2 * P - NC1 * P * hf))
                    down1_high(i, slot)
                    if last is None and slot:
                        act.wait_ge(up_ready, 2 * NC1 - 1)
                        norm_high(1, 1)
                    silu1(i * 4 + (2 * slot + 1), 1)
                    hidden1_high(i * 4 + 2 * slot, 0)

            norm_high(1, 0)
            for g in range(NG):
                act.wait_ge(rw_tp, g + 1)
                copy(rwr[:, 512 * g:512 * g + 512], bank(4 + g)).then_inc(rwr_hi, 1)
            chunk_pair1(0, 0)
            with act.Fori(1, NC1 // 2 - 1) as i:
                chunk_pair1(i, 0)
            chunk_pair1(NC1 // 2 - 1, 0, None)
            with act.Fori(NC1 // 2, NC1 - 1) as i:
                chunk_pair1(i, 1)
            chunk_pair1(NC1 - 1, 1, True)
            hidden1_high(4 * NC1 - 1, 1)

            def attention_tail(L, base):
                act.wait_ge(sim_sub, base + 3)
                for hf in range(2):
                    act.wait_ge(sim_sub, base + hf + 3)
                    act.activation(e2[:, 8 * hf:8 * hf + 8, :], s2[:, 8 * hf:8 * hf + 8, :], ACT.Exp).then_inc(sim_exp, 1)
                for g in range(NG):
                    act.wait_ge(e2_tp, 2 * base + g + 1)
                    copy(e2T[0:C, 512 * g:512 * g + 512], psum[0:C, 2 + g, :]).then_inc(e2_sb, 1)

            load_table(ACT.Exp)
            ln_evac(4)
            act.wait_ge(x_done, 4 * NT)
            attention_tail(4, 0)

            load_table(ACT.Sigmoid)
            ln_evac(5)
            act.wait_ge(x_done, 5 * NT)
            act.wait_ge(rl_mm, 3)
            act.activation(pr2, psum[:, 4, 0:NT * E2].rearrange("p (t e) -> p t e", e=E2), ACT.Sigmoid).then_inc(rl_sig, 1)
            norm_high(0, 0)
            norm_high(0, 1)
            norm_high(1, 0)
            def up2_high(i, slot, local):
                act.wait_ge(up_ready, i * 4 + (2 * slot - 2))
                copy(wgu[:, slot, 0, 0:P], w2part(local, 0)).then_inc(wgu_hi, 1)

            def down2_high(i, slot, local):
                act.wait_ge(down_done, i * 4 + (2 * slot - 2))
                copy(wdn[:, slot, 0, :], w2part(local, 1)).then_inc(wdn_hi, 1)

            def relu2(n, k):
                act.wait_ge(up_ready, n + 1)
                act.wait_ge(hid_done, n - 1)
                act.activation(r2[:, k, :], bank(k), ACT.Relu).then_inc(nl_done, 1)

            def hidden2_high(n, k):
                act.wait_ge(hid_done, n + 1)
                act.wait_ge(down_done, n - 3)
                copy(hidden2_part(k, 0), h2[:, k % 2, :]).then_inc(hh_hi, 1)

            def chunk_pair2(i, hf, first=False, last=False, ends=False):
                for slot in range(2):
                    relu2(i * 4 + 2 * slot, 0)
                    if slot == 0:
                        up2_high(i, 1, i * 2 + (1 - 2 * NC1 - NC2 * hf))
                    elif not last:
                        up2_high(i + 1, 0, i * 2 + (2 - 2 * NC1 - NC2 * hf))
                    if slot or not first:
                        hidden2_high(i * 4 + (2 * slot - 1), (2 * slot - 1) % 4)
                    if ends and slot:
                        act.wait_ge(up_ready, 4 * NC1 + 2 * NC2 - 1)
                        norm_high(1, 1)
                    relu2(i * 4 + (2 * slot + 1), 1)
                    down2_high(i, slot, i * 2 + (slot - 2 * NC1 - NC2 * hf))
                    hidden2_high(i * 4 + 2 * slot, 2 * slot)

            act.wait_ge(w2_in, 32)
            up2_high(NC1, 0, 0)
            for q in range(2):
                act.wait_ge(rw_tp, NG + q + 1)
                copy(cT[:, 1024 * q:1024 * q + 1024], bank(2 + q).bitcast(BF16)).then_inc(rw_sb, 1)
            chunk_pair2(NC1, 0, first=True)
            with act.Fori(NC1 + 1, NC1 + NC2 // 2 - 1) as i:
                chunk_pair2(i, 0)
            chunk_pair2(NC1 + NC2 // 2 - 1, 0, ends=True)
            with act.Fori(NC1 + NC2 // 2, NC1 + NC2 - 1) as i:
                chunk_pair2(i, 1)
            chunk_pair2(NC1 + NC2 - 1, 1, last=True)
            hidden2_high(4 * (NC1 + NC2) - 1, 3)
            act.wait_ge(down_done, 4 * (NC1 + NC2))
            for q in range(NG):
                copy(o2T[:, 512 * q:512 * q + 512], bank(4 + q)).then_inc(o2_sb, 1)

            load_table(ACT.Exp)
            ln_evac(6)
            act.wait_ge(x_done, 6 * NT)
            attention_tail(6, 2)
            for g in range(NG):
                act.wait_ge(c3_mm, g + 1)
                copy(c3T[:, 512 * g:512 * g + 512], bank((0, 1, 2, 3)[g])).then_inc(c3_sb, 1)

            load_table(ACT.Silu)
            act.wait_ge(wq_done, 1)
            copy(w1r, w1q)

            def token_scale(g):
                act.wait_ge(qi_done, 2 * g + 2)
                for t in range(4 * g, 4 * g + 4):
                    last = act.activation(qa[:, t, :], qa[:, t, :], ACT.Copy, scale=rs3[:, t:t + 1])
                last.then_inc(xq_done, 1)

            def token_high(g):
                act.wait_ge(xq_tp, g + 1)
                copy(xq_high[:, 512 * g:512 * g + 512], bank(2 + g % 2)).then_inc(xq_hi, 1)

            def unit_in(n):
                c = n % NC3
                act.wait_ge(l1_ready, n + 1)
                if n == 0:
                    act.wait_ge(pool_made, 4)
                if n >= 4:
                    act.wait_ge(g3_done, n - 3)
                act.activation(hpad[:, n % 4, :, 1:N + 1], bank(n % 2).rearrange("p (b n) -> p b n", b=2), ACT.Copy, scale=wm[:, 0:1])
                act.activation(yc[:, n % 4, :], bank(n % 2), ACT.Identity, scale=cwm[:, c:c + 1],
                               bias=cols[:, CONV + 4 * c + 3:CONV + 4 * c + 4]).then_inc(hpad_done, 1)

            def unit_out(n):
                g, c = n // NC3, n % NC3
                act.wait_ge(conv_done, n + 1)
                act.activation(g3[:, c, 512 * g:512 * g + 512], yc[:, n % 4, :], ACT.Silu).then_inc(g3_done, 1)

            token_scale(0)
            token_high(0)
            token_scale(1)
            token_high(1)
            for turn in range(TURNS3):
                if turn in (1, 2):
                    token_scale(turn + 1)
                    token_high(turn + 1)
                if 2 * turn < UNITS:
                    unit_in(2 * turn)
                    unit_in(2 * turn + 1)
                q = turn - 4
                if 0 <= q < PAIRS:
                    act.wait_ge(gi_tp, q + 1)
                    if q >= 2:
                        act.wait_ge(l2_ready, q - 1)
                    copy(giT[:, q % 2].rearrange("p c n -> p (c n)"), bank(6).bitcast(BF16)).then_inc(gi_sb, 1)
                if 2 <= 2 * turn < UNITS + 2:
                    unit_out(2 * turn - 2)
                    unit_out(2 * turn - 1)
                q = turn - 3
                if 0 <= q < PAIRS:
                    act.wait_ge(qs4_done, q + 1)
                    if q >= 2:
                        act.wait_ge(gi_done, q - 1)
                    for k in range(2):
                        last = act.activation(ga[:, q % 2, k, :], bank(2 + 2 * (q % 2) + k), ACT.Copy, scale=qs4[:, 2 * q + k:2 * q + k + 1])
                    last.then_inc(ga_done, 1)

        @block.vector
        def _(dve):
            step = [0]

            def then(ins):
                step[0] += 1
                ins.then_inc(dve_step, 1)
                dve.wait_ge(dve_step, step[0])

            def ln_stats(L, g):
                ts = range(4 * g, 4 * g + 4)
                if L == 0:
                    dve.wait_ge(x_in[g], 16)
                if L > 0:
                    dve.wait_ge(x_done, NT * (L - 1) + 4 * g + 4)
                for t in ts:
                    last = dve.bn_stats(stats[:, t, :], X[:, t, :])
                then(last)
                for t in ts:
                    last = dve.bn_aggr(mv[:, t, :], stats[:, t, :])
                then(last)
                s = slice(4 * g, 4 * g + 4)
                dve.tensor_scalar(veps[:, s], mv[:, s, 1], EPS, None, ALU.add).then_inc(ln_var, 1)

            def ln_apply(L, g):
                dve.wait_ge(ln_rstd, NG * L + g + 1)
                if g >= 1 and applied_behind(L, g - 1):
                    dve.wait_ge(ln_xn, NG * L + g)
                for t in range(4 * g, 4 * g + 4):
                    last = dve.tensor_scalar(xn[:, t, :], X[:, t, :], mv[:, t, 0:1], rstd[:, t:t + 1], ALU.subtract, ALU.mult)
                last.then_inc(ln_xn, 1)

            def norm_behind(L, t):
                if t % 4 == 3:
                    ln_stats(L, t // 4)
                    if L == 7 and t >= 8:
                        token_integers(t // 4 - 2)
                    if L == 7 and t >= 4:
                        token_scales(t // 4 - 1)
                if L == 7:
                    return
                if t % 4 == 1 and t >= 4 and not applied_behind(L, t // 4 - 1):
                    ln_apply(L, t // 4 - 1)
                if t == NT - 1 and L != 1:
                    ln_apply(L, NG - 1)

            def output_groups(L, base):
                for g in range(NG):
                    r = slice(4 * g, 4 * g + 4)
                    dve.wait_ge(ffn_tp, base + g + 1)
                    dve.tensor_tensor(X[:, r, :], bank(g).rearrange("p (t d) -> p t d", t=4), X[:, r, :], ALU.add).then_inc(x_done, 4)
                    ln_stats(L, g)
                    if g >= 1 and not applied_behind(L, g - 1):
                        ln_apply(L, g - 1)
                ln_apply(L, NG - 1)

            def token_scales(g):
                r = slice(4 * g, 4 * g + 4)
                dve.wait_ge(ln_xn, NG * 7 + g + 1)
                then(dve.tensor_reduce(am3[:, r], xn[:, r, :], AX.X, ALU.max, apply_absolute_value=True))
                then(dve.tensor_scalar(am3[:, r], am3[:, r], 1e-5, None, ALU.max))
                dve.tensor_scalar(rs3[:, r], am3[:, r], 1.0 / 127.0, None, ALU.mult)
                then(dve.reciprocal(qs3[:, r], am3[:, r]))
                dve.tensor_scalar(qs3[:, r], qs3[:, r], 127.0, None, ALU.mult).then_inc(qi_done, 1)

            def token_integers(g):
                r = slice(4 * g, 4 * g + 4)
                dve.wait_ge(ln_rstd, NG * 7 + g + 1)
                then(dve.tensor_scalar(qa[:, r, :], qa[:, r, :], MAGIC, MAGIC + 127.0, ALU.add, ALU.min))
                dve.tensor_scalar(qa[:, r, :], qa[:, r, :], MAGIC - 128.0, MAGIC, ALU.max, ALU.subtract).then_inc(qi_done, 1)

            ln_stats(0, 0)
            for g in range(1, NG):
                ln_stats(0, g)
                ln_apply(0, g - 1)
            ln_apply(0, NG - 1)
            dve.wait_ge(krep_done, 1)
            dve.wait_ge(consts, 1)
            for b in range(0, B, 2):
                dve.tensor_tensor(kbd[:, b], wide(krep[:, b * C:(b + 1) * C].unsqueeze(1), H0, C),
                                  wide(headmask[:, :].unsqueeze(2), H0, C), ALU.mult).then_inc(kbd_done[0], 1)
            dve.wait_ge(w_slots, 16 * N_SLOTS)
            for t in range(ES // P):
                last = dve.bn_stats(sstats[:, t, :], slot_raw[:, t, :])
            then(last)
            for t in range(ES // P):
                last = dve.bn_aggr(smv[:, t, :], sstats[:, t, :])
            then(last)
            dve.tensor_scalar(srstd[:, 0, :], smv[:, :, 1], EPS, None, ALU.add).then_inc(se_var, 1)
            dve.tensor_scalar(slot_gs[:, :], cols[:, COL["slot_g"]:COL["slot_g"] + 2], scal[:, 0:1], None, ALU.mult).then_inc(se_n, 1)
            dve.wait_ge(se_rstd, 1)
            for t in range(ES // P):
                last = dve.tensor_scalar(slot_n[:, t, :], slot_raw[:, t, :], smv[:, t, 0:1], srstd[:, 1, t:t + 1], ALU.subtract, ALU.mult)
            last.then_inc(se_n, 1)
            for t in range(NT + 3):
                if t < NT:
                    dve.wait_ge(sim_ready, t + 1)
                    sim = psum[:, 2 * (t % 2):2 * (t % 2) + 2, :].rearrange("p a (h k) -> p (a h) k", k=C)
                    then(dve.tensor_reduce(mx0[:, t % 2, :], sim, AX.X, ALU.max))
                    if t >= 2:
                        dve.wait_ge(exp_done, t - 1)
                    dve.tensor_tensor(simS[:, t % 2], sim, wide(mx0[:, t % 2, :].unsqueeze(2), H0, C), ALU.subtract).then_inc(sim_used, 1)
                if t >= 3:
                    u = t - 3
                    dve.wait_ge(out_ready, u + 1)
                    dve.tensor_tensor(X[:, u, :], X[:, u, :], psum[:, 7, 0:D], ALU.add).then_inc(x_done, 1)
                    norm_behind(1, u)
                if 2 <= t <= NT + 1:
                    u = t - 2
                    dve.wait_ge(av_ready, u + 1)
                    av = psum[:, 6, 0:H0 * (HD + 1)].rearrange("p (h k) -> p h k", k=HD + 1)
                    then(dve.reciprocal(rden0[:, u % 2, :], av[:, :, HD]))
                    if u >= 2:
                        dve.wait_ge(yT_ready, u - 1)
                    dve.tensor_tensor(y0[:, u % 2], av[:, :, 0:HD], wide(rden0[:, u % 2, :].unsqueeze(2), H0, HD), ALU.mult)\
                        .then_inc(y_ready, 1)


            def bmax(k):
                dve.wait_ge(bl_ready, k + 1)
                if k >= 2:
                    dve.wait_ge(bexp_done, k - 1)
                dve.tensor_reduce(nmB[:, k % 2, :], bank(k % 2).rearrange("p (c n) -> p c n", c=2), AX.X, ALU.max, negate=True)\
                    .then_inc(bmax_done, 1)

            def brec(k):
                dve.wait_ge(bexp_done, k + 1)
                if k >= 2:
                    dve.wait_ge(bnorm_done, k - 1)
                dve.reciprocal(recB[:, k % 2, :], sumB[:, k % 2, :]).then_inc(brec_done, 1)

            def amax(t):
                dve.wait_ge(al_ready, t + 1)
                dve.tensor_reduce(nmA[:, t:t + 1], psum[:, 2:4, :].rearrange("p a n -> p (a n)"), AX.X, ALU.max, negate=True)\
                    .then_inc(amax_done, 1)

            def qt_evac(b, j):
                k = 4 * b + j
                dve.wait_ge(bT_ready, k + 1)
                if b >= 1:
                    dve.wait_ge(slots_mm, 2 * b - 1 + j // 2)
                dve.tensor_copy(qt[:, :, N * j:N * j + N], bank(4 + j % 2).rearrange("p (a n) -> p a n", a=TB)).then_inc(qt_sb, 1)

            bmax(0)
            ln_apply(1, NG - 1)
            bmax(1)
            brec(0)
            for q in range(4 * B):
                if q + 1 < 4 * B:
                    brec(q + 1)
                if q % 2 == 0:
                    amax(q // 2)
                qt_evac(q // 4, q % 4)
                if q + 2 < 4 * B:
                    bmax(q + 2)
            dve.wait_ge(aexp_done, NT)
            dve.reciprocal(rinvA, rsumA)

            def slot_halves(e, k):
                if later(e, 2):
                    dve.wait_ge(eu_ready, e * 2 - 2)
                slots_e = slotsT[:, bass.ds(e, 1), :, :].rearrange("p a b s -> p (a b s)")
                r = slice(512 * k, 512 * k + 512)
                dve.tensor_copy(xh[:, 0, r], slots_e).then_inc(xh_hi, 1)
                dve.wait_ge(xh_hi, e + 1)
                dve.tensor_tensor(xh[:, 1, r], slots_e, xh[:, 0, r].bitcast(F32), ALU.subtract).then_inc(xh_lo, 1)

            def hidden0(n, e, f):
                dve.wait_ge(eu_ready, n + 1)
                dve.wait_ge(gelu_done, n + 1)
                if later(n, 2):
                    dve.wait_ge(hh_hi, n - 1)
                    dve.wait_ge(hh_lo, n - 1)
                    dve.wait_ge(hh_lo2, n - 1)
                dve.scalar_tensor_tensor(h0[:, f, :], bank(2 + f), ebias[:, bass.ds(e, 1), 2 + f:3 + f].rearrange("p a b -> p (a b)"),
                                         gel[:, f, :], ALU.add, ALU.mult).then_inc(h0_done, 1)

            def down0_halves(n, k, f, loaded):
                dve.wait_ge(edn_in[k], loaded)
                if later(n, 2):
                    dve.wait_ge(ed_ready, n - 1)
                raw = edn[:, k, P * f:P * f + P]
                dve.tensor_copy(wdn[:, f, 0, :], raw).then_inc(wdn_hi, 1)
                dve.wait_ge(wdn_hi, n + 1)
                dve.tensor_tensor(wdn[:, f, 1, :], raw, wdn[:, f, 0, :].bitcast(F32), ALU.subtract).then_inc(wdn_lo, 1)

            def low0(n, f):
                r = slice(LOW0, 512)
                dve.wait_ge(hh_hi, n + 1)
                dve.tensor_tensor(hh[:, f, 1, r], h0[:, f, r], hh[:, f, 0, r].bitcast(F32), ALU.subtract).then_inc(hh_lo2, 1)

            def eo_high(c):
                dve.wait_ge(eoT_tp[1], c + 1)
                dve.tensor_copy(eo[:, bass.ds(c, 1), 4:8, :].rearrange("p a b o -> p (a b o)"), bank(7)).then_inc(eo_tok[1], 1)

            def expert_pair(i, last=False):
                for k in range(2):
                    for f in range(2):
                        n = i * 4 + (2 * k + f)
                        hidden0(n, i * 2 + k, f)
                        if later(i, 1) or k or f:
                            low0(n - 1, 1 - f)
                        if f:
                            down0_halves(n - 1, k, 0, i * 16 + 16)
                        elif k:
                            down0_halves(n - 1, 0, 1, i * 16 + 16)
                        elif later(i, 1):
                            down0_halves(n - 1, 1, 1, i * 16)
                        if f and not last:
                            slot_halves(i * 2 + (k + 2), k)
                        if f == 0 and k == 0 and later(i, 2):
                            eo_high(i - 2)

            dve.wait_ge(slots_sb, 2 * B)
            slot_halves(0, 0)
            slot_halves(1, 1)
            expert_pair(0)
            expert_pair(1)
            with dve.Fori(2, E0 // 2 - 1) as i:
                expert_pair(i)
            expert_pair(E0 // 2 - 1, True)
            down0_halves(STEPS0 - 1, 1, 1, 8 * E0)
            low0(STEPS0 - 1, 1)
            eo_high(E0 // 2 - 2)
            eo_high(E0 // 2 - 1)
            for t in range(NT):
                dve.wait_ge(comb_ready, t + 1)
                dve.scalar_tensor_tensor(X[:, t, :], psum[:, 2 + t % 4, 0:D], rinvA[:, t:t + 1], X[:, t, :], ALU.mult, ALU.add)\
                    .then_inc(x_done, 1)
                norm_behind(2, t)

            dve.wait_ge(w_rest, 16 * (len(REST) + 1))
            dve.memset(btT, 0.0)
            dve.tensor_scalar(cw, ctxT[:, :], cols[:, COL["w_sim3"]:COL["w_sim3"] + 1], cols[:, COL["w_sim1"]:COL["w_sim1"] + 1],
                              ALU.mult, ALU.add).then_inc(cw_done, 1)
            for hf in range(2):
                r = slice(8 * hf, 8 * hf + 8)
                sim = bank(4 + hf).rearrange("p (t j) -> p t j", j=C)
                dve.wait_ge(sim_mm, hf + 1)
                then(dve.tensor_reduce(mx1[:, r], sim, AX.X, ALU.max))
                dve.tensor_copy(mx1b.rearrange("p (a q r) -> p q a r", a=TB, q=B // 2)[:, 2 * hf:2 * hf + 2],
                                mx1[:, r].rearrange("p (q a r) -> p q a r", q=2, a=TB))
                dve.tensor_tensor(s1[:, r, :], sim, wide(mx1[:, r].unsqueeze(2), 8, C), ALU.subtract).then_inc(sim_sub, 1)
            for hf in range(2):
                r = slice(8 * hf, 8 * hf + 8)
                dve.wait_ge(sim_exp, hf + 1)
                then(dve.tensor_reduce(den1[:, r], e1[:, r, :], AX.X, ALU.add))
                then(dve.reciprocal(rden1[:, r], den1[:, r]))
                dve.tensor_tensor(e1n[:, r, :], e1[:, r, :], wide(rden1[:, r].unsqueeze(2), 8, C), ALU.mult).then_inc(e1_norm, 1)
                if hf == 0:
                    dve.wait_ge(bt_tp, 1)
                    dve.tensor_reduce(bsm[0:B, 0:1], psum[0:B, 7, 0:N], AX.X, ALU.max, negate=True).then_inc(bt_max, 1)
            dve.wait_ge(bt_exp, 1)
            then(dve.reciprocal(bsm[0:B, 2:3], bsm[0:B, 1:2]))
            dve.tensor_scalar(btn[0:B, :], bt[0:B, :], bsm[0:B, 2:3], None, ALU.mult).then_inc(bt_norm, 1)
            for g in range(NG):
                dve.wait_ge(hq_sb, g + 1)
                dve.tensor_tensor(hq_part(xhT, g), hq_part(hqT, g), hq_part(xnT, g), ALU.mult).then_inc(xh_done, 1)
                if g == 1:
                    dve.wait_ge(hc_sb, 2)
                    for b in range(B):
                        last = dve.tensor_scalar(xcT[:, N * b:N * b + N], xnT[:, N * b:N * b + N], hcT[:, b:b + 1], None, ALU.mult)
                        if b % 4 == 3:
                            last.then_inc(xc_done, 1)
            dve.wait_ge(xbias_done, 1)
            for t in range(NT):
                dve.wait_ge(qv_ready, t + 1)
                dve.tensor_tensor(X[:, t, :], psum[:, 3 + t % 3, 0:D], X[:, t, :], ALU.add).then_inc(x_done, 1)
                norm_behind(3, t)

            def rank_of(dst, v, a, b2, n):
                own = wide(v.unsqueeze(3), n, 8, 8)
                other = wide(v.unsqueeze(2), n, 8, 8)
                dve.tensor_tensor(b2, other, own, ALU.is_equal)
                then(dve.tensor_tensor(a, other, own, ALU.is_gt))
                then(dve.tensor_tensor(b2, b2, wide(ltmask[:, :, :].unsqueeze(1), n, 8, 8), ALU.mult))
                then(dve.tensor_tensor(a, a, b2, ALU.add))
                then(dve.tensor_reduce(dst, a, AX.X, ALU.add))


            def routing():
                dve.wait_ge(rl_sig, 2)
                then(dve.tensor_tensor(sfc, sc1, wide(gbias[:, :].unsqueeze(1), NT, E1), ALU.add))
                v = sfc.rearrange("p t (g j) -> p (t g) j", j=8)
                hi = t1.rearrange("p t (g j) -> p (t g) j", j=8)
                lo = t2.rearrange("p t (g j) -> p (t g) j", j=8)
                tmp = t3.rearrange("p t (g j) -> p (t g) j", j=8)
                dve.tensor_tensor(hi[:, :, 0:4], v[:, :, 0:4], v[:, :, 4:8], ALU.max)
                then(dve.tensor_tensor(lo[:, :, 0:4], v[:, :, 0:4], v[:, :, 4:8], ALU.min))
                at = 0
                for k in (2, 1):
                    x0, x1, y = slice(at, at + k), slice(at + k, at + 2 * k), slice(at + 2 * k, at + 3 * k)
                    dve.tensor_tensor(tmp[:, :, 0:k], hi[:, :, x0], hi[:, :, x1], ALU.min)
                    dve.tensor_tensor(tmp[:, :, 4:4 + k], lo[:, :, x0], lo[:, :, x1], ALU.max)
                    then(dve.tensor_tensor(hi[:, :, y], hi[:, :, x0], hi[:, :, x1], ALU.max))
                    then(dve.tensor_tensor(lo[:, :, y], tmp[:, :, 0:k], tmp[:, :, 4:4 + k], ALU.max))
                    at += 2 * k
                then(dve.tensor_tensor(gs.rearrange("p t g -> p (t g)"), hi[:, :, at], lo[:, :, at], ALU.add))
                rank_of(rank, gs, t1.rearrange("p t (g j) -> p t g j", j=8), t2.rearrange("p t (g j) -> p t g j", j=8), NT)
                then(dve.tensor_scalar(rank, rank, 3.5, None, ALU.is_lt))
                then(dve.tensor_tensor(t1.rearrange("p t (g j) -> p t g j", j=8), sfc.rearrange("p t (g j) -> p t g j", j=8),
                                       wide(rank.unsqueeze(3), NT, 8, 8), ALU.mult))
                for t in range(NT):
                    last = dve.max(top8[:, t, :], t1[:, t, :])
                then(last)
                for t in range(NT):
                    last = dve.match_replace(t2[:, t, :], top8[:, t, :], t1[:, t, :], -3.0e38)
                then(last)
                then(dve.tensor_tensor(t3, t1, t2, ALU.not_equal))
                then(dve.tensor_tensor(t3, t3, sc1, ALU.mult))
                then(dve.tensor_reduce(rsum1[:, 0, :], t3, AX.X, ALU.add))
                then(dve.tensor_scalar(rsum1[:, 0, :], rsum1[:, 0, :], 1e-20, None, ALU.add))
                then(dve.reciprocal(rsum1[:, 1, :], rsum1[:, 0, :]))
                then(dve.tensor_scalar(rsum1[:, 1, :], rsum1[:, 1, :], 2.5, None, ALU.mult))
                for k in range(2):
                    last = dve.tensor_tensor(rwp[:, :, k, :], t3, wide(rsum1[:, 1, :].unsqueeze(2), NT, E1), ALU.mult)
                last.then_inc(rw_done, 1)

            routing()
            for g in range(NG):
                r = slice(512 * g, 512 * g + 512)
                dve.wait_ge(rwr_hi, g + 1)
                dve.tensor_tensor(rwr[E1:P, r], psum[E1:P, 4 + g, :], rwr[E1:P, r].bitcast(F32), ALU.subtract).then_inc(rwr_lo, 1)

            def hidden1(n, k):
                dve.wait_ge(up_ready, n + 1)
                dve.wait_ge(nl_done, n + 1)
                dve.tensor_tensor(u1[:, k, :], bank(2 + k), sil[:, k, :], ALU.mult).then_inc(prod_done, 1)
                dve.wait_ge(prod_done, n + 1)
                if later(n, 2):
                    dve.wait_ge(hh_hi, n - 1 + STEPS0)
                    dve.wait_ge(hh_lo, n - 1 + STEPS0)
                dve.tensor_tensor(h1[:, k, :], bank(4 + k), u1[:, k, :], ALU.mult).then_inc(hid_done, 1)

            def sum1(hf):
                dve.wait_ge(down_done, 2 * NC1 * (hf + 1))
                for q in range(2):
                    r = slice(1024 * hf + 512 * q, 1024 * hf + 512 * q + 512)
                    dve.tensor_tensor(osh[:, r], osh[:, r], bank(6 + q), ALU.add).then_inc(o1_done, 1)

            for s in range(4):
                hidden1(s, s % 2)
            with dve.Fori(1, NC1 // 2) as i:
                for s in range(4):
                    hidden1(i * 4 + s, s % 2)
            for s in range(4):
                hidden1(2 * NC1 + s, s % 2)
                if s == 1:
                    sum1(0)
            with dve.Fori(NC1 // 2 + 1, NC1) as i:
                for s in range(4):
                    hidden1(i * 4 + s, s % 2)
            sum1(1)
            output_groups(4, 0)

            def project(L, base, qb_, kb_, vrow, mm):
                dve.wait_ge(qk2_mm, mm + 1)
                if kb_ is None:
                    dve.tensor_copy(k2T, bank(0)).then_inc(qk2_sb, 1)
                else:
                    dve.tensor_scalar(k2T, bank(0), cols[:, kb_:kb_ + 1], None, ALU.add).then_inc(qk2_sb, 1)
                if L == 4:
                    weight_scales()
                for g in range(NG):
                    dve.wait_ge(qk2_mm, mm + g + 2)
                    dve.tensor_scalar(q2T[:, 512 * g:512 * g + 512], bank(2 + g), cols[:, qb_:qb_ + 1], float(D) ** -0.5, ALU.add, ALU.mult)\
                        .then_inc(qk2_sb, 1)
                dve.wait_ge(v2_mm, mm // 5 + 1)
                dve.tensor_tensor(v2[0:C], psum[0:C, 6:8, :].rearrange("p a (b d) -> p (a b) d", d=D),
                                  rows[0:C, vrow, :].unsqueeze(1).broadcast_to([C, B, D]), ALU.add).then_inc(v2_sb, 1)

            def softmax(base):
                for hf in range(2):
                    r = slice(8 * hf, 8 * hf + 8)
                    sim = bank(hf).rearrange("p (t j) -> p t j", j=C)
                    dve.wait_ge(sim_mm, base + hf + 3)
                    then(dve.tensor_reduce(mx2[:, r], sim, AX.X, ALU.max))
                    dve.tensor_tensor(s2[:, r, :], sim, wide(mx2[:, r].unsqueeze(2), 8, C), ALU.subtract).then_inc(sim_sub, 1)
                for hf in range(2):
                    r = slice(8 * hf, 8 * hf + 8)
                    dve.wait_ge(sim_exp, base + hf + 3)
                    then(dve.tensor_reduce(den2[:, r], e2[:, r, :], AX.X, ALU.add))
                    then(dve.reciprocal(rden2[:, r], den2[:, r]))

            both = (w1f[:, :], w2f[:, :, :].rearrange("p c o -> p (c o)"))

            def weight_sums():
                for k in range(2):
                    last = dve.tensor_reduce(wsum[:, k:k + 1], both[k], AX.X, ALU.add, apply_absolute_value=True)
                last.then_inc(wsum_done, 1)

            def weight_scales():
                dve.wait_ge(wsum_mm, 1)
                then(dve.tensor_scalar(wm, psum[:, 1, 0:2], 1.0 / (D * HID3), 1e-5, ALU.mult, ALU.max))
                then(dve.reciprocal(wr, wm))

            def integer_weights():
                for k in range(2):
                    last = dve.tensor_scalar(wa[:, k, :], both[k], wr[:, k:k + 1], MAGIC, ALU.mult, ALU.add)
                then(last)
                for k in range(2):
                    last = dve.tensor_scalar(wa[:, k, :], wa[:, k, :], MAGIC + 1.0, MAGIC - 1.0, ALU.min, ALU.max)
                then(last)
                dve.tensor_scalar(w1q, wa[:, 0, :], MAGIC, None, ALU.subtract)
                dve.tensor_scalar(w2q.rearrange("p c o -> p (c o)"), wa[:, 1, :], MAGIC, None, ALU.subtract).then_inc(wq_done, 1)

            dve.wait_ge(x_done, 4 * NT)
            weight_sums()
            project(4, 0, COL["q2_b"], COL["k2_b"], ROW["v2_b"], 0)
            softmax(0)
            for t in range(NT):
                dve.wait_ge(av2_ready, t + 1)
                dve.scalar_tensor_tensor(X[:, t, :], psum[:, t % 4, 0:D], rden2[:, t:t + 1], X[:, t, :], ALU.mult, ALU.add)\
                    .then_inc(x_done, 1)
                norm_behind(5, t)

            integer_weights()
            dve.wait_ge(rl_sig, 3)
            rank_of(rank2, pr2, g2a, g2b, NT)
            then(dve.tensor_scalar(rank2, rank2, 1.5, None, ALU.is_lt))
            then(dve.tensor_tensor(rank2, rank2, pr2, ALU.mult))
            then(dve.tensor_reduce(rs2[:, 0, :], rank2, AX.X, ALU.add))
            then(dve.tensor_scalar(rs2[:, 0, :], rs2[:, 0, :], 1e-20, None, ALU.add))
            then(dve.reciprocal(rs2[:, 1, :], rs2[:, 0, :]))
            then(dve.tensor_tensor(rank2, rank2, wide(rs2[:, 1, :].unsqueeze(2), NT, E2), ALU.mult))
            dve.wait_ge(pool_made, 3)
            then(dve.tensor_copy(cpk[:, :, 0:E2], rank2))
            then(dve.tensor_tensor(rank2, rank2, cpk[:, :, 0:E2], ALU.subtract))
            then(dve.tensor_copy(cpk[:, :, E2:2 * E2], rank2))
            then(dve.tensor_tensor(rank2, rank2, cpk[:, :, E2:2 * E2], ALU.subtract))
            dve.tensor_copy(cpk[:, :, 2 * E2:3 * E2], rank2).then_inc(rw_done, 1)

            def hidden2(n, s, first):
                k = s % 2
                dve.wait_ge(nl_done, n + 1)
                dve.tensor_tensor(u2[:, k, :], bank(2 + k), r2[:, k, :], ALU.mult).then_inc(prod_done, 1)
                dve.wait_ge(prod_done, n + 1)
                dve.wait_ge(hh_hi, n - 1 + STEPS0)
                dve.wait_ge(hh_lo, n - 1 + STEPS0)
                dve.tensor_tensor(h2[:, k, :], u2[:, k, :], r2[:, k, :], ALU.mult).then_inc(hid_done, 1)
                if not first:
                    low2(n - 1, (s - 1) % 4)

            def low2(n, k):
                r = slice(LOW2, 512)
                dve.wait_ge(hh_hi, n + 1 + STEPS0)
                dve.tensor_tensor(hidden2_part(k, 1)[:, r], h2[:, k % 2, r], hidden2_part(k, 0)[:, r].bitcast(F32), ALU.subtract).then_inc(hh_lo2, 1)

            for s in range(4):
                hidden2(4 * NC1 + s, s, s == 0)
            with dve.Fori(NC1 + 1, NC1 + NC2) as i:
                for s in range(4):
                    hidden2(i * 4 + s, s, False)
            low2(4 * (NC1 + NC2) - 1, 3)
            output_groups(6, NG)

            project(6, 2, COL["q3_b"], None, ROW["v3_b"], 5)
            softmax(2)
            dve.wait_ge(xbias_done, 2)
            for t in range(NT):
                dve.wait_ge(av2_ready, NT + t + 1)
                dve.scalar_tensor_tensor(X[:, t, :], psum[:, 4 + t % 4, 0:D], rden2[:, t:t + 1], X[:, t, :], ALU.mult, ALU.add)\
                    .then_inc(x_done, 1)
                norm_behind(7, t)

            dve.tensor_scalar(cwm, cols[:, CONV + 1:NCOL:4], wm[:, 0:1], None, ALU.mult)

            def token_low(g):
                r = slice(512 * g, 512 * g + 512)
                dve.wait_ge(xq_hi, g + 1)
                dve.tensor_tensor(xq_low[:, r], bank(2 + g % 2), xq_high[:, r].bitcast(F32), ALU.subtract).then_inc(xq_lo, 1)

            def convolve(n):
                c = n % NC3
                w = CONV + 4 * c
                dve.wait_ge(hpad_done, n + 1)
                y = yc[:, n % 4, :].rearrange("p (b n) -> p b n", b=2)
                then(dve.scalar_tensor_tensor(y, hpad[:, n % 4, :, 0:N], cols[:, w:w + 1], y, ALU.mult, ALU.add))
                dve.scalar_tensor_tensor(y, hpad[:, n % 4, :, 2:N + 2], cols[:, w + 2:w + 3], y, ALU.mult, ALU.add).then_inc(conv_done, 1)

            def quant_scale(q):
                r = slice(2 * q, 2 * q + 2)
                b = 2 + 2 * (q % 2)
                dve.wait_ge(g3_tp, q + 1)
                then(dve.tensor_reduce(am4[:, r], psum[:, b:b + 2, :], AX.X, ALU.max, apply_absolute_value=True))
                then(dve.tensor_scalar(am4[:, r], am4[:, r], 1e-5, None, ALU.max))
                then(dve.reciprocal(qs4[:, r], am4[:, r]))
                dve.tensor_scalar(rs4[:, r], am4[:, r], wm[:, 1:2], 1.0 / 127.0, ALU.mult, ALU.mult)
                dve.tensor_scalar(qs4[:, r], qs4[:, r], 127.0, None, ALU.mult).then_inc(qs4_done, 1)

            def integers(q):
                dve.wait_ge(ga_done, q + 1)
                then(dve.tensor_scalar(ga[:, q % 2], ga[:, q % 2], MAGIC, MAGIC + 127.0, ALU.add, ALU.min))
                if q >= 2:
                    dve.wait_ge(gi_tp, q - 1)
                dve.tensor_scalar(gi[:, q % 2].rearrange("p c n -> p (c n)"), ga[:, q % 2].rearrange("p t n -> p (t n)"),
                                  MAGIC - 128.0, MAGIC, ALU.max, ALU.subtract).then_inc(gi_done, 1)

            token_low(0)
            token_integers(2)
            token_low(1)
            token_scales(3)
            for turn in range(TURNS3):
                if turn == 1:
                    token_integers(3)
                if turn in (1, 2):
                    token_low(turn + 1)
                if 0 <= turn - 4 < PAIRS:
                    integers(turn - 4)
                if 0 <= turn - 3 < PAIRS:
                    quant_scale(turn - 3)
                if 2 * turn < UNITS:
                    convolve(2 * turn)
                    convolve(2 * turn + 1)
                q = turn - 5
                if q >= 0:
                    dve.wait_ge(l2_ready, q + 1)
                    for k in range(2):
                        t = 2 * q + k
                        dve.scalar_tensor_tensor(X[:, t, :], psum[:, 7, P * k:P * k + P], rs4[:, t:t + 1], X[:, t, :], ALU.mult, ALU.add)\
                            .then_inc(x_done, 1)

        @block.tensor
        def _(pe):
            def mm(dst, lhsT, rhs, start=True, stop=True):
                return pe.matmul(dst, lhsT=lhsT, rhs=rhs, start=start, stop=stop)

            def product(dst, w, x):
                mm(dst, w(0), x(0), True, False)
                mm(dst, w(0), x(1), False, False)
                return mm(dst, w(1), x(0), False, True)

            def ln_transpose(L, g):
                pe.wait_ge(ln_xn, NG * L + g + 1)
                if g >= 2:
                    pe.wait_ge(ln_xnT, NG * L + g - 1)
                if g == 1 and L == 1:
                    pe.wait_ge(x_done, NT)
                for j in range(4):
                    last = pe.transpose(psum[:, 6 + g % 2, P * j:P * j + P], xn[:, 4 * g + j, :], ident[:, :])
                last.then_inc(ln_tp, 1)

            def ln_transposes(L):
                for g in range(NG):
                    ln_transpose(L, g)

            pe.wait_ge(w_l0, 16 * N_L0)
            mm(bank(0), wk0[:, :], ctxT[:, :])
            for b in range(B):
                last = mm(psum[:, 1, HD * b:HD * b + HD], ctxTd[:, P * b:P * b + P], wv0[:, :])
            last.then_inc(kv_mm, 1)
            pe.wait_ge(consts, 1)
            ln_transposes(0)
            for g in range(NG):
                pe.wait_ge(ln_xnT, g + 1)
                mm(bank(2 + g), wq0[:, :], xnT[:, 512 * g:512 * g + 512]).then_inc(q_mm, 1)
            pe.wait_ge(vaug_done, 1)
            for t in range(NT + 3):
                if t < NT:
                    b = t // TB
                    pe.wait_ge(q_sb, max(t // 4 + 1, 2))
                    pe.wait_ge(kbd_done[b % 2], b // 2 + 1)
                    if t >= 2:
                        pe.wait_ge(sim_used, t - 1)
                    for hf in range(2):
                        last = mm(bank(2 * (t % 2) + hf), qT[:, P * t:P * t + P],
                                  kbd[:, b, 8 * hf:8 * hf + 8, :].rearrange("p h k -> p (h k)"))
                    last.then_inc(sim_ready, 1)
                if t == NT:
                    pe.wait_ge(se_n, 2)
                    pe.wait_ge(sim_used, NT - 1)
                    for g in range(2):
                        for j in range(4):
                            last = pe.transpose(psum[:, g, P * j:P * j + P], slot_n[:, 4 * g + j, :], ident[:, :])
                        last.then_inc(se_tp, 1)
                if t >= 3:
                    u = t - 3
                    pe.wait_ge(y_ready, u + 1)
                    if u >= 1:
                        pe.wait_ge(x_done, u)
                    pe.transpose(psum[:, 7, 256:384], y0[:, u % 2].rearrange("p h k -> p (h k)"), ident[:, :]).then_inc(yT_ready, 1)
                if 1 <= t <= NT:
                    u = t - 1
                    pe.wait_ge(exp_done, u + 1)
                    pe.wait_ge(et_sb, u) if u >= 1 else pe.wait_ge(q_sb, 4)
                    for j in range(H0 // 2):
                        last = pe.transpose(psum[:, 4 + j // 4, P * (j % 4):P * (j % 4) + P], simE[:, u % 2, P * j:P * j + P], ident[:, :])
                    last.then_inc(et_ready, 1)
                if t >= 3:
                    u = t - 3
                    if u == 0:
                        pe.wait_ge(w_slots, 16 * N_SLOTS)
                    pe.wait_ge(yT_sb, u + 1)
                    mm(psum[:, 7, 0:D], y0T[:, u % 2, :], wo0[:, :]).then_inc(out_ready, 1)
                if 2 <= t <= NT + 1:
                    u = t - 2
                    b = u // TB
                    pe.wait_ge(et_sb, u + 1)
                    if u >= 1:
                        pe.wait_ge(y_ready, u)
                    for j in range(H0 // 2):
                        w = 2 * (HD + 1)
                        last = mm(psum[:, 6, w * j:w * j + w], simET[:, u % 2, P * j:P * j + P],
                                  vaug[:, b].rearrange("p h k -> p (h k)"))
                    last.then_inc(av_ready, 1)

            for g in range(NG - 1):
                ln_transpose(1, g)
            pe.wait_ge(x_done, NT)

            def logits_slots(k):
                b, j = k // 4, k % 4
                pe.wait_ge(ln_xnT, NG + b // 2 + 1)
                if k >= 2:
                    pe.wait_ge(bexp_done, k - 1)
                for c in range(2):
                    ch = 2 * j + c
                    last = mm(psum[:, k % 2, N * c:N * c + N], seT[:, P * ch:P * ch + P], xnT[:, N * b:N * b + N])
                last.then_inc(bl_ready, 1)

            def logits_tokens(t):
                if t >= 1:
                    pe.wait_ge(aexp_done, t)
                for hf in range(2):
                    last = mm(bank(2 + hf), xnT[:, P * t:P * t + P], seT[:, 512 * hf:512 * hf + 512])
                last.then_inc(al_ready, 1)

            def dispatch_T(k):
                b, j = k // 4, k % 4
                pe.wait_ge(bnorm_done, k + 1)
                if k >= 2:
                    pe.wait_ge(pt_sb, k // 2)
                    pe.wait_ge(qt_sb, k - 1)
                for a in range(TB):
                    for c in range(2):
                        last = pe.transpose(psum[:, 4 + j % 2, N * a + P * c:N * a + P * c + P], qb[:, k % 2, c, P * a:P * a + P], ident[:, :])
                last.then_inc(bT_ready, 1)

            def combine_T(t):
                pe.wait_ge(aexp_done, t + 1)
                pe.wait_ge(qt_sb, 2 * t + 2)
                for c in range(NC0):
                    last = pe.transpose(psum[:, 4 + c // 4, P * (c % 4):P * (c % 4) + P], pbuf[:, t % 2, P * c:P * c + P], ident[:, :])
                last.then_inc(pT_ready, 1)

            def slots_part(b, hf, a):
                if a == 0:
                    pe.wait_ge(qt_sb, 4 * b + 2 * hf + 2)
                    if b:
                        pe.wait_ge(slots_sb, 2 * (b - 1) + hf + 1)
                    else:
                        pe.wait_ge(ln_xnT, 2 * NG)
                last = mm(bank(6 + hf), xn[:, 2 * b + a, :], qt[:, a, 512 * hf:512 * hf + 512], a == 0, a == TB - 1)
                if a == TB - 1:
                    last.then_inc(slots_mm, 1)

            pe.wait_ge(se_T, 2)
            logits_slots(0)
            ln_transpose(1, NG - 1)
            logits_slots(1)
            for q in range(4 * B + 2):
                if q < 4 * B:
                    if q % 2 == 0:
                        logits_tokens(q // 2)
                    dispatch_T(q)
                    if q + 2 < 4 * B:
                        logits_slots(q + 2)
                if q >= 2:
                    slots_part((q - 2) // 4, (q - 2) % 4 // 2, q % 2)
                if q % 2 and q < 4 * B:
                    combine_T(q // 2)

            pe.wait_ge(slots_sb, 2 * B)
            pe.wait_ge(pt_sb, NT)

            def gate_up0(n, k, f):
                slots_e = slice(512 * k, 512 * k + 512)
                pe.wait_ge(wgu_lo, n + 1)
                if later(n, 2):
                    pe.wait_ge(gelu_done, n - 1)
                product(bank(f), lambda h: wgu[:, f, h, 0:P], lambda h: xh[:, h, slots_e]).then_inc(eg_ready, 1)
                if later(n, 2):
                    pe.wait_ge(h0_done, n - 1)
                product(bank(2 + f), lambda h: wgu[:, f, h, P:2 * P], lambda h: xh[:, h, slots_e]).then_inc(eu_ready, 1)

            def down0(n, k, f, evacuated=None):
                pe.wait_ge(wdn_lo, n + 1)
                pe.wait_ge(hh_lo, n + 1)
                pe.wait_ge(hh_lo2, n + 1)
                if evacuated is not None:
                    pe.wait_ge(eo_sb, evacuated)
                mm(bank(4 + k), wdn[:, f, 0, :], hh[:, f, 0, :], f == 0, False)
                mm(bank(4 + k), wdn[:, f, 0, :], hh[:, f, 1, :], False, False)
                mm(bank(4 + k), wdn[:, f, 1, :], hh[:, f, 0, :], False, f == 1).then_inc(ed_ready, 1)

            def outputs_T(c):
                pe.wait_ge(eo_sb, c * 2 + 2)
                for hf in range(2):
                    if later(c, 1):
                        pe.wait_ge(eo_tok[hf], c)
                    for j in range(4):
                        last = pe.transpose(psum[:, 6 + hf, P * j:P * j + P], eoT[:, 4 * hf + j].rearrange("p e s -> p (e s)"), ident[:, :])
                    last.then_inc(eoT_tp[hf], 1)

            def expert_pair(i):
                for k in range(2):
                    pe.wait_ge(xh_lo, i * 2 + (k + 1))
                    for f in range(2):
                        n = i * 4 + (2 * k + f)
                        gate_up0(n, k, f)
                        if later(i, 1) or k:
                            starts = f == 0 and (later(i, 2) or (later(i, 1) and k == 1))
                            down0(n - 2, 1 - k, f, i * 2 + (k - 2) if starts else None)
                if later(i, 1):
                    outputs_T(i - 1)

            expert_pair(0)
            expert_pair(1)
            with pe.Fori(2, E0 // 2) as i:
                expert_pair(i)
            down0(STEPS0 - 2, 1, 0, E0 - 2)
            down0(STEPS0 - 1, 1, 1)
            outputs_T(E0 // 2 - 1)
            for t in range(NT):
                b = t // TB
                pe.wait_ge(eo_tok[b // 4], E0 // 2)
                if t >= 4:
                    pe.wait_ge(x_done, NT + t - 3)
                for c in range(NC0):
                    last = mm(psum[:, 2 + t % 4, 0:D], PT[:, c, P * t:P * t + P], eo[:, c, b, :], c == 0, c == NC0 - 1)
                last.then_inc(comb_ready, 1)

            pe.wait_ge(eo_tok[1], E0 // 2)
            pe.wait_ge(w_rest, 16 * (len(REST) + 1))
            for q in range(B // 2):
                last = mm(psum[:, 0, q:q + 1], ctxT[:, P * q:P * q + P], cols[:, COL["w_sim2"]:COL["w_sim2"] + 1])
            last.then_inc(simT_mm, 1)

            def sim_T(q):
                pe.wait_ge(simT_sb, q + 2)
                for a in range(TB):
                    last = pe.transpose(psum[:, 4 + q // 2, 256 * (q % 2) + P * a:256 * (q % 2) + P * a + P],
                                        simT[:, q, P * a:P * a + P], ident[:, :])
                if q % 2:
                    last.then_inc(sim_mm, 1)

            pe.wait_ge(cw_done, 1)
            for q in range(B // 2 + 2):
                if q < B // 2:
                    ln_transpose(2, q)
                if 1 <= q <= B // 2:
                    pe.wait_ge(ln_xnT, 2 * NG + q)
                    if q == 1:
                        pe.wait_ge(simT_sb, 1)
                    mm(bank(q - 1), cw[:, P * q - P:P * q], xnT[:, 512 * q - 512:512 * q]).then_inc(simT_mm, 1)
                if q == 2:
                    pe.wait_ge(x_done, 2 * NT)
                if q >= 2:
                    sim_T(q - 2)
            pe.wait_ge(sim_sub, 2)
            for a in range(TB):
                last = pe.transpose(psum[0:B, 7, P * a:P * a + P], mx1b[:, B * a:B * a + B], ident[:, :])
            last.then_inc(bt_tp, 1)
            for u in range(NT // 2):
                pe.wait_ge(e1_norm, u // 4 + 1)
                last = pe.transpose(psum[:, 2 + u // 4, P * (u % 4):P * (u % 4) + P],
                                    e1n[:, 2 * u:2 * u + 2, :].rearrange("p r j -> p (r j)"), ident[:, :])
                if u % 4 == 3:
                    last.then_inc(aT_tp, 1)
            pe.wait_ge(bt_norm, 1)
            for a in range(TB):
                last = pe.transpose(psum[:, 7, 256 + B * a:256 + B * a + B], btn[0:B, P * a:P * a + P], ident[0:B, 0:B])
            last.then_inc(bt_tp, 1)

            def attended(b):
                q, r = b // 2, b % 2
                pe.wait_ge(aT_sb, q // 2 + 1)
                own = slice(C * r, C * r + C)
                last = mm(psum[:, HQ_BANKS[2 * (q // 2) + r], N * (q % 2):N * (q % 2) + N], ctx_tok[own, q, :], aT[own, q, :])
                if q % 2:
                    last.then_inc(hq_mm, 1)

            pe.wait_ge(ctx_in, 16)
            for b in range(B // 2):
                attended(b)
            pe.wait_ge(btT_sb, 1)
            for t in range(NT):
                last = mm(psum[0:B, 7, 288:288 + D], btT[:, B * t:B * t + B], xn[:, t, :], t == 0, t == NT - 1)
            last.then_inc(hc_mm, 1)
            for b in range(B // 2, B):
                if b == B - 2:
                    pe.wait_ge(hc_sb, 1)
                    pe.transpose(psum[:, 7, 416:416 + B], hc[0:B, :], ident[0:B, 0:B]).then_inc(hc_mm, 1)
                attended(b)
            pe.wait_ge(aT_sb, 2)
            for t in range(NT):
                pe.wait_ge(xh_done, t // 8 * 2 + 2)
                pe.wait_ge(xc_done, t // 8 + 1)
                if t >= 3:
                    pe.wait_ge(x_done, 2 * NT + t - 2)
                for k, feat in enumerate((xnT, hqT, xhT, xcT)):
                    last = mm(psum[:, 3 + t % 3, 0:D], feat[:, P * t:P * t + P], wqv[:, k, :], k == 0, k == 3)
                last.then_inc(qv_ready, 1)

            for g in range(NG + 1):
                if g < NG:
                    ln_transpose(3, g)
                if g >= 1:
                    pe.wait_ge(ln_xnT, 3 * NG + g)
                    for t in range(4 * g - 4, 4 * g):
                        last = mm(psum[:, t // 8, E1 * (t % 8):E1 * (t % 8) + E1], xnT[:, P * t:P * t + P], gw1[:, :])
                    if g % 2 == 0:
                        last.then_inc(rl_mm, 1)
            pe.wait_ge(x_done, 3 * NT)

            def shared_gate_up(m):
                g, c = m // 2, m % 2
                if m >= 2:
                    pe.wait_ge(sil_s, m - 1)
                mm(psum[0:I1, 2 + c, :], sgT[:, I1 * c:I1 * c + I1], xnT[:, 512 * g:512 * g + 512])
                mm(psum[0:I1, 4 + c, :], suT[:, I1 * c:I1 * c + I1], xnT[:, 512 * g:512 * g + 512]).then_inc(sg_ready, 1)

            def gate_up1(n, k, slot, hf):
                if later(n, 2):
                    pe.wait_ge(nl_done, n - 1)
                product(bank(k), lambda h: wgu[:, slot, h, 0:P], lambda h: norm_half(hf, k, h)).then_inc(gate_ready, 1)
                if later(n, 2):
                    pe.wait_ge(hid_done, n - 1)
                product(bank(2 + k), lambda h: wgu[:, slot, h, P:2 * P], lambda h: norm_half(hf, k, h))

            def rows1(k, slot, hf):
                mm(bank(4 + k), selr[:, slot, :], rwr[:, 1024 * hf + 512 * k:1024 * hf + 512 * k + 512]).then_inc(up_ready, 1)

            for g in range(NG + 1):
                if g < NG:
                    shared_gate_up(2 * g)
                    shared_gate_up(2 * g + 1)
                else:
                    pe.wait_ge(rl_sig, 2)
                    pe.wait_ge(sil_s, 2 * NG)
                    pe.wait_ge(xh_lo, 2 + E0)
                    pe.wait_ge(wgu_lo, 1 + STEPS0)
                    for k in range(2):
                        gate_up1(k, k, 0, 0)
                if g >= 1:
                    pe.wait_ge(hs_done, 2 * g)
                    if g >= 3:
                        pe.wait_ge(osh_done, g - 2)
                    for c in range(SH1):
                        last = mm(bank(7 - g % 2), sdT[:, c, :], h1[0:I1, c, :], c == 0, c == SH1 - 1)
                    last.then_inc(sd_ready, 1)
            def down1(n, k, slot, start=False, stop=False):
                pe.wait_ge(hh_lo, n + 1 + STEPS0)
                mm(bank(6 + k), wdn[:, slot, 0, :], hh[:, k, 0, :], start, False)
                mm(bank(6 + k), wdn[:, slot, 0, :], hh[:, k, 1, :], False, False)
                mm(bank(6 + k), wdn[:, slot, 1, :], hh[:, k, 0, :], False, stop).then_inc(down_done, 1)

            def first_chunk1():
                pe.wait_ge(rw_done, 1)
                for g in range(NG):
                    if g == 2:
                        pe.wait_ge(osh_done, NG)
                    for j in range(4):
                        last = pe.transpose(psum[:, 4 + g, P * j:P * j + P], rwp[:, 4 * g + j].rearrange("p k e -> p (k e)"), ident[:, :])
                    last.then_inc(rw_tp, 1)
                for k in range(2):
                    pe.wait_ge(rwr_lo, k + 1)
                    rows1(k, 0, 0)
                pe.wait_ge(rwr_lo, NG)

            def chunk_pair1(i, hf, first=False):
                for slot in range(2):
                    if first and not hf and not slot:
                        first_chunk1()
                        continue
                    pe.wait_ge(wgu_lo, i * 2 + (slot + 1) + STEPS0)
                    for k in range(2):
                        if first and hf and slot == 0:
                            pe.wait_ge(xh_lo, 2 + k + 1 + E0)
                        gate_up1(i * 4 + (2 * slot + k), k, slot, hf)
                        rows1(k, slot, hf)
                        if k == 0:
                            pe.wait_ge(wdn_lo, i * 2 + slot + STEPS0)
                        if first and hf and slot:
                            pe.wait_ge(o1_done, k + 1)
                        down1(i * 4 + (2 * slot + k - 2), k, 1 - slot, first and slot == 1, first and slot == 0)

            for hf in range(2):
                chunk_pair1(NC1 // 2 * hf, hf, True)
                with pe.Fori(0, (NC1 // 2 - 1) // 3) as j:
                    for r in range(3):
                        chunk_pair1(j * 3 + (NC1 // 2 * hf + 1 + r), hf)
            pe.wait_ge(wdn_lo, 2 * NC1 + STEPS0)
            for k in range(2):
                down1(4 * NC1 - 2 + k, k, 1, False, True)
            pe.wait_ge(o1_done, 4)
            for g in range(NG):
                for j in range(4):
                    last = pe.transpose(psum[:, g, P * j:P * j + P], osh[:, 512 * g + P * j:512 * g + P * j + P], ident[:, :])
                last.then_inc(ffn_tp, 1)

            def project(L, wq_, wk_, wv_):
                mm(bank(0), wk_[:, :], ctxT[:, :]).then_inc(qk2_mm, 1)
                for g in range(NG):
                    pe.wait_ge(ln_xnT, NG * L + g + 1)
                    mm(bank(2 + g), wq_[:, :], xnT[:, 512 * g:512 * g + 512]).then_inc(qk2_mm, 1)
                for b in range(B):
                    last = mm(psum[0:C, 6 + b // 4, D * (b % 4):D * (b % 4) + D], ctxT[:, C * b:C * b + C], wv_[:, :])
                last.then_inc(v2_mm, 1)

            def scores(base):
                for t in range(NT):
                    b = t // TB
                    pe.wait_ge(qk2_sb, 5 * base // 2 + t // 4 + 2)
                    last = mm(psum[:, t // 8, C * (t % 8):C * (t % 8) + C], q2T[:, P * t:P * t + P], k2T[:, C * b:C * b + C])
                    if t % 8 == 7:
                        last.then_inc(sim_mm, 1)
                pe.wait_ge(qk2_sb, 5 * base // 2 + 5)
                for t in range(NT):
                    pe.wait_ge(sim_exp, base + t // 8 + 3)
                    last = pe.transpose(psum[0:C, 2 + t // 4, P * (t % 4):P * (t % 4) + P], e2[:, t, :], ident[:, :])
                    if t % 4 == 3:
                        last.then_inc(e2_tp, 1)

            ln_transposes(4)
            pe.wait_ge(x_done, 4 * NT)
            pe.wait_ge(wsum_done, 1)
            mm(psum[:, 1, 0:2], ones[:, :], wsum).then_inc(wsum_mm, 1)
            project(4, wq2, wk2, wv2)
            scores(0)
            for t in range(NT):
                b = t // TB
                pe.wait_ge(e2_sb, max(t // 4 + 1, 2 if t == 3 else 1))
                if t >= 4:
                    pe.wait_ge(x_done, 4 * NT + t - 3)
                if t == 0:
                    pe.wait_ge(v2_sb, 1)
                mm(psum[:, t % 4, 0:D], e2T[0:C, P * t:P * t + P], v2[0:C, b, :]).then_inc(av2_ready, 1)

            for g in range(NG + 1):
                if g < NG:
                    ln_transpose(5, g)
                if g >= 1:
                    pe.wait_ge(ln_xnT, 5 * NG + g)
                    for t in range(4 * g - 4, 4 * g):
                        last = mm(psum[:, 4, E2 * t:E2 * t + E2], xnT[:, P * t:P * t + P], rw2[:, :])
            last.then_inc(rl_mm, 1)
            pe.wait_ge(x_done, 5 * NT)
            pe.wait_ge(xh_lo, 6 + E0)

            def up2(n, k, slot, hf):
                pe.wait_ge(prod_done, n - 1)
                product(bank(k), lambda h: wgu[:, slot, h, 0:P], lambda h: norm_half(hf, k, h))

            def rows2(local, k, hf):
                mm(bank(2 + k), sel2[:, bass.ds(local, 1), :].rearrange("p a n -> p (a n)"),
                   cT[:, 1024 * hf + 512 * k:1024 * hf + 512 * k + 512]).then_inc(up_ready, 1)

            def down2(n, k, slot, hf, start=False, stop=False):
                pe.wait_ge(hh_lo, n + 1 + STEPS0)
                pe.wait_ge(hh_lo2, n + (1 - 4 * NC1) + STEPS0)
                acc = bank(4 + 2 * hf + k % 2)
                mm(acc, wdn[:, slot, 0, :], hidden2_part(k, 0), start, False)
                mm(acc, wdn[:, slot, 0, :], hidden2_part(k, 1), False, False)
                mm(acc, wdn[:, slot, 1, :], hidden2_part(k, 0), False, stop).then_inc(down_done, 1)

            def first_chunk2():
                for k in range(2):
                    up2(4 * NC1 + k, k, 0, 0)
                pe.wait_ge(rw_done, 2)
                for q in range(2):
                    half = bank(2 + q).bitcast(BF16)
                    for j in range(8):
                        last = pe.transpose(half[:, P * j:P * j + P], cpk[:, 8 * q + j, :], identb[:, :])
                    last.then_inc(rw_tp, 1)
                pe.wait_ge(rw_sb, 2)
                pe.wait_ge(pool_made, 2)
                for k in range(2):
                    rows2(0, k, 0)

            def chunk_pair2(i, hf, pair=None):
                for slot in range(2):
                    pe.wait_ge(wgu_lo, i * 2 + (slot + 1) + STEPS0)
                    if pair == 0 and not hf and not slot:
                        first_chunk2()
                        continue
                    for k in range(2):
                        if pair == 0 and hf and slot == 0:
                            pe.wait_ge(xh_lo, 6 + k + 1 + E0)
                        up2(i * 4 + (2 * slot + k), k, slot, hf)
                        rows2(i * 2 + (slot - 2 * NC1 - NC2 * hf), k, hf)
                        back = 4 if pair is None else 4 * pair + 2 * slot + k - 3
                        if back < 0 and hf == 0:
                            continue
                        if k == 1:
                            pe.wait_ge(wdn_lo, i * 2 + slot + STEPS0)
                        down2(i * 4 + (2 * slot + k - 3), (2 * slot + k + 1) % 4, slot if k == 0 else 1 - slot,
                              hf - (back < 0), back in (0, 1), back in (-2, -1))

            for hf in range(2):
                start = NC1 + NC2 // 2 * hf
                chunk_pair2(start, hf, 0)
                chunk_pair2(start + 1, hf, 1)
                with pe.Fori(0, (NC2 // 2 - 2) // 2) as j:
                    for r in range(2):
                        chunk_pair2(j * 2 + (start + 2 + r), hf)
            down2(4 * (NC1 + NC2) - 3, 1, 0, 1)
            pe.wait_ge(wdn_lo, 2 * (NC1 + NC2) + STEPS0)
            for k in (2, 3):
                down2(4 * (NC1 + NC2) - 4 + k, k, 1, 1, False, True)
            for g in range(NG):
                pe.wait_ge(o2_sb, g + 1)
                for j in range(4):
                    last = pe.transpose(psum[:, g, P * j:P * j + P], o2T[:, 512 * g + P * j:512 * g + P * j + P], ident[:, :])
                last.then_inc(ffn_tp, 1)

            ln_transposes(6)
            pe.wait_ge(x_done, 6 * NT)
            project(6, wq3, wk3, wv3)
            scores(2)
            pe.wait_ge(v2_sb, 2)
            for b in range(B):
                g = b // 2
                pe.wait_ge(e2_sb, NG + max(g, 2) + 1 if g >= 2 else NG + g + 1)
                if g >= 2:
                    pe.wait_ge(e2_sb, 2 * NG)
                last = mm(psum[:, (0, 1, 2, 3)[g], N * (b % 2):N * (b % 2) + N], v2[0:C, b, :], e2T[0:C, N * b:N * b + N])
                if b % 2:
                    last.then_inc(c3_mm, 1)
            for t in range(NT):
                pe.wait_ge(c3_sb, t // 4 + 1)
                if t >= 4:
                    pe.wait_ge(x_done, 6 * NT + t - 3)
                mm(psum[:, 4 + t % 4, 0:D], c3T[:, P * t:P * t + P], wo3[:, :]).then_inc(av2_ready, 1)

            def tokens_T(g):
                pe.wait_ge(xq_done, g + 1)
                if g >= 2:
                    pe.wait_ge(xq_lo, g - 1)
                for j in range(4):
                    last = pe.transpose(psum[:, 2 + g % 2, P * j:P * j + P], qa[:, 4 * g + j, :], ident[:, :])
                last.then_inc(xq_tp, 1)

            def unit(n):
                g, c = n // NC3, n % NC3
                r = slice(512 * g, 512 * g + 512)
                if c == 0:
                    pe.wait_ge(xq_lo, g + 1)
                if n >= 2:
                    pe.wait_ge(hpad_done, n - 1)
                mm(bank(n % 2), w1r[:, P * c:P * c + P], xq_high[:, r], True, False)
                mm(bank(n % 2), w1r[:, P * c:P * c + P], xq_low[:, r], False, True).then_inc(l1_ready, 1)

            def hidden_T(q):
                pe.wait_ge(g3_done, NC3 * (q // 2) + NC3)
                if q >= 2:
                    pe.wait_ge(ga_done, q - 1)
                else:
                    pe.wait_ge(xq_lo, NG)
                    pe.wait_ge(x_done, 7 * NT)
                for k in range(2):
                    t = 2 * q + k
                    for c in range(NC3):
                        last = pe.transpose(psum[:, 2 + 2 * (q % 2) + k, P * c:P * c + P], g3[:, c, P * t:P * t + P], ident[:, :])
                last.then_inc(g3_tp, 1)

            def integers_T(q):
                pe.wait_ge(gi_done, q + 1)
                if q:
                    pe.wait_ge(gi_sb, q)
                half = bank(6).bitcast(BF16)
                for c in range(2 * NC3):
                    last = pe.transpose(half[:, P * c:P * c + P], gi[:, q % 2, c, :], identb[:, :])
                last.then_inc(gi_tp, 1)

            def output3(q):
                pe.wait_ge(gi_sb, q + 1)
                if q:
                    pe.wait_ge(x_done, 7 * NT + 2 * q)
                for k in range(2):
                    for c in range(NC3):
                        last = mm(psum[:, 7, P * k:P * k + P], giT[:, q % 2, NC3 * k + c, :], w2q[:, c, :], c == 0, c == NC3 - 1)
                last.then_inc(l2_ready, 1)

            tokens_T(0)
            tokens_T(1)
            for turn in range(TURNS3):
                if turn in (1, 2):
                    tokens_T(turn + 1)
                if 2 * turn < UNITS:
                    unit(2 * turn)
                    unit(2 * turn + 1)
                if 0 <= turn - 3 < PAIRS:
                    hidden_T(turn - 3)
                if 0 <= turn - 4 < PAIRS:
                    integers_T(turn - 4)
                if 0 <= turn - 5 < PAIRS:
                    output3(turn - 5)


def kernel(**inputs):
    import numpy as np
    import concourse.bacc as _bacc
    from concourse import mybir as _mybir
    from concourse.bass_utils import run_bass_kernel_spmd as _run

    v = {k: np.asarray(a) for k, a in inputs.items()}

    def columns(a, n):
        return a.reshape(a.shape[0], n, P).transpose(2, 0, 1)

    ctx = v["ctx_1024"].reshape(B * C, D)
    ctxT = ctx.T
    conv = np.concatenate([v["L3_ffn_conv_w"].reshape(HID3, 3), v["L3_ffn_conv_b"].reshape(HID3, 1)], axis=1)
    w_sim = v["L1_xattn_w_sim"].reshape(3, D)
    cols = np.concatenate([
        np.stack([v["L0_ffn_norm_g"], v["L0_ffn_norm_b"], v["L0_ffn_slot_g"], v["L0_ffn_slot_b"], w_sim[0], w_sim[1], w_sim[2],
                  v["L2_xattn_Wq_b"], v["L2_xattn_Wk_b"], v["L3_xattn_bq"]], axis=1),
        conv.reshape(NC3, P, 4).transpose(1, 0, 2).reshape(P, 4 * NC3)], axis=1)
    egu = np.concatenate([v["L0_ffn_Wg"], v["L0_ffn_Wu"]], axis=2)
    edn = v["L0_ffn_Wd"].reshape(E0, 2, P, D).transpose(0, 2, 1, 3).reshape(E0, P, 2 * D)
    ebias = np.concatenate([columns(v["L0_ffn_bg"], 2), columns(v["L0_ffn_bu"], 2), columns(v["L0_ffn_bd"], 1)], axis=2)
    w1 = np.concatenate([
        v["L1_ffn_Wg"].reshape(NC1, P, D).transpose(0, 2, 1), v["L1_ffn_Wu"].reshape(NC1, P, D).transpose(0, 2, 1),
        v["L1_ffn_Wd"].transpose(0, 2, 1).reshape(NC1, P, D)], axis=2)
    w2 = np.concatenate([v["L2_ffn_w1"].reshape(D, NC2, P).transpose(1, 0, 2), v["L2_ffn_w2"].reshape(NC2, P, D)], axis=2).transpose(1, 0, 2)
    laid = {
        "x": v["x"].reshape(T, D),
        "ctx": ctx,
        "ctxT": ctxT,
        "ctxTd": np.repeat(ctxT.reshape(D, B, 1, C), 2, axis=2).reshape(D, B * 2 * C),
        "cols": cols,
        "rows": np.stack([v["L1_xattn_b_qv"], v["L2_xattn_Wv_b"], v["L3_xattn_bv"], v["L3_xattn_bo"]]),
        "scal": np.concatenate([v["L0_ffn_scale"], v["L1_xattn_b_sim"]]),
        "gbias": v["L1_ffn_gate_bias"],
        "wq0": v["L0_xattn_Wq"],
        "wk0": np.tile(v["L0_xattn_Wkv"][:, 0:HD], (1, H0)),
        "wv0": v["L0_xattn_Wkv"][:, HD:2 * HD],
        "wo0": v["L0_xattn_Wo"],
        "slots": v["L0_ffn_slot_embeds"].reshape(ES, D),
        "egu": egu,
        "edn": edn,
        "ebias": ebias,
        "w1": w1,
        "w2": w2,
        "wqv": v["L1_xattn_W_qv"].reshape(4, P, D).transpose(1, 0, 2),
        "gw1": v["L1_ffn_gate_w"].T,
        "sgT": v["L1_ffn_Sg"].T,
        "suT": v["L1_ffn_Su"].T,
        "sdT": v["L1_ffn_Sd"].T.reshape(SH1, I1, D).transpose(1, 0, 2),
        "wq2": v["L2_xattn_Wq_w"].T,
        "wk2": v["L2_xattn_Wk_w"].T,
        "wv2": v["L2_xattn_Wv_w"].T,
        "rw2": v["L2_ffn_router_w"].T,
        "wq3": v["L3_xattn_Wq"].T,
        "wk3": v["L3_xattn_Wk"].T,
        "wv3": v["L3_xattn_Wv"].T,
        "wo3": v["L3_xattn_Wo"].T,
        "w1f": v["L3_ffn_w1"].T,
        "w2f": v["L3_ffn_w2"].T.reshape(NC3, P, D).transpose(1, 0, 2),
    }
    nc = _bacc.Bacc("TRN2", target_bir_lowering=False, num_devices=1)
    arrays, args = {}, {}
    for name, a in laid.items():
        a = np.ascontiguousarray(a)
        arrays[f"in_{name}"] = a
        args[name] = nc.dram_tensor(f"in_{name}", a.shape, _mybir.dt.from_np(a.dtype), kind="ExternalInput").ap()
    out = nc.dram_tensor("out", (T, D), F32, kind="ExternalOutput").ap()
    build_program(nc, args, out)
    r = _run(nc, [arrays], core_ids=[0])
    return r.results[0]["out"].reshape(B, N, D)
```
